# Optimizing a Trainium2 kernel written in Bass

```python
import numpy as np
import jax
import jax.numpy as jnp

def _softmax(x, axis=-1):
    return jax.nn.softmax(x, axis=axis)

def _gelu(x):
    return jax.nn.gelu(x, approximate=True)

def _silu(x):
    return jax.nn.silu(x)

def _sigmoid(x):
    return jax.nn.sigmoid(x)

def _layernorm(x, axis=-1, eps=1e-05):
    m = jnp.mean(x, axis=axis, keepdims=True)
    v = jnp.var(x, axis=axis, keepdims=True)
    return (x - m) / jnp.sqrt(v + eps)

def _scatter_add(tgt, idx, src, axis=0):
    return tgt.at[idx].add(src)

def _segment_sum(src, seg, n):
    return jax.ops.segment_sum(src, seg, n)
kernel_name = 'mk_perceiver_d1_seqx_r4_0b481d'

def setup_inputs(seed: int=0):
    np.random.seed(seed)
    _w = jnp.asarray

    def _rec_inputs():
        import jax
        import jax.numpy as jnp
        _rk = jax.random.key(seed)
        x = -0.0005207 + 1.001 * jax.random.normal(jax.random.fold_in(_rk, 1), (4, 256, 256), jnp.float32)
        _lenS = 256 - jax.random.randint(jax.random.fold_in(_rk, 7), (4,), 0, max(1, 256 // 4) + 1, jnp.int32)
        _lenS2 = 4096 - jax.random.randint(jax.random.fold_in(_rk, 8), (4,), 0, max(1, 4096 // 4) + 1, jnp.int32)
        _ctx_1024P = jax.random.normal(jax.random.fold_in(_rk, 11), (4, 16, 256), jnp.float32)
        _ctx_1024c = jax.random.dirichlet(jax.random.fold_in(_rk, 511), 0.3 * jnp.ones((16,), jnp.float32), (4, 4096))
        _ctx_1024t = jnp.einsum('bsk,bkd->bsd', _ctx_1024c, _ctx_1024P)
        _ctx_1024t = _ctx_1024t * jax.lax.rsqrt(jnp.mean(jnp.square(_ctx_1024t)) + 1e-12) * 0.953939
        ctx_1024 = 4.13588e-05 + 0.999923 * (_ctx_1024t + 0.3 * jax.random.normal(jax.random.fold_in(_rk, 611), (4, 4096, 256), jnp.float32))
        _validS = jnp.arange(256)[None, :] < _lenS[:, None]
        _validS2 = jnp.arange(4096)[None, :] < _lenS2[:, None]
        _causal = jnp.tril(jnp.ones((256, 256), dtype=bool))
        mask_BxS2_bf1 = jnp.ones((4, 4096), dtype=bool)
        return (x, ctx_1024, mask_BxS2_bf1)
    x, ctx_1024, mask_BxS2_bf1 = _rec_inputs()

    def _L0_xattn_setup():
        import jax, jax.numpy as jnp
        import numpy as np
        B, T, S, DM, H, D, TOPK = (4, 128, 512, 256, 16, 64, 32)
        INNER = H * D
        key = jax.random.key(seed)
        ks = jax.random.split(key, 7)
        x = jax.random.normal(ks[0], (B, T, DM), dtype=jnp.float32)
        mem_keys = jax.random.normal(ks[1], (B, S, DM), dtype=jnp.float32)
        mem_values = jax.random.normal(ks[2], (B, S, DM), dtype=jnp.float32)
        mem_mask = jnp.ones((B, S), dtype=bool)
        sc = 0.02
        Wq = sc * jax.random.normal(ks[3], (DM, INNER), dtype=jnp.float32)
        Wk = sc * jax.random.normal(ks[4], (DM, INNER), dtype=jnp.float32)
        Wv = sc * jax.random.normal(ks[5], (DM, INNER), dtype=jnp.float32)
        Wo = sc * jax.random.normal(ks[6], (INNER, DM), dtype=jnp.float32)
        inv_temp = jnp.ones((H,), dtype=jnp.float32)
        return {'x': x, 'mem_keys': mem_keys, 'mem_values': mem_values, 'mem_mask': mem_mask, 'Wq': Wq, 'Wk': Wk, 'Wv': Wv, 'Wo': Wo, 'inv_temp': inv_temp}
    _L0_xattn_all = _L0_xattn_setup()
    _L0_xattn_in = {k: v for k, v in _L0_xattn_all.items() if k in ('Wq', 'Wk', 'Wv', 'Wo', 'inv_temp')}
    del _L0_xattn_all

    def _L0_attn_setup():
        import jax, jax.numpy as jnp
        import numpy as np
        import math
        D_MODEL = 256
        N_HEADS = 16
        D_K = D_MODEL // N_HEADS
        BATCH = 4
        SEQ = 512
        TRAINING_PROGRESS = 0.25
        CONVERGENCE_PHASE = 0.5
        TENSION = abs(1.0 - 1.0)

        def _pos_encoding(seq_len, d, yellow):
            phase_mod = 0.1 * math.sin(2.0 * math.pi * TRAINING_PROGRESS)
            i_even = jnp.arange(0, d, 2, dtype=jnp.float32)
            denom = jnp.power(10000.0, 2.0 * i_even / d) * (1.0 + yellow * phase_mod)
            pos = jnp.arange(seq_len, dtype=jnp.float32)
            ang = pos[:, None] / denom[None, :]
            pe = jnp.zeros((seq_len, d), jnp.float32)
            pe = pe.at[:, 0::2].set(jnp.sin(ang))
            pe = pe.at[:, 1::2].set(jnp.cos(ang))
            return pe
        key = jax.random.key(seed)
        ks = jax.random.split(key, 8)
        x = jax.random.normal(ks[0], (BATCH, SEQ, D_MODEL), dtype=jnp.float32)
        rby = jax.random.uniform(ks[1], (3,), dtype=jnp.float32)
        s = 0.02
        Wq = jax.random.normal(ks[2], (D_MODEL, D_MODEL), dtype=jnp.float32) * s
        Wk = jax.random.normal(ks[3], (D_MODEL, D_MODEL), dtype=jnp.float32) * s
        Wv = jax.random.normal(ks[4], (D_MODEL, D_MODEL), dtype=jnp.float32) * s
        Wo = jax.random.normal(ks[5], (D_MODEL, D_MODEL), dtype=jnp.float32) * s
        bq = jnp.zeros((D_MODEL,), jnp.float32)
        bk = jnp.zeros((D_MODEL,), jnp.float32)
        bv = jnp.zeros((D_MODEL,), jnp.float32)
        bo = jnp.zeros((D_MODEL,), jnp.float32)
        ln_gamma = jnp.ones((D_MODEL,), jnp.float32)
        ln_beta = jnp.zeros((D_MODEL,), jnp.float32)
        return {'x': x, 'rby': rby, 'Wq': Wq, 'bq': bq, 'Wk': Wk, 'bk': bk, 'Wv': Wv, 'bv': bv, 'Wo': Wo, 'bo': bo, 'ln_gamma': ln_gamma, 'ln_beta': ln_beta}
    _L0_attn_all = _L0_attn_setup()
    _L0_attn_in = {k: v for k, v in _L0_attn_all.items() if k in ('rby', 'Wq', 'bq', 'Wk', 'bk', 'Wv', 'bv', 'Wo', 'bo', 'ln_gamma', 'ln_beta')}
    del _L0_attn_all

    def _L0_ffn_setup():
        import jax, jax.numpy as jnp
        import numpy as np
        BLOCK = 16
        _GRID = jnp.array([0.0, 0.5, 1.0, 1.5, 2.0, 3.0, 4.0, 6.0], dtype=jnp.float32)
        _MID = jnp.array([0.25, 0.75, 1.25, 1.75, 2.5, 3.5, 5.0], dtype=jnp.float32)

        def fp4_quant_dequant(x):
            shape = x.shape
            xb = x.reshape(shape[:-1] + (shape[-1] // BLOCK, BLOCK))
            scale = jnp.max(jnp.abs(xb), axis=-1, keepdims=True) / 6.0
            scale = jnp.maximum(scale, jnp.float32(1e-12))
            xn = xb / scale
            idx = jnp.searchsorted(_MID, jnp.abs(xn))
            q = _GRID[idx] * jnp.sign(xn) * scale
            return q.reshape(shape)

        def fp4_linear(x, w):
            xq = fp4_quant_dequant(x)
            wq = fp4_quant_dequant(w)
            return jnp.einsum('bsk,nk->bsn', xq, wq)
        key = jax.random.key(seed)
        k1, k2, k3, k4 = jax.random.split(key, 4)
        H, I = (256, 704)
        x = jax.random.normal(k1, (4, 1024, H), dtype=jnp.float32)
        w_gate = jax.random.normal(k2, (I, H), dtype=jnp.float32) * 0.02
        w_up = jax.random.normal(k3, (I, H), dtype=jnp.float32) * 0.02
        w_down = jax.random.normal(k4, (H, I), dtype=jnp.float32) * 0.02
        return {'x': x, 'w_gate': w_gate, 'w_up': w_up, 'w_down': w_down}
    _L0_ffn_all = _L0_ffn_setup()
    _L0_ffn_in = {k: v for k, v in _L0_ffn_all.items() if k in ('w_gate', 'w_up', 'w_down')}
    del _L0_ffn_all
    return {'x': x, 'ctx_1024': ctx_1024, 'mask_BxS2_bf1': mask_BxS2_bf1, 'L0_xattn_Wq': _L0_xattn_in['Wq'], 'L0_xattn_Wk': _L0_xattn_in['Wk'], 'L0_xattn_Wv': _L0_xattn_in['Wv'], 'L0_xattn_Wo': _L0_xattn_in['Wo'], 'L0_xattn_inv_temp': _L0_xattn_in['inv_temp'], 'L0_attn_rby': _L0_attn_in['rby'], 'L0_attn_Wq': _L0_attn_in['Wq'], 'L0_attn_bq': _L0_attn_in['bq'], 'L0_attn_Wk': _L0_attn_in['Wk'], 'L0_attn_bk': _L0_attn_in['bk'], 'L0_attn_Wv': _L0_attn_in['Wv'], 'L0_attn_bv': _L0_attn_in['bv'], 'L0_attn_Wo': _L0_attn_in['Wo'], 'L0_attn_bo': _L0_attn_in['bo'], 'L0_attn_ln_gamma': _L0_attn_in['ln_gamma'], 'L0_attn_ln_beta': _L0_attn_in['ln_beta'], 'L0_ffn_w_gate': _L0_ffn_in['w_gate'], 'L0_ffn_w_up': _L0_ffn_in['w_up'], 'L0_ffn_w_down': _L0_ffn_in['w_down']}

def reference(x, ctx_1024, mask_BxS2_bf1, L0_xattn_Wq, L0_xattn_Wk, L0_xattn_Wv, L0_xattn_Wo, L0_xattn_inv_temp, L0_attn_rby, L0_attn_Wq, L0_attn_bq, L0_attn_Wk, L0_attn_bk, L0_attn_Wv, L0_attn_bv, L0_attn_Wo, L0_attn_bo, L0_attn_ln_gamma, L0_attn_ln_beta, L0_ffn_w_gate, L0_ffn_w_up, L0_ffn_w_down):
    import jax
    import jax.numpy as jnp

    def _L0_xattn_ref(x, mem_keys, mem_values, mem_mask, Wq, Wk, Wv, Wo, inv_temp):
        import jax, jax.numpy as jnp
        import numpy as np
        B, T, S, DM, H, D, TOPK = (4, 128, 512, 256, 16, 64, 32)
        INNER = H * D
        b, t, _ = x.shape
        s = mem_keys.shape[1]
        q = (x @ Wq).reshape(b, t, H, D).transpose(0, 2, 1, 3)
        k = (mem_keys @ Wk).reshape(b, s, H, D).transpose(0, 2, 1, 3)
        v = (mem_values @ Wv).reshape(b, s, H, D).transpose(0, 2, 1, 3)
        q = q * inv_temp.reshape(1, H, 1, 1)
        scores = jnp.einsum('bhtd,bhsd->bhts', q, k) / jnp.asarray(np.sqrt(D), x.dtype)
        scores = jnp.where(mem_mask[:, None, None, :], scores, -jnp.inf)
        full_attn = jax.nn.softmax(scores, axis=-1)
        topk_vals = jax.lax.top_k(scores, TOPK)[0]
        threshold = topk_vals[..., -1:]
        topk_mask = (scores >= threshold).astype(scores.dtype)
        sparse_attn = full_attn * topk_mask
        sparse_attn = sparse_attn / (jnp.sum(sparse_attn, axis=-1, keepdims=True) + 1e-08)
        attn = full_attn + jax.lax.stop_gradient(sparse_attn - full_attn)
        out = jnp.einsum('bhts,bhsd->bhtd', attn, v)
        out = out.transpose(0, 2, 1, 3).reshape(b, t, INNER)
        return out @ Wo

    def _L0_attn_ref(x, rby, Wq, bq, Wk, bk, Wv, bv, Wo, bo, ln_gamma, ln_beta):
        import jax, jax.numpy as jnp
        import numpy as np
        import math
        D_MODEL = 256
        N_HEADS = 16
        D_K = D_MODEL // N_HEADS
        BATCH = 4
        SEQ = 512
        TRAINING_PROGRESS = 0.25
        CONVERGENCE_PHASE = 0.5
        TENSION = abs(1.0 - 1.0)

        def _pos_encoding(seq_len, d, yellow):
            phase_mod = 0.1 * math.sin(2.0 * math.pi * TRAINING_PROGRESS)
            i_even = jnp.arange(0, d, 2, dtype=jnp.float32)
            denom = jnp.power(10000.0, 2.0 * i_even / d) * (1.0 + yellow * phase_mod)
            pos = jnp.arange(seq_len, dtype=jnp.float32)
            ang = pos[:, None] / denom[None, :]
            pe = jnp.zeros((seq_len, d), jnp.float32)
            pe = pe.at[:, 0::2].set(jnp.sin(ang))
            pe = pe.at[:, 1::2].set(jnp.cos(ang))
            return pe
        B, S, d = x.shape
        red, blue, yellow = (rby[0], rby[1], rby[2])
        x = x + _pos_encoding(S, d, yellow)[None, :, :]

        def proj(W, b):
            return (x @ W.T + b).reshape(B, S, N_HEADS, D_K).transpose(0, 2, 1, 3)
        Q, K, V = (proj(Wq, bq), proj(Wk, bk), proj(Wv, bv))
        scale = jnp.sqrt(D_K * (1.0 + TENSION * red))
        logits = jnp.einsum('bhqd,bhkd->bhqk', Q, K) / scale
        scale_matrix = 1.0 + red * 0.1 + blue * 0.05 + yellow * 0.15
        logits = logits * scale_matrix
        attn = jax.nn.softmax(logits, axis=-1)
        eps_adaptive = 0.1 * math.sin(2.0 * math.pi * CONVERGENCE_PHASE)
        out = jnp.einsum('bhqk,bhkd->bhqd', attn, V) * (1.0 + yellow * eps_adaptive)
        out = out.transpose(0, 2, 1, 3).reshape(B, S, d)
        out = out @ Wo.T + bo
        x = x + out
        mean = jnp.mean(x, axis=-1, keepdims=True)
        var = jnp.var(x, axis=-1, keepdims=True)
        eps_rby = 1e-05 * (1.0 + blue * 0.1)
        gamma_rby = ln_gamma * (1.0 + red * 0.1 + yellow * 0.05)
        normalized = (x - mean) / jnp.sqrt(var + eps_rby)
        return normalized * gamma_rby + ln_beta

    def _L0_ffn_ref(x, w_gate, w_up, w_down):
        import jax, jax.numpy as jnp
        import numpy as np
        BLOCK = 16
        _GRID = jnp.array([0.0, 0.5, 1.0, 1.5, 2.0, 3.0, 4.0, 6.0], dtype=jnp.float32)
        _MID = jnp.array([0.25, 0.75, 1.25, 1.75, 2.5, 3.5, 5.0], dtype=jnp.float32)

        def fp4_quant_dequant(x):
            shape = x.shape
            xb = x.reshape(shape[:-1] + (shape[-1] // BLOCK, BLOCK))
            scale = jnp.max(jnp.abs(xb), axis=-1, keepdims=True) / 6.0
            scale = jnp.maximum(scale, jnp.float32(1e-12))
            xn = xb / scale
            idx = jnp.searchsorted(_MID, jnp.abs(xn))
            q = _GRID[idx] * jnp.sign(xn) * scale
            return q.reshape(shape)

        def fp4_linear(x, w):
            xq = fp4_quant_dequant(x)
            wq = fp4_quant_dequant(w)
            return jnp.einsum('bsk,nk->bsn', xq, wq)
        gate = fp4_linear(x, w_gate)
        y = fp4_linear(x, w_up)
        h = jax.nn.silu(gate) * y
        return fp4_linear(h, w_down)
    x = x + _L0_xattn_ref(_layernorm(x, axis=-1), ctx_1024, ctx_1024, mask_BxS2_bf1, L0_xattn_Wq, L0_xattn_Wk, L0_xattn_Wv, L0_xattn_Wo, L0_xattn_inv_temp)
    x = x + _L0_attn_ref(_layernorm(x, axis=-1), L0_attn_rby, L0_attn_Wq, L0_attn_bq, L0_attn_Wk, L0_attn_bk, L0_attn_Wv, L0_attn_bv, L0_attn_Wo, L0_attn_bo, L0_attn_ln_gamma, L0_attn_ln_beta)
    x = x + _L0_ffn_ref(_layernorm(x, axis=-1), L0_ffn_w_gate, L0_ffn_w_up, L0_ffn_w_down)
    return x

_drawn_inputs = setup_inputs


def setup_inputs(seed=0):
    import zlib

    import numpy as np

    out = dict(_drawn_inputs(seed))
    spreads = {'L0_xattn_inv_temp': (1.0, 0.6),
     'L0_attn_bq': (0.0, 0.8),
     'L0_attn_bk': (0.0, 0.8),
     'L0_attn_bv': (0.0, 0.593),
     'L0_attn_bo': (0.0, 0.1),
     'L0_attn_ln_gamma': (1.0, 0.2),
     'L0_attn_ln_beta': (0.0, 0.1)}
    factors = {'L0_attn_Wq': 8.0,
     'L0_attn_Wk': 8.0,
     'L0_ffn_w_gate': 3.435,
     'L0_ffn_w_up': 3.061,
     'L0_ffn_w_down': 3.006}
    for name, (base, spread) in spreads.items():
        noise = np.random.default_rng([zlib.crc32(name.encode()), seed]).standard_normal(out[name].shape)
        drawn = base * np.exp(spread * noise) if base else spread * noise
        out[name] = jnp.asarray(drawn.astype(out[name].dtype))
    for name, factor in factors.items():
        out[name] = (out[name] * factor).astype(out[name].dtype)
    return out
```

```python
import math
from contextlib import ExitStack

import numpy as np
import concourse.bass as bass
from concourse import mybir

F32 = mybir.dt.float32
BF16 = mybir.dt.bfloat16
I32 = mybir.dt.int32
U8 = mybir.dt.uint8
U32 = mybir.dt.uint32
ALU = mybir.AluOpType
ACT = mybir.ActivationFunctionType
AX = mybir.AxisListType
RMAX = bass.bass_isa.ReduceOp.max

P = 128
B, T, DM = 4, 256, 256
S = 4096
H, D = 16, 64
TOPK = 32
NB = 2 * H // 2 // 2
PAIRS = B * NB
TT = T // P
CH = 1024
NC = S // CH
GRP = 128
NG = S // GRP
MASKED = -1.0e30
LOWEST = -3.0e38
EPS = 1e-5


def pair_schedule():
    order = []
    for j in range(4):
        for c in range(NC):
            order.append(("S", j, c))
            order.append(("T", j, c))
            if c == 1:
                order.append(("KKVV"[j], 2 * (j % 2), 0))
                if j == 3:
                    order.append(("OP", 0, 0))
            if c == 2 and j == 2:
                order.append(("QO", 0, 0))
            if c == 3:
                order.append(("KKVV"[j], 2 * (j % 2) + 1, 0))
    return order


ORDER = pair_schedule()
USES = len(ORDER)
assert USES % 3 == 0
PROLOGUE = ([("X", c, 0) for c in range(2)] + [("Q", 0, 0)] + [("K", n, 0) for n in range(NC)] +
            [("V", n, 0) for n in range(NC)])


def uses_of(g):
    def there(use):
        kind, j, _ = use
        late = (kind == "T" and j < 2) or kind == "OP"
        if g == 0:
            return not late
        if g == PAIRS - 1:
            return kind not in "KV"
        if g == PAIRS:
            return late or kind == "QO"
        return True
    uses = [u for u in ORDER if there(u)]
    if g == PAIRS:
        uses.remove(("OP", 0, 0))
        uses.append(("OP", 0, 0))
    return uses


INDEX = {}
for _use in PROLOGUE:
    INDEX[(-1, _use)] = len(INDEX)
for _g in range(PAIRS + 1):
    for _use in uses_of(_g):
        INDEX[(_g, _use)] = len(INDEX)
for _g in range(1, PAIRS - 1):
    assert all(INDEX[(_g, u)] == INDEX[(1, u)] + (_g - 1) * USES for u in ORDER)


def use_index(g, use):
    if isinstance(g, int):
        return INDEX[(g, use)]
    return g * USES + (INDEX[(1, use)] - USES)


def use_slot(g, use):
    return INDEX[(g if isinstance(g, int) else 1, use)] % 3


def build(nc, x, ctx_t, mask, w_pack, w_out, out, **later):
    with nc.sbuf_tensor("x_sb", [P, B * TT, DM], F32) as x_sb, nc.sbuf_tensor("ident", [P, P], F32) as ident:
        with ExitStack() as ctx:
            cross_attention(nc, ctx, x, ctx_t, mask, w_pack, w_out, x_sb, ident)
        with ExitStack() as ctx:
            self_attention_and_ffn(nc, ctx, x_sb, ident, out, **later)


def cross_attention(nc, ctx, x, ctx_t, mask, w_pack, w_out, x_sb, ident):
    def sb(name, shape, dt=F32):
        return ctx.enter_context(nc.sbuf_tensor(name, shape, dt))

    def psum(name, shape, dt=F32):
        return ctx.enter_context(nc.psum_tensor(name, shape, dt))

    def sem(name):
        return ctx.enter_context(nc.semaphore(name))

    WCOLS = 6 * P + 1
    ctx_sb = sb("ctx_sb", [P, 2, S])
    xnT = sb("xnT", [P, 2, B * T])
    weights = sb("weights", [P, 2, WCOLS])
    wo_sb = sb("wo_sb", [P, 2, DM])
    kT = sb("kT", [P, 2, S])
    v_sb = sb("v_sb", [P, 2, S // P, P])
    qT = sb("qT", [P, 2, T])
    scores = sb("scores", [P, 2, S])
    probs = sb("probs", [P, 2, S])
    probsT = sb("probsT", [P, 2, CH])
    cand = sb("cand", [P, 8 * NG])
    cand_left = sb("cand_left", [P, 8 * NG])
    top = sb("top", [P, 2, TOPK])
    slow_in = sb("slow_in", [P, CH])
    slow_cand = sb("slow_cand", [P, NC * TOPK])
    over = sb("over", [P, NG])
    waited = sb("waited", [P, NC + 1])
    suspect = sb("suspect", [P, 1])
    suspect_twice = sb("suspect_twice", [P, 1])
    suspect_all = sb("suspect_all", [P, 1])
    suspect_int = sb("suspect_int", [P, 2], I32)
    neg_max = sb("neg_max", [P, 2])
    full_sum = sb("full_sum", [P, 2])
    kept_sum = sb("kept_sum", [P, 2])
    denom = sb("denom", [P, 2])
    inv_denom = sb("inv_denom", [P, 2])
    o_pair = sb("o_pair", [P, TT, P])
    oT = sb("oT", [P, TT * P])
    o_proj = sb("o_proj", [P, TT, DM])
    mask_u8 = slow_in[0:B, :].bitcast(U8)
    mask_bias = sb("mask_bias", [B, S], BF16)
    pick = sb("pick", [B, B, P], BF16)
    stats = sb("stats", [P, B * TT, 6])
    mean_var = sb("mean_var", [P, B * TT, 2])
    std = sb("std", [P, B * TT])
    rstd = sb("rstd", [P, B * TT])
    xn = probs[:, 1, 0:B * TT * DM].rearrange("p (i c) -> p i c", c=DM)
    eps_col = sb("eps_col", [P, 1])

    ring = [psum(f"ring{i}", [P, CH]) for i in range(3)]
    o_acc = [psum(f"o_acc{i}", [P, 512]) for i in range(2)]

    x_in = sem("x_in")
    mask_in = sem("mask_in")
    weights_in = [sem("weights_in0"), sem("weights_in1")]
    wo_in = [sem("wo_in0"), sem("wo_in1")]
    ctx_in = [sem(f"ctx_in{n}") for n in range(NC)]
    ident_step = sem("ident_step")
    pick_ready = sem("pick_ready")
    bias_ready = sem("bias_ready")
    ln_step = sem("ln_step")
    std_ready = sem("std_ready")
    xn_ready = sem("xn_ready")
    ring_full = sem("ring_full")
    ring_free = sem("ring_free")
    max_ready = sem("max_ready")
    exp_done = sem("exp_done")
    masked = sem("masked")
    denom_ready = sem("denom_ready")
    norm_ready = sem("norm_ready")
    pv_done = sem("pv_done")
    o_read = sem("o_read")
    x_added = sem("x_added")
    suspect_sent = sem("suspect_sent")
    suspect_step = sem("suspect_step")
    suspect_ready = sem("suspect_ready")
    topk_step = sem("topk_step")

    block = ctx.enter_context(nc.Block())
    LOOPS = PAIRS // 2

    @block.sync
    def _(sp):
        def load_weights(g, parity, p):
            sp.dma_start(weights[:, parity, :], w_pack[p]).then_inc(weights_in[parity], 16)

        def load_wo(g, parity, p):
            sp.dma_start(wo_sb[:, parity, :], w_out[p]).then_inc(wo_in[parity], 16)

        def load_ctx(b, n):
            sp.dma_start(ctx_sb[:, :, n * CH:(n + 1) * CH],
                         ctx_t[b, :, :, n * CH:(n + 1) * CH].rearrange("c p s -> p c s")).then_inc(ctx_in[n], 16)

        sp.dma_start(x_sb[:], x.rearrange("b (t p) c -> p (b t) c", p=P)).then_inc(x_in, 16)
        sp.dma_start(mask_u8, mask).then_inc(mask_in, 16)
        load_weights(0, 0, 0)
        for n in range(NC):
            load_ctx(0, n)
        load_weights(1, 1, 1)
        load_wo(0, 0, 0)
        sp.wait_ge(ring_full, len(PROLOGUE))
        load_weights(2, 0, 2)

        def after_pair(k, parity, p):
            sp.wait_ge(ring_full, use_index(k, ORDER[-1]) + 1)
            load_weights(k + 3, 1 - parity, (p + 3) % NB)
            load_wo(k + 1, 1 - parity, (p + 1) % NB)

        def next_context(b):
            for n in range(NC):
                sp.wait_ge(ring_full, use_index(NB * b - 2, ("V", n, 0)) + 1)
                load_ctx(b, n)

        for k in range(PAIRS - 1):
            if (k + 2) % NB == 0 and k + 2 < PAIRS:
                next_context((k + 2) // NB)
            if k + 3 < PAIRS:
                after_pair(k, k % 2, k % NB)
            else:
                sp.wait_ge(ring_full, use_index(k, ORDER[-1]) + 1)
                load_wo(k + 1, (k + 1) % 2, (k + 1) % NB)

    @block.gpsimd
    def _(pool):
        pool.memset(ident[:], 0.0).then_inc(ident_step, 1)
        pool.memset(pick[:], 0.0).then_inc(ident_step, 1)
        pool.wait_ge(ident_step, 2)
        pool.affine_select(out=ident[:], in_=ident[:], compare_op=ALU.not_equal, fill=1.0, base=0,
                           pattern=[[-1, P]], channel_multiplier=1).then_inc(ident_step, 1)
        pool.affine_select(out=pick[:], in_=pick[:], compare_op=ALU.not_equal, fill=1.0, base=0,
                           pattern=[[-1, B], [0, P]], channel_multiplier=1).then_inc(pick_ready, 1)
        pool.wait_ge(mask_in, 16)
        pool.tensor_scalar(mask_bias[:], mask_u8, -1.0, -MASKED, ALU.add, ALU.mult).then_inc(bias_ready, 1)

        def reduce_suspect(t):
            pool.wait_ge(suspect_sent, t + 1)
            pool.tensor_tensor(suspect_twice[:], suspect[:], suspect[:], ALU.add).then_inc(suspect_step, 1)
            pool.wait_ge(suspect_step, 1)
            pool.partition_all_reduce(suspect_all[:], suspect_twice[:], P, RMAX).then_inc(suspect_step, 1)
            pool.wait_ge(suspect_step, 2)
            pool.tensor_copy(suspect_int[:, 0:1], suspect_all[:]).then_inc(suspect_step, 1)
            pool.wait_ge(suspect_step, 3)
            pool.sem_clear(suspect_step)
            pool.sem_inc(suspect_ready, 1)

        def add_output(g, row):
            pool.wait_ge(ring_free, use_index(g + 1, ("OP", 0, 0)) + 1)
            pool.tensor_tensor(row, row, o_proj[:], ALU.add).then_inc(x_added, 1)

        def x_rows(g):
            if isinstance(g, int):
                b = g // NB
                return x_sb[:, b * TT:(b + 1) * TT, :]
            return x_sb[:, bass.ds((g // NB) * TT, TT), :]

        for j in range(4):
            reduce_suspect(j)
        with pool.Fori(1, PAIRS - 1) as g:
            for j in range(4):
                reduce_suspect(4 * g + j)
            pool.wait_ge(ring_free, use_index(g, ("OP", 0, 0)) + 1)
            row = x_rows(g - 1)
            pool.tensor_tensor(row, row, o_proj[:], ALU.add).then_inc(x_added, 1)
        for j in range(4):
            reduce_suspect(4 * (PAIRS - 1) + j)
        for g in (PAIRS - 2, PAIRS - 1):
            add_output(g, x_rows(g))

    @block.vector
    def _(dve):
        steps = [0]

        def then(ins):
            steps[0] += 1
            ins.then_inc(ln_step, 1)
            dve.wait_ge(ln_step, steps[0])

        dve.memset(eps_col[:], EPS)
        dve.wait_ge(x_in, 16)
        for i in range(B * TT):
            last = dve.bn_stats(stats[:, i, :], x_sb[:, i, :])
        then(last)
        for i in range(B * TT):
            last = dve.bn_aggr(mean_var[:, i, :], stats[:, i, :])
        then(last)
        dve.wait_ge(std_ready, 1)
        then(dve.reciprocal(rstd[:], std[:]))
        for i in range(B * TT):
            last = dve.tensor_scalar(xn[:, i, :], x_sb[:, i, :], mean_var[:, i, 0:1], rstd[:, i:i + 1],
                                     ALU.subtract, ALU.mult)
        last.then_inc(xn_ready, 1)

        PER_TILE = 8

        def largest(g, j):
            t, q = 4 * g + j, j % 2
            n = [0]

            def link(ins):
                n[0] += 1
                ins.then_inc(topk_step, 1)
                dve.wait_ge(topk_step, n[0])

            for c in range(NC):
                dve.wait_ge(ring_free, use_index(g, ("S", j, c)) + 1)
                dve.memset(waited[:, c:c + 1], 0.0)
                for i in range(CH // GRP):
                    k = c * (CH // GRP) + i
                    last = dve.max(cand[:, 8 * k:8 * k + 8], scores[:, q, k * GRP:(k + 1) * GRP])
            link(last)
            link(dve.max(top[:, q, 0:8], cand[:]))
            dve.tensor_scalar(neg_max[:, q:q + 1], top[:, q, 0:1], -float(D) ** -0.5, None,
                              ALU.mult).then_inc(max_ready, 1)
            for r in range(1, TOPK // 8):
                link(dve.match_replace(cand_left[:], top[:, q, 8 * r - 8:8 * r], cand[:] if r == 1 else cand_left[:],
                                       LOWEST))
                link(dve.max(top[:, q, 8 * r:8 * r + 8], cand_left[:]))
            assert n[0] == PER_TILE
            dve.tensor_scalar(over[:], cand[:, 7:8 * NG:8], top[:, q, TOPK - 1:TOPK], None, ALU.is_gt, ALU.add,
                              accum_out=suspect[:]).then_inc(suspect_sent, 1)

        def keep(t, q):
            dve.wait_ge(exp_done, t + 1)
            dve.scalar_tensor_tensor(out=probs[:, q, :], in0=scores[:, q, :], scalar=top[:, q, TOPK - 1:TOPK],
                                     in1=probs[:, q, :], op0=ALU.is_ge, op1=ALU.mult,
                                     accum_out=kept_sum[:, q:q + 1]).then_inc(masked, 1)
            dve.wait_ge(masked, t + 1)
            dve.scalar_tensor_tensor(out=denom[:, q:q + 1], in0=full_sum[:, q:q + 1], scalar=1e-8,
                                     in1=kept_sum[:, q:q + 1], op0=ALU.mult, op1=ALU.add).then_inc(denom_ready, 1)
            dve.wait_ge(denom_ready, t + 1)
            dve.reciprocal(inv_denom[:, q:q + 1], denom[:, q:q + 1]).then_inc(norm_ready, 1)

        def settle(t, q):
            dve.wait_ge(suspect_ready, t + 1)
            dve.memset(waited[:, NC:NC + 1], 0.0).then_inc(topk_step, 1)
            dve.wait_ge(topk_step, PER_TILE + 1)
            flag = dve.value_load(suspect_int[0:1, 0:1], min_val=0, max_val=2 * NG)
            dve.sem_clear(topk_step)
            with dve.If(flag):
                for c in range(NC):
                    for r in range(TOPK // 8):
                        src = scores[:, q, c * CH:(c + 1) * CH] if r == 0 else slow_in[:]
                        at = c * TOPK + 8 * r
                        dve.max(slow_cand[:, at:at + 8], src)
                        dve.drain()
                        if r < TOPK // 8 - 1:
                            dve.match_replace(slow_in[:], slow_cand[:, at:at + 8], src, LOWEST)
                            dve.drain()
                for r in range(TOPK // 8):
                    dve.max(top[:, q, 8 * r:8 * r + 8], slow_cand[:])
                    dve.drain()
                    if r < TOPK // 8 - 1:
                        dve.match_replace(slow_cand[:], top[:, q, 8 * r:8 * r + 8], slow_cand[:], LOWEST)
                        dve.drain()

        def pair(g, first=False):
            for j in range(4):
                t = 4 * g + j
                largest(g, j)
                if not (first and j == 0):
                    keep(t - 1, (j - 1) % 2)
                settle(t, j % 2)

        pair(0, first=True)
        with dve.Fori(1, PAIRS - 1) as g:
            pair(g)
        pair(PAIRS - 1)
        keep(4 * PAIRS - 1, 1)

    @block.scalar
    def _(act):
        act.wait_ge(ln_step, 2)
        act.activation(std[:], mean_var[:, :, 1], ACT.Sqrt, bias=eps_col[:]).then_inc(std_ready, 1)

        def copy(dst, src):
            return act.activation(dst, src, ACT.Copy)

        def take_q(parity, slot):
            return act.activation(qT[:, parity, :], ring[slot][:, 0:T], ACT.Copy,
                                  scale=weights[:, parity, 6 * P:6 * P + 1])

        def take_kv(kind, parity, n, slot):
            if kind == "K":
                return copy(kT[:, parity, n * CH:(n + 1) * CH], ring[slot][:])
            return copy(v_sb[:, parity, n * (CH // P):(n + 1) * (CH // P), :],
                        ring[slot][:].rearrange("p (a c) -> p a c", c=P))

        for use in PROLOGUE:
            kind, n, _ = use
            slot = use_slot(-1, use)
            act.wait_ge(ring_full, use_index(-1, use) + 1)
            if kind == "X":
                ins = copy(xnT[:, n, :], ring[slot][:])
            elif kind == "Q":
                ins = take_q(0, slot)
            else:
                ins = take_kv(kind, 0, n, slot)
            ins.then_inc(ring_free, 1)

        def exponentials(t, q):
            act.wait_ge(max_ready, t + 1)
            act.activation(probs[:, q, :], scores[:, q, :], ACT.Exp, bias=neg_max[:, q:q + 1], scale=float(D) ** -0.5,
                           accum_out=full_sum[:, q:q + 1]).then_inc(exp_done, 1)

        def take_output(t, j):
            head, half = j // 2, j % 2
            act.wait_ge(pv_done, 4 * t + 4)
            act.wait_ge(norm_ready, t + 1)
            act.activation(o_pair[:, half, head * D:(head + 1) * D], o_acc[j % 2][:, 0:D], ACT.Copy,
                           scale=inv_denom[:, j % 2:j % 2 + 1]).then_inc(o_read, 1)

        def pair(g, parity):
            first, last, left = (isinstance(g, int) and g == k for k in (0, PAIRS - 1, PAIRS))
            for use in (uses_of(g) if isinstance(g, int) else ORDER):
                kind, j, c = use
                t = 4 * g + j
                slot = use_slot(g, use)
                if left and kind == "QO":
                    take_output(4 * PAIRS - 1, 3)
                act.wait_ge(ring_full, use_index(g, use) + 1)
                if kind == "S":
                    if not (first and j < 2):
                        act.wait_ge(masked, t - 1)
                    copy(scores[:, j % 2, c * CH:(c + 1) * CH], ring[slot][:]).then_inc(ring_free, 1)
                elif kind == "T":
                    if not (first and j == 2 and c < 2):
                        act.wait_ge(pv_done, 4 * (t - 2) + (c - 1))
                    copy(probsT[:, c % 2, :], ring[slot][:]).then_inc(ring_free, 1)
                elif kind in "KV":
                    take_kv(kind, 1 - parity, j, slot).then_inc(ring_free, 1)
                elif kind == "QO":
                    if not first:
                        ins = copy(oT[:], ring[slot][:, 512:512 + TT * P])
                    if not (last or left):
                        ins = take_q(1 - parity, slot)
                    ins.then_inc(ring_free, 1)
                elif kind == "OP":
                    if not (isinstance(g, int) and g == 1):
                        act.wait_ge(x_added, g - 1)
                    copy(o_proj[:].rearrange("p t c -> p (t c)"), ring[slot][:, 0:TT * DM]).then_inc(ring_free, 1)
                if c == 1 and (kind == "T" or (kind == "S" and first and j < 2)):
                    if not (first and j < 3):
                        take_output(t - 3, (j - 3) % 4)
                    if not (first and j == 0) and not (left and j == 1):
                        exponentials(t - 1, (j - 1) % 2)

        pair(0, 0)
        pair(1, 1)
        with act.Fori(1, PAIRS // 2 - 1) as i:
            pair(2 * i, 0)
            pair(2 * i + 1, 1)
        pair(PAIRS - 2, 0)
        pair(PAIRS - 1, 1)
        pair(PAIRS, 0)

    @block.tensor
    def _(pe):
        def begin(index):
            if not (isinstance(index, int) and index < 3):
                pe.wait_ge(ring_free, index - 2)

        def turn_x(c, slot):
            for i in range(B * TT):
                last = pe.transpose(ring[slot][:, i * P:(i + 1) * P], xn[:, i, c * P:(c + 1) * P], ident[:])
            return last

        def project_q(g, parity, slot):
            if isinstance(g, int):
                at = g // NB * T
            else:
                at = (g // NB) * T
            for c in range(2):
                last = pe.matmul(ring[slot][:, 0:T], weights[:, parity, c * P:(c + 1) * P],
                                 xnT[:, c, bass.ds(at, T)], start=(c == 0), stop=(c == 1))
            return last

        def project_k(parity, n, slot):
            for u in range(CH // 512):
                for c in range(2):
                    at = n * CH + u * 512
                    last = pe.matmul(ring[slot][:, u * 512:(u + 1) * 512], weights[:, parity, (2 + c) * P:(3 + c) * P],
                                     ctx_sb[:, c, at:at + 512], start=(c == 0), stop=(c == 1))
            return last

        def project_v(parity, n, slot):
            for i in range(CH // P):
                for c in range(2):
                    at = n * CH + i * P
                    last = pe.matmul(ring[slot][:, i * P:(i + 1) * P], ctx_sb[:, c, at:at + P],
                                     weights[:, parity, (4 + c) * P:(5 + c) * P], start=(c == 0), stop=(c == 1))
            return last

        def need_context(g, n):
            pe.wait_ge(ctx_in[n], (g // NB) * 16 + 16)

        pe.wait_ge(ident_step, 3)
        pe.wait_ge(xn_ready, 1)
        for use in PROLOGUE:
            kind, n, _ = use
            slot = use_slot(-1, use)
            begin(use_index(-1, use))
            if kind == "X":
                ins = turn_x(n, slot)
            elif kind == "Q":
                pe.wait_ge(weights_in[0], 16)
                pe.wait_ge(ring_free, 2)
                ins = project_q(0, 0, slot)
            elif kind == "K":
                need_context(0, n)
                ins = project_k(0, n, slot)
            else:
                ins = project_v(0, n, slot)
            ins.then_inc(ring_full, 1)
        pe.wait_ge(pick_ready, 1)
        pe.wait_ge(bias_ready, 1)
        pe.wait_ge(ring_free, len(PROLOGUE))

        def multiply_values(tile, j, v_parity, c, index):
            pe.wait_ge(ring_free, index + 1)
            head = j // 2
            for i in range(CH // P):
                last = pe.matmul(o_acc[j % 2][:, 0:D], probsT[:, c % 2, i * P:(i + 1) * P],
                                 v_sb[:, v_parity, c * (CH // P) + i, head * D:(head + 1) * D],
                                 start=(c == 0 and i == 0), stop=(c == NC - 1 and i == CH // P - 1))
            last.then_inc(pv_done, 1)

        def pair(g, i, parity):
            first, last, left = (isinstance(g, int) and g == k for k in (0, PAIRS - 1, PAIRS))

            def tile_back(j, steps):
                back = j - steps
                return 4 * g + back, back % 4, parity if back >= 0 else 1 - parity

            def last_chunk(j):
                tile, jj, vp = tile_back(j, 3)
                where = (g, ("T", j - 1, NC - 1)) if j else ((g - 1), ("T", 3, NC - 1))
                multiply_values(tile, jj, vp, NC - 1, use_index(*where))

            for use in (uses_of(g) if isinstance(g, int) else ORDER):
                kind, j, c = use
                slot = use_slot(g, use)
                index = use_index(g, use)
                if left and kind == "T" and c == 0:
                    last_chunk(j)
                if left and kind == "QO":
                    last_chunk(2)
                begin(index)
                if kind == "S":
                    head, half = j // 2, j % 2
                    b = g // NB
                    for u in range(CH // 512):
                        o = ring[slot][:, u * 512:(u + 1) * 512]
                        at = c * CH + u * 512
                        pe.matmul(o, qT[head * D:(head + 1) * D, parity, half * P:(half + 1) * P],
                                  kT[head * D:(head + 1) * D, parity, at:at + 512], start=True, stop=False)
                        row = pick[:, b, :] if isinstance(g, int) else pick[:, bass.ds(b, 1), :].rearrange("k a t -> k (a t)")
                        ins = pe.matmul(o, row, mask_bias[:, at:at + 512], start=False, stop=True)
                    ins.then_inc(ring_full, 1)
                    if c == 0 and not (first and j < 3):
                        last_chunk(j)
                elif kind == "T":
                    tile, jj, vp = tile_back(j, 2)
                    if c == 0:
                        pe.wait_ge(masked, tile + 1)
                    for k in range(CH // P):
                        at = c * CH + k * P
                        ins = pe.transpose(ring[slot][:, k * P:(k + 1) * P], probs[:, jj % 2, at:at + P], ident[:])
                    ins.then_inc(ring_full, 1)
                    if c == 1 and not (first and j < 4):
                        pe.wait_ge(o_read, tile - 1)
                    if c >= 1:
                        multiply_values(tile, jj, vp, c - 1, use_index(g, ("T", j, c - 1)))
                elif kind in "KV":
                    if j == 0 and kind == "K":
                        pe.wait_ge(weights_in[1 - parity], (i + 1 + parity) * 16)
                    if kind == "K":
                        need_context(g + 1, j)
                        project_k(1 - parity, j, slot).then_inc(ring_full, 1)
                    else:
                        project_v(1 - parity, j, slot).then_inc(ring_full, 1)
                elif kind == "QO":
                    if not first:
                        pe.wait_ge(o_read, 4 * g)
                        for half in range(TT):
                            ins = pe.transpose(ring[slot][:, 512 + half * P:512 + (half + 1) * P], o_pair[:, half, :],
                                               ident[:])
                    if not (last or left):
                        ins = project_q(g + 1, 1 - parity, slot)
                    ins.then_inc(ring_full, 1)
                elif kind == "OP":
                    pe.wait_ge(ring_free, use_index(g, ("QO", 0, 0)) + 1)
                    pe.wait_ge(wo_in[1 - parity], (i + parity) * 16)
                    for half in range(TT):
                        ins = pe.matmul(ring[slot][:, half * DM:(half + 1) * DM], oT[:, half * P:(half + 1) * P],
                                        wo_sb[:, 1 - parity, :], start=True, stop=True)
                    ins.then_inc(ring_full, 1)

        pair(0, 0, 0)
        pair(1, 0, 1)
        with pe.Fori(1, PAIRS // 2 - 1) as i:
            pair(2 * i, i, 0)
            pair(2 * i + 1, i, 1)
        pair(PAIRS - 2, PAIRS // 2 - 1, 0)
        pair(PAIRS - 1, PAIRS // 2 - 1, 1)
        pair(PAIRS, PAIRS // 2, 0)


I = 704
IT = -(-I // P)
FH, FD = 16, 16
FPAD = 32
QC = FH * FPAD // P
HG = 4
UNITS = TT * (FH // HG)
BLK = 16
PHASE = 0.1 * math.sin(2.0 * math.pi * 0.25)
OUT_EPS = 0.1 * math.sin(2.0 * math.pi * 0.5)
ROUND_HALF = 1.5 * 2.0 ** 22
ROUND_ONE = 1.5 * 2.0 ** 23
ROUND_TWO = 1.5 * 2.0 ** 24
TWO_PI_A = 6.28125
TWO_PI_B = float(np.float32(2.0 * math.pi - 6.28125))
TWO_PI_C = 2.0 * math.pi - 6.28125 - TWO_PI_B
PI_BELOW = 3.1415925


def head_of(u, h):
    return h * (FH // HG) + u % (FH // HG)


def self_attention_and_ffn(nc, ctx, x_sb, ident, out, sa_wq, sa_wk, sa_wv, sa_wo, sa_cols, sa_rows, rby, freqs, positions,
                           w_gate, w_up, w_down):
    def sb(name, shape, dt=F32):
        return ctx.enter_context(nc.sbuf_tensor(name, shape, dt))

    def psum(name, shape, dt=F32):
        return ctx.enter_context(nc.psum_tensor(name, shape, dt))

    def sem(name):
        return ctx.enter_context(nc.semaphore(name))

    wq_sb = sb("wq_sb", [P, 2, QC * P])
    wk_sb = sb("wk_sb", [P, 2, QC * P])
    wv_sb = sb("wv_sb", [P, 2, DM])
    wo2_sb = sb("wo2_sb", [P, 2, DM])
    cols = sb("cols", [P, 2, QC])
    rows = sb("rows", [P, 4, DM])
    rby_sb = sb("rby_sb", [P, 3])
    freqs_sb = sb("freqs_sb", [P, DM // 2])
    pos_sb = sb("pos_sb", [P, TT])
    logit_scale = sb("logit_scale", [P, 1])
    out_scale = sb("out_scale", [P, 1])
    eps2 = sb("eps2", [P, 1])
    eps1 = sb("eps1", [P, 1])
    gamma_scale = sb("gamma_scale", [P, 1])
    small = sb("small", [P, 1])
    angle = sb("angle", [P, TT, DM // 2])
    turns = sb("turns", [P, TT, DM // 2])
    reduced = sb("reduced", [P, 2, TT, DM // 2])
    encoding = sb("encoding", [P, TT, DM])
    gate_in = sb("gate_in", [P, IT * DM])
    up_in = sb("up_in", [P, IT * DM])
    down_in = sb("down_in", [P, TT * I])
    gateT = sb("gateT", [P, 2, IT * P])
    upT = sb("upT", [P, 2, IT * P])
    downT = sb("downT", [P, IT, DM])
    WIDE = IT * DM
    qa = sb("qa", [P, WIDE])
    qb = sb("qb", [P, WIDE])
    qn = sb("qn", [P, WIDE])
    scale = sb("scale", [P, WIDE // BLK])
    inv_scale = sb("inv_scale", [P, WIDE // BLK])
    stats2 = sb("stats2", [P, TT, 6])
    mv2 = sb("mv2", [P, TT, 2])
    std2 = sb("std2", [P, TT])
    rstd2 = sb("rstd2", [P, TT])
    xq = sb("xq", [P, TT, DM])
    turned = sb("turned", [P, 2, T])
    q_sb = sb("q_sb", [P, QC, T])
    k_sb = sb("k_sb", [P, QC, T])
    v2_sb = sb("v2_sb", [P, TT, DM])
    neg_top = sb("neg_top", [P, 2, HG])
    e_sb = sb("e_sb", [P, 2, HG, T])
    sums = sb("sums", [P, TT, FH])
    inv_sums = sb("inv_sums", [P, TT, FH])
    eT_sb = sb("eT_sb", [P, 2, HG * TT * P])
    o_sb = sb("o_sb", [P, TT, DM])
    y_sb = sb("y_sb", [P, TT, DM])
    xf = sb("xf", [P, TT, DM])
    xfq = sb("xfq", [P, TT, DM])
    silu_sb = sb("silu_sb", [P, I])
    h_sb = sb("h_sb", [P, I])
    hq_sb = sb("hq_sb", [P, I])
    hT_sb = sb("hT_sb", [P, IT * P])
    x_out = sb("x_out", [P, TT, DM])

    logits = [psum(f"logits{i}", [P, HG * T]) for i in range(2)]
    eT_ps = psum("eT_ps", [P, HG * TT * P])
    o_ps = psum("o_ps", [P, 512])
    turn_ps = psum("turn_ps", [P, 512])

    consts_in = sem("consts_in")
    ffn_in = sem("ffn_in")
    prep_step = sem("prep_step")
    reduced_ready = sem("reduced_ready")
    encoding_ready = sem("encoding_ready")
    w_quant = sem("w_quant")
    w_turned = sem("w_turned")
    w_taken = sem("w_taken")
    dve_step = sem("dve_step")
    var_ready = sem("var_ready")
    std_done = sem("std_done")
    rows_ready = sem("rows_ready")
    turned_full = sem("turned_full")
    turned_taken = sem("turned_taken")
    q_full, k_full, v_full = sem("q_full"), sem("k_full"), sem("v_full")
    q_taken, k_taken, v_taken = sem("q_taken"), sem("k_taken"), sem("v_taken")
    logits_full, top_ready, exp_ready = sem("logits_full"), sem("top_ready"), sem("exp_ready")
    eT_full, eT_taken, av_done = sem("eT_full"), sem("eT_taken"), sem("av_done")
    proj_full = sem("proj_full")
    gate_full, up_full, silu_ready = sem("gate_full"), sem("up_full"), sem("silu_ready")
    hq_ready, hT_full, hT_taken = sem("hq_ready"), sem("hT_full"), sem("hT_taken")
    down_full, row_done, out_done = sem("down_full"), sem("row_done"), [sem(f"out_done{i}") for i in range(TT)]

    block = ctx.enter_context(nc.Block())
    HALVES = [(0, 512), (512, I - 512)]

    def weight_turned(dst, n):
        if dst == 2:
            return downT[:, 2 * n:2 * n + 2, :].rearrange("p a c -> p (a c)")
        return (gateT, upT)[dst][:, n, :]

    WEIGHT_TURNS = [(0, 0), (0, 1), (1, 0), (1, 1), (2, 0), (2, 1), (2, 2)]


    @block.sync
    def _(sp):
        for dst, src in ((wq_sb, sa_wq), (wk_sb, sa_wk), (wv_sb, sa_wv), (wo2_sb, sa_wo), (cols, sa_cols),
                         (rows, sa_rows), (rby_sb, rby), (freqs_sb, freqs), (pos_sb, positions)):
            sp.dma_start(dst[:], src).then_inc(consts_in, 16)
        for dst, src in ((gate_in, w_gate), (up_in, w_up), (down_in, w_down)):
            sp.dma_start(dst[:], src).then_inc(ffn_in, 16)
        out_rows = out.rearrange("b (t p) c -> b p t c", p=P)
        with sp.Fori(0, B) as b:
            for half in range(TT):
                sp.wait_ge(row_done, b * TT + half + 1)
                sp.dma_start(out_rows[b, :, half, :], x_out[:, half, :]).then_inc(out_done[half], 16)
        for half in range(TT):
            sp.wait_ge(out_done[half], 16 * B)

    @block.vector
    def _(dve):
        class Chain:
            def __init__(self, sem):
                self.sem, self.n = sem, 0

            def __call__(self, ins):
                self.n += 1
                ins.then_inc(self.sem, 1)
                dve.wait_ge(self.sem, self.n)

            def restart(self):
                self.n += 1
                dve.memset(small[:], 0.0).then_inc(self.sem, 1)
                dve.wait_ge(self.sem, self.n)
                dve.sem_clear(self.sem)

        def quantise(link, dst, src, n):
            k = n // BLK
            blocks = src.rearrange("p (k e) -> p k e", e=BLK)

            def blocked(t):
                return t[:, 0:n].rearrange("p (k e) -> p k e", e=BLK)

            def spread(t):
                return t[:, 0:k].unsqueeze(2).broadcast_to((P, k, BLK))

            link(dve.tensor_reduce(scale[:, 0:k], blocks, AX.X, ALU.max, apply_absolute_value=True))
            link(dve.tensor_scalar(scale[:, 0:k], scale[:, 0:k], 1.0 / 6.0, 1e-12, ALU.mult, ALU.max))
            link(dve.reciprocal(inv_scale[:, 0:k], scale[:, 0:k]))
            link(dve.tensor_scalar(inv_scale[:, 0:k], inv_scale[:, 0:k], 1.0 - 2.0 ** -24, None, ALU.mult))
            link(dve.tensor_tensor(blocked(qn), blocks, spread(inv_scale), ALU.mult))
            link(dve.tensor_scalar(qn[:, 0:n].bitcast(U32), qn[:, 0:n].bitcast(U32), 0x7FFFFFFF, None,
                                   ALU.bitwise_and))
            link(dve.tensor_scalar(qa[:, 0:n], qn[:, 0:n], 2.0, ROUND_HALF, ALU.min, ALU.add))
            link(dve.tensor_scalar(qb[:, 0:n], qn[:, 0:n], 4.0, 2.0, ALU.min, ALU.max))
            link(dve.tensor_scalar(qb[:, 0:n], qb[:, 0:n], ROUND_ONE, ROUND_ONE + 2.0, ALU.add, ALU.subtract))
            link(dve.scalar_tensor_tensor(out=qa[:, 0:n], in0=qa[:, 0:n], scalar=ROUND_HALF, in1=qb[:, 0:n],
                                          op0=ALU.subtract, op1=ALU.add))
            link(dve.tensor_scalar(qn[:, 0:n], qn[:, 0:n], 4.0, ROUND_TWO, ALU.max, ALU.add))
            link(dve.scalar_tensor_tensor(out=qa[:, 0:n], in0=qn[:, 0:n], scalar=ROUND_TWO + 4.0, in1=qa[:, 0:n],
                                          op0=ALU.subtract, op1=ALU.add))
            link(dve.tensor_tensor(blocked(qa), blocked(qa), spread(scale), ALU.mult))
            return dve.scalar_tensor_tensor(out=dst.bitcast(U32), in0=src.bitcast(U32), scalar=0x80000000,
                                            in1=qa[:, 0:n].bitcast(U32), op0=ALU.bitwise_and, op1=ALU.bitwise_or)

        link = Chain(prep_step)
        dve.memset(eps1[:], EPS)
        dve.wait_ge(consts_in, 16 * 9)
        red, blue, yellow = (rby_sb[:, i:i + 1] for i in range(3))
        MUL, ADD = ALU.mult, ALU.add

        def weighted(dst, base, *terms):
            link(dve.memset(dst, base))
            for col, w in terms:
                link(dve.scalar_tensor_tensor(out=dst, in0=col, scalar=w, in1=dst, op0=MUL, op1=ADD))

        weighted(logit_scale[:], 1.0, (red, 0.1), (blue, 0.05), (yellow, 0.15))
        link(dve.tensor_scalar(logit_scale[:], logit_scale[:], FD ** -0.5, None, MUL))
        weighted(out_scale[:], 1.0, (yellow, OUT_EPS))
        weighted(gamma_scale[:], 1.0, (red, 0.1), (yellow, 0.05))
        weighted(eps2[:], 1.0, (blue, 0.1))
        link(dve.tensor_scalar(eps2[:], eps2[:], EPS, None, MUL))
        link(dve.tensor_scalar(rows[:, 2, :], rows[:, 2, :], gamma_scale[:], None, MUL))
        weighted(small[:], 1.0, (yellow, PHASE))
        link(dve.tensor_scalar(freqs_sb[:], freqs_sb[:], small[:], None, MUL))
        link(dve.reciprocal(freqs_sb[:], freqs_sb[:]))
        for half in range(TT):
            link(dve.tensor_scalar(angle[:, half, :], freqs_sb[:], pos_sb[:, half:half + 1], None, MUL))
        for c in range(2):
            link(dve.tensor_scalar(turns[:], angle[:], 0.5 / math.pi, 0.25 * c, MUL, ADD))
            link(dve.tensor_scalar(turns[:], turns[:], ROUND_ONE, ROUND_ONE, ADD, ALU.subtract))
            link(dve.scalar_tensor_tensor(out=reduced[:, c], in0=turns[:], scalar=-TWO_PI_A, in1=angle[:], op0=MUL, op1=ADD))
            for part in (TWO_PI_B, TWO_PI_C):
                link(dve.scalar_tensor_tensor(out=reduced[:, c], in0=turns[:], scalar=-part, in1=reduced[:, c],
                                              op0=MUL, op1=ADD))
            if c:
                link(dve.tensor_scalar(reduced[:, c], reduced[:, c], 0.5 * math.pi, None, ADD))
            link(dve.tensor_scalar(reduced[:, c], reduced[:, c], PI_BELOW, -PI_BELOW, ALU.min, ALU.max))
        dve.sem_inc(reduced_ready, 1)
        dve.wait_ge(ffn_in, 16 * 3)
        for t, n in ((gate_in, IT * DM), (up_in, IT * DM), (down_in, TT * I)):
            link(quantise(link, t[:, 0:n], t[:, 0:n], n))
            dve.sem_inc(w_quant, 1)
        dve.wait_ge(encoding_ready, 1)

        def normalise(link, dst, src, k, eps_ready=None):
            for half in range(TT):
                ins = dve.bn_stats(stats2[:, half, :], src[:, half, :])
            link(ins)
            for half in range(TT):
                ins = dve.bn_aggr(mv2[:, half, :], stats2[:, half, :])
            ins.then_inc(var_ready, 1)
            dve.wait_ge(std_done, k + 1)
            link(dve.reciprocal(rstd2[:], std2[:]))
            for half in range(TT):
                ins = dve.tensor_scalar(dst[:, half, :], src[:, half, :], mv2[:, half, 0:1], rstd2[:, half:half + 1],
                                        ALU.subtract, MUL)
            return ins

        def batch(b):
            link = Chain(dve_step)
            x_rows = x_sb[:, bass.ds(b * TT, TT), :]
            link(normalise(link, xq, x_rows, 3 * b))
            dve.tensor_tensor(xq[:], xq[:], encoding[:], ADD).then_inc(rows_ready, 1)
            dve.wait_ge(q_full, b + 1)
            for c in range(QC):
                ins = dve.tensor_scalar(q_sb[:, c, :], logits[0][:, c * T:(c + 1) * T], cols[:, 0, c:c + 1],
                                        logit_scale[:], ADD, MUL)
            ins.then_inc(q_taken, 1)
            dve.wait_ge(v_full, b + 1)
            dve.tensor_tensor(v2_sb[:], o_ps[:].rearrange("p (t c) -> p t c", c=DM),
                              rows[:, 0, :].unsqueeze(1).broadcast_to((P, TT, DM)), ADD).then_inc(v_taken, 1)

            def take_turned(u):
                dve.wait_ge(eT_full, b * UNITS + u + 1)
                if u >= 2:
                    dve.wait_ge(av_done, b * UNITS + u - 1)
                dve.tensor_copy(eT_sb[:, u % 2, :], eT_ps[:]).then_inc(eT_taken, 1)

            for u in range(UNITS):
                dve.wait_ge(logits_full, b * UNITS + u + 1)
                if u >= 2:
                    dve.wait_ge(exp_ready, b * UNITS + u - 1)
                dve.tensor_reduce(neg_top[:, u % 2, :], logits[u % 2][:].rearrange("p (h k) -> p h k", k=T), AX.X,
                                  ALU.max, negate=True).then_inc(top_ready, 1)
                if u >= 1:
                    take_turned(u - 1)
            take_turned(UNITS - 1)
            dve.wait_ge(exp_ready, (b + 1) * UNITS)
            link(dve.reciprocal(inv_sums[:], sums[:]))
            link(dve.tensor_scalar(inv_sums[:], inv_sums[:], out_scale[:], None, MUL))
            dve.wait_ge(av_done, (b + 1) * UNITS)
            dve.tensor_tensor(o_sb[:].rearrange("p t (h d) -> p (t h) d", d=FD), o_ps[:].rearrange("p (k d) -> p k d", d=FD),
                              inv_sums[:].rearrange("p t h -> p (t h)").unsqueeze(2).broadcast_to((P, TT * FH, FD)),
                              MUL).then_inc(rows_ready, 1)
            link(dve.tensor_tensor(xq[:], xq[:], rows[:, 1, :].unsqueeze(1).broadcast_to((P, TT, DM)), ADD))
            dve.wait_ge(proj_full, b + 1)
            link(dve.tensor_tensor(y_sb[:], eT_ps[:, 0:512].rearrange("p (t c) -> p t c", c=DM), xq[:], ADD))
            link(normalise(link, y_sb, y_sb, 3 * b + 1))
            link(dve.tensor_tensor(y_sb[:], y_sb[:], rows[:, 2, :].unsqueeze(1).broadcast_to((P, TT, DM)), MUL))
            link(dve.tensor_tensor(y_sb[:], y_sb[:], rows[:, 3, :].unsqueeze(1).broadcast_to((P, TT, DM)), ADD))
            link(dve.tensor_tensor(y_sb[:], y_sb[:], x_rows, ADD))
            link(normalise(link, xf, y_sb, 3 * b + 2))
            flat = "p t c -> p (t c)"
            quantise(link, xfq[:].rearrange(flat), xf[:].rearrange(flat), TT * DM).then_inc(rows_ready, 1)
            for half in range(TT):
                n = b * TT + half + 1
                dve.wait_ge(silu_ready, n)
                dve.wait_ge(up_full, n)
                link(dve.tensor_tensor(h_sb[:], silu_sb[:], logits[1][:, 0:I], MUL))
                quantise(link, hq_sb[:], h_sb[:], I).then_inc(hq_ready, 1)
                dve.wait_ge(down_full, n)
                if not isinstance(b, int):
                    dve.wait_ge(out_done[half], 16 * b)
                dve.tensor_tensor(x_out[:, half, :], o_ps[:, 0:DM], y_sb[:, half, :], ADD).then_inc(row_done, 1)
            link.restart()

        batch(0)
        with dve.Fori(1, B) as b:
            batch(b)

    @block.scalar
    def _(act):
        act.wait_ge(reduced_ready, 1)
        act.activation(encoding[:, :, 0:DM:2], reduced[:, 0], ACT.Sin)
        act.activation(encoding[:, :, 1:DM:2], reduced[:, 1], ACT.Sin).then_inc(encoding_ready, 1)
        for k, (dst, n) in enumerate(WEIGHT_TURNS):
            act.wait_ge(w_turned, k + 1)
            act.activation(weight_turned(dst, n), logits[k % 2][:, 0:IT * P] if dst < 2 else
                           logits[k % 2][:, 0:512], ACT.Copy).then_inc(w_taken, 1)

        def std(k, eps):
            act.wait_ge(var_ready, k + 1)
            act.activation(std2[:], mv2[:, :, 1], ACT.Sqrt, bias=eps[:]).then_inc(std_done, 1)

        def take_turned(k):
            act.wait_ge(turned_full, k + 1)
            act.activation(turned[:].rearrange("p c t -> p (c t)"), turn_ps[:], ACT.Copy).then_inc(turned_taken, 1)

        with act.Fori(0, B) as b:
            std(3 * b, eps1)
            take_turned(3 * b)
            act.wait_ge(k_full, b + 1)
            for c in range(QC):
                ins = act.activation(k_sb[:, c, :], logits[1][:, c * T:(c + 1) * T], ACT.Identity, bias=cols[:, 1, c:c + 1])
            ins.then_inc(k_taken, 1)
            for u in range(UNITS):
                act.wait_ge(top_ready, b * UNITS + u + 1)
                if u >= 2:
                    act.wait_ge(eT_full, b * UNITS + u - 1)
                for h in range(HG):
                    half, head = u // (FH // HG), head_of(u, h)
                    ins = act.activation(e_sb[:, u % 2, h, :], logits[u % 2][:, h * T:(h + 1) * T], ACT.Exp,
                                         bias=neg_top[:, u % 2, h:h + 1], accum_out=sums[:, half, head:head + 1])
                ins.then_inc(exp_ready, 1)
            take_turned(3 * b + 1)
            std(3 * b + 1, eps2)
            std(3 * b + 2, eps1)
            take_turned(3 * b + 2)
            for half in range(TT):
                n = b * TT + half + 1
                act.wait_ge(gate_full, n)
                act.activation(silu_sb[:], logits[0][:, 0:I], ACT.Silu).then_inc(silu_ready, 1)
                act.wait_ge(hT_full, n)
                act.activation(hT_sb[:, 0:5 * P], eT_ps[:, 0:5 * P], ACT.Copy)
                act.activation(hT_sb[0:I - 5 * P, 5 * P:6 * P], eT_ps[0:I - 5 * P, 5 * P:6 * P], ACT.Copy).then_inc(hT_taken, 1)

    @block.tensor
    def _(pe):
        for k, (dst, n) in enumerate(WEIGHT_TURNS):
            pe.wait_ge(w_quant, dst + 1)
            if k >= 2:
                pe.wait_ge(w_taken, k - 1)
            o = logits[k % 2]
            if dst < 2:
                src = (gate_in, up_in)[dst]
                for i in range(IT):
                    ins = pe.transpose(o[:, i * P:(i + 1) * P], src[:, i * DM + n * P:i * DM + (n + 1) * P], ident[:])
            else:
                for i in range(2):
                    kk = 2 * n + i
                    w = min(P, I - kk * P)
                    for r in range(TT):
                        ins = pe.transpose(o[0:w, i * DM + r * P:i * DM + (r + 1) * P],
                                           down_in[:, r * I + kk * P:r * I + kk * P + w], ident[:])
            ins.then_inc(w_turned, 1)
        pe.wait_ge(w_taken, len(WEIGHT_TURNS))

        def turn(k, src):
            pe.wait_ge(rows_ready, k + 1)
            for c in range(2):
                for half in range(TT):
                    at = c * T + half * P
                    ins = pe.transpose(turn_ps[:, at:at + P], src[:, half, c * P:(c + 1) * P], ident[:])
            ins.then_inc(turned_full, 1)
            pe.wait_ge(turned_taken, k + 1)

        def halves(half):
            return slice(half * P, (half + 1) * P)

        with pe.Fori(0, B) as b:
            turn(3 * b, xq)
            for w, o, full in ((wq_sb, logits[0], q_full), (wk_sb, logits[1], k_full)):
                for m in range(QC):
                    for c in range(2):
                        ins = pe.matmul(o[:, m * T:(m + 1) * T], w[:, c, m * P:(m + 1) * P], turned[:, c, :],
                                        start=(c == 0), stop=(c == 1))
                ins.then_inc(full, 1)
            for half in range(TT):
                for c in range(2):
                    ins = pe.matmul(o_ps[:, half * DM:(half + 1) * DM], turned[:, c, halves(half)], wv_sb[:, c, :],
                                    start=(c == 0), stop=(c == 1))
            ins.then_inc(v_full, 1)
            pe.wait_ge(q_taken, b + 1)
            pe.wait_ge(k_taken, b + 1)

            def values(u):
                pe.wait_ge(eT_taken, b * UNITS + u + 1)
                half = u // (FH // HG)
                for h in range(HG):
                    head = head_of(u, h)
                    for s in range(TT):
                        at = (h * TT + s) * P
                        ins = pe.matmul(o_ps[:, half * DM + head * FD:half * DM + (head + 1) * FD],
                                        eT_sb[:, u % 2, at:at + P], v2_sb[:, s, head * FD:(head + 1) * FD],
                                        start=(s == 0), stop=(s == TT - 1))
                ins.then_inc(av_done, 1)

            def turn_probs(u):
                pe.wait_ge(exp_ready, b * UNITS + u + 1)
                if u >= 1:
                    pe.wait_ge(eT_taken, b * UNITS + u)
                for h in range(HG):
                    for s in range(TT):
                        at = (h * TT + s) * P
                        ins = pe.transpose(eT_ps[:, at:at + P], e_sb[:, u % 2, h, s * P:(s + 1) * P], ident[:])
                ins.then_inc(eT_full, 1)

            for u in range(UNITS):
                half = u // (FH // HG)
                if u >= 2:
                    pe.wait_ge(exp_ready, b * UNITS + u - 1)
                for h in range(HG):
                    head = head_of(u, h)
                    r = head * FPAD % P
                    ins = pe.matmul(logits[u % 2][:, h * T:(h + 1) * T], q_sb[r:r + FPAD, head * FPAD // P, halves(half)],
                                    k_sb[r:r + FPAD, head * FPAD // P, :], start=True, stop=True)
                ins.then_inc(logits_full, 1)
                if u == 1:
                    pe.wait_ge(v_taken, b + 1)
                if u >= 1:
                    turn_probs(u - 1)
                if u >= 2:
                    values(u - 2)
            turn_probs(UNITS - 1)
            values(UNITS - 2)
            values(UNITS - 1)
            turn(3 * b + 1, o_sb)
            for half in range(TT):
                for c in range(2):
                    ins = pe.matmul(eT_ps[:, half * DM:(half + 1) * DM], turned[:, c, halves(half)], wo2_sb[:, c, :],
                                    start=(c == 0), stop=(c == 1))
            ins.then_inc(proj_full, 1)
            turn(3 * b + 2, xfq)
            for half in range(TT):
                n = b * TT + half + 1
                for w, o, full in ((gateT, logits[0], gate_full), (upT, logits[1], up_full)):
                    for at, width in HALVES:
                        for c in range(2):
                            ins = pe.matmul(o[:, at:at + width], turned[:, c, halves(half)], w[:, c, at:at + width],
                                            start=(c == 0), stop=(c == 1))
                    ins.then_inc(full, 1)
                pe.wait_ge(hq_ready, n)
                for i in range(IT):
                    w = min(P, I - i * P)
                    ins = pe.transpose(eT_ps[0:w, i * P:(i + 1) * P], hq_sb[:, i * P:i * P + w], ident[:])
                ins.then_inc(hT_full, 1)
                pe.wait_ge(hT_taken, n)
                for i in range(IT):
                    w = min(P, I - i * P)
                    ins = pe.matmul(o_ps[:, 0:DM], hT_sb[0:w, i * P:(i + 1) * P], downT[0:w, i, :],
                                    start=(i == 0), stop=(i == IT - 1))
                ins.then_inc(down_full, 1)
                pe.wait_ge(row_done, n)


def kernel(**inputs):
    import concourse.bacc as _bacc
    from concourse.bass_utils import run_bass_kernel_spmd as _run

    a = {k: np.asarray(v) for k, v in inputs.items()}
    half = P // 2

    def pair_columns(w):
        return w.reshape(2, P, NB, P).transpose(2, 1, 0, 3).reshape(NB, P, 2 * P)

    def rows_of(w):
        return w.reshape(-1, P, w.shape[1]).transpose(1, 0, 2)

    def padded_heads(w):
        w = w.reshape(FH, FD, -1)
        return np.concatenate([w, np.zeros((FH, FPAD - FD, w.shape[2]), w.dtype)], axis=1).reshape(FH * FPAD, -1)

    def across(v):
        return np.broadcast_to(v[None, ...], (P,) + v.shape)

    def padded_rows(w):
        return np.concatenate([w, np.zeros((IT * P - I, w.shape[1]), w.dtype)], axis=0)

    freqs = np.power(np.float32(10000.0), (2.0 * np.arange(0, DM, 2, dtype=np.float32) / DM).astype(np.float32))
    temps = np.repeat(a["L0_xattn_inv_temp"].reshape(NB, 2), half, axis=1)[:, :, None]
    arrays = {
        "x": a["x"],
        "ctx_t": a["ctx_1024"].transpose(0, 2, 1).reshape(B, 2, P, S),
        "mask": a["mask_BxS2_bf1"].view(np.uint8),
        "w_pack": np.concatenate([pair_columns(a["L0_xattn_Wq"]), pair_columns(a["L0_xattn_Wk"]),
                                  pair_columns(a["L0_xattn_Wv"]), temps], axis=2),
        "w_out": a["L0_xattn_Wo"].reshape(NB, P, DM),
        "sa_wq": rows_of(padded_heads(a["L0_attn_Wq"]).T),
        "sa_wk": rows_of(padded_heads(a["L0_attn_Wk"]).T),
        "sa_wv": rows_of(a["L0_attn_Wv"].T),
        "sa_wo": rows_of(a["L0_attn_Wo"].T),
        "sa_cols": np.stack([padded_heads(a[f"L0_attn_b{n}"][:, None]).reshape(QC, P).T for n in "qk"], axis=1),
        "sa_rows": across(np.stack([a["L0_attn_bv"], a["L0_attn_bo"], a["L0_attn_ln_gamma"], a["L0_attn_ln_beta"]])),
        "rby": across(a["L0_attn_rby"]),
        "freqs": across(freqs.astype(np.float32)),
        "positions": np.arange(T, dtype=np.float32).reshape(TT, P).T,
        "w_gate": rows_of(padded_rows(a["L0_ffn_w_gate"])).reshape(P, IT * DM),
        "w_up": rows_of(padded_rows(a["L0_ffn_w_up"])).reshape(P, IT * DM),
        "w_down": rows_of(a["L0_ffn_w_down"]).reshape(P, TT * I),
    }
    nc = _bacc.Bacc("TRN2", target_bir_lowering=False, num_devices=1, dynamic_dma_scratch_size=1024)
    aps = {}
    arrays = {k: np.ascontiguousarray(v) for k, v in arrays.items()}
    for name, v in arrays.items():
        aps[name] = nc.dram_tensor(name, v.shape, mybir.dt.from_np(v.dtype), kind="ExternalInput").ap()
    out = nc.dram_tensor("out", (B, T, DM), F32, kind="ExternalOutput").ap()
    build(nc, out=out, **aps)
    r = _run(nc, [arrays], core_ids=[0])
    return r.results[0]["out"]
```

```python
import math
from contextlib import ExitStack

import numpy as np
import concourse.bass as bass
from concourse import mybir

F32 = mybir.dt.float32
F32R = mybir.dt.float32r
BF16 = mybir.dt.bfloat16
I32 = mybir.dt.int32
U8 = mybir.dt.uint8
U32 = mybir.dt.uint32
ALU = mybir.AluOpType
ACT = mybir.ActivationFunctionType
AX = mybir.AxisListType
RMAX = bass.bass_isa.ReduceOp.max

P = 128
B, T, DM = 4, 256, 256
S = 4096
H, D = 16, 64
TOPK = 32
NB = 2 * H // 2 // 2
PAIRS = B * NB
TT = T // P
CH = 1024
NC = S // CH
GRP = 128
NG = S // GRP
RUN = 512
RUNS = B * S // RUN
SLOW = 8 * NG
MASKED = -1.0e30
LOWEST = -3.0e38
EPS = 1e-5


def pair_schedule():
    behind = {(1, 2): ["V0"], (1, 3): ["V1"], (2, 0): ["V2"], (2, 1): ["V3"], (2, 2): ["QO", "K0"], (2, 3): ["K1"],
              (3, 0): ["K2"], (3, 1): ["K3"], (3, 2): ["OP"]}
    order = []
    for j in range(4):
        for c in range(NC):
            order += [("S", j, c), ("T", j, c)]
            for what in behind.get((j, c), []):
                order.append((what, 0, 0) if what in ("QO", "OP") else (what[0], int(what[1]), 0))
    return order


ORDER = pair_schedule()
USES = len(ORDER)
assert USES % 3 == 0
PROLOGUE = [("X", c, 0) for c in range(2)] + [("Q", 0, 0)] + [("K", n, 0) for n in range(NC)]


def uses_of(g):
    def there(use):
        kind, j, _ = use
        late = (kind == "T" and j < 2) or kind == "OP"
        if g == 0:
            return not late
        if g == PAIRS - 1:
            return kind != "K"
        if g == PAIRS:
            return late or kind == "QO"
        return True
    uses = [u for u in ORDER if there(u)]
    if g == PAIRS:
        uses.remove(("OP", 0, 0))
        uses.append(("OP", 0, 0))
    return uses


INDEX = {}
for _use in PROLOGUE:
    INDEX[(-1, _use)] = len(INDEX)
for _g in range(PAIRS + 1):
    for _use in uses_of(_g):
        INDEX[(_g, _use)] = len(INDEX)
for _g in range(1, PAIRS - 1):
    assert all(INDEX[(_g, u)] == INDEX[(1, u)] + (_g - 1) * USES for u in ORDER)


def use_index(g, use):
    if isinstance(g, int):
        return INDEX[(g, use)]
    return g * USES + (INDEX[(1, use)] - USES)


def use_slot(g, use):
    return INDEX[(g if isinstance(g, int) else 1, use)] % 3


def build(nc, x, ctx_t, mask, w_pack, w_out, out, **later):
    with nc.sbuf_tensor("x_sb", [P, B * TT, DM], F32) as x_sb, nc.sbuf_tensor("ident", [P, P], F32) as ident:
        with ExitStack() as ctx:
            cross_attention(nc, ctx, x, ctx_t, mask, w_pack, w_out, x_sb, ident)
        with ExitStack() as ctx:
            self_attention_and_ffn(nc, ctx, x_sb, ident, out, **later)


def cross_attention(nc, ctx, x, ctx_t, mask, w_pack, w_out, x_sb, ident):
    def sb(name, shape, dt=F32):
        return ctx.enter_context(nc.sbuf_tensor(name, shape, dt))

    def psum(name, shape, dt=F32):
        return ctx.enter_context(nc.psum_tensor(name, shape, dt))

    def sem(name):
        return ctx.enter_context(nc.semaphore(name))

    WQ, WK, WV = 0, 4 * P, 6 * P
    WT = 8 * P
    WCOLS = 8 * P + 2
    ctx_sb = sb("ctx_sb", [P, 2, S])
    xnT = sb("xnT", [P, 2, B * T])
    weights = sb("weights", [P, 2, WCOLS])
    wo_sb = sb("wo_sb", [P, 2, DM])
    keys = sb("keys", [P, S])
    keys_split = sb("keys_split", [P, 2, S], F32R)
    v_sb = sb("v_sb", [P, S // P, P])
    q_both = sb("q_both", [P, 2, T])
    q_high = sb("q_high", [P, 2, 2, T], F32R)
    q_low = sb("q_low", [P, 2, 2, T], F32R)
    scores = sb("scores", [P, 2, S])
    probs = sb("probs", [P, 2, S])
    probsT = sb("probsT", [P, 2, CH])
    cand = sb("cand", [P, 8 * NG])
    cand_left = sb("cand_left", [P, 8 * NG])
    top = sb("top", [P, 2, TOPK])
    slow_cand = sb("slow_cand", [P, S // SLOW * TOPK])
    over = sb("over", [P, NG])
    waited = sb("waited", [P, NC + 1])
    pool_waited = sb("pool_waited", [P, NC + 1])
    suspect = sb("suspect", [P, 1])
    suspect_twice = sb("suspect_twice", [P, 1])
    suspect_all = sb("suspect_all", [P, 1])
    suspect_int = sb("suspect_int", [P, 2], I32)
    neg_max = sb("neg_max", [P, 2])
    full_sum = sb("full_sum", [P, 2])
    kept_sum = sb("kept_sum", [P, 2])
    denom = sb("denom", [P, 2])
    inv_denom = sb("inv_denom", [P, 2])
    o_pair = sb("o_pair", [P, TT, P])
    o_proj = sb("o_proj", [P, TT, DM])
    oT = o_proj[:].rearrange("p t c -> p (t c)")[:, 0:TT * P]
    mask_u8 = scores[0:RUNS, 1, 0:RUN // 4].bitcast(U8)
    mask_bias = sb("mask_bias", [RUNS, RUN], BF16)
    pick = sb("pick", [RUNS, RUNS], BF16)
    counts = sb("counts", [RUNS, RUN])
    missing = sb("missing", [RUNS, 1])
    missing_all = sb("missing_all", [RUNS, 1])
    missing_int = sb("missing_int", [RUNS, 2], I32)
    stats = sb("stats", [P, B * TT, 6])
    mean_var = sb("mean_var", [P, B * TT, 2])
    std = sb("std", [P, B * TT])
    rstd = sb("rstd", [P, B * TT])
    xn = probs[:, 1, 0:B * TT * DM].rearrange("p (i c) -> p i c", c=DM)
    eps_col = sb("eps_col", [P, 1])

    ring = [psum(f"ring{i}", [P, CH]) for i in range(3)]
    o_acc = [psum(f"o_acc{i}", [P, 512]) for i in range(2)]

    x_in = sem("x_in")
    mask_in = sem("mask_in")
    weights_in = [sem("weights_in0"), sem("weights_in1")]
    wo_in = [sem("wo_in0"), sem("wo_in1")]
    ctx_in = [sem(f"ctx_in{n}") for n in range(NC)]
    ident_step = sem("ident_step")
    pick_ready = sem("pick_ready")
    bias_ready = sem("bias_ready")
    missing_counted, missing_step, missing_ready = sem("missing_counted"), sem("missing_step"), sem("missing_ready")
    ln_step = sem("ln_step")
    std_ready = sem("std_ready")
    xn_ready = sem("xn_ready")
    ring_full = sem("ring_full")
    ring_free = sem("ring_free")
    max_ready = sem("max_ready")
    exp_done = sem("exp_done")
    masked = sem("masked")
    denom_ready = sem("denom_ready")
    norm_ready = sem("norm_ready")
    pv_done = sem("pv_done")
    o_read = sem("o_read")
    x_added = sem("x_added")
    suspect_sent = sem("suspect_sent")
    keys_high, keys_low, q_high_done, q_split = sem("keys_high"), sem("keys_low"), sem("q_high_done"), sem("q_split")
    suspect_step = sem("suspect_step")
    suspect_ready = sem("suspect_ready")
    topk_step = sem("topk_step")

    block = ctx.enter_context(nc.Block())
    LOOPS = PAIRS // 2

    @block.sync
    def _(sp):
        def load_weights(g, parity, p):
            sp.dma_start(weights[:, parity, :], w_pack[p]).then_inc(weights_in[parity], 16)

        def load_wo(g, parity, p):
            sp.dma_start(wo_sb[:, parity, :], w_out[p]).then_inc(wo_in[parity], 16)

        def load_ctx(b, n):
            sp.dma_start(ctx_sb[:, :, n * CH:(n + 1) * CH],
                         ctx_t[b, :, :, n * CH:(n + 1) * CH].rearrange("c p s -> p c s")).then_inc(ctx_in[n], 16)

        sp.dma_start(x_sb[:], x.rearrange("b (t p) c -> p (b t) c", p=P)).then_inc(x_in, 16)
        sp.dma_start(mask_u8, mask.rearrange("b (n k) -> (b n) k", k=RUN)).then_inc(mask_in, 16)
        load_weights(0, 0, 0)
        for n in range(NC):
            load_ctx(0, n)
        load_weights(1, 1, 1)
        load_wo(0, 0, 0)

        for k in range(PAIRS):
            if k % NB == NB - 1 and k + 1 < PAIRS:
                for n in range(NC):
                    sp.wait_ge(ring_full, use_index(k, ("V", n, 0)) + 1)
                    load_ctx((k + 1) // NB, n)
            if k + 2 < PAIRS:
                sp.wait_ge(ring_full, use_index(k, ("V", NC - 1, 0)) + 1)
                load_weights(k + 2, k % 2, (k + 2) % NB)
            if k + 1 < PAIRS:
                sp.wait_ge(ring_full, use_index(k, ORDER[-1]) + 1)
                load_wo(k + 1, (k + 1) % 2, (k + 1) % NB)

    @block.gpsimd
    def _(pool):
        pool.memset(ident[:], 0.0).then_inc(ident_step, 1)
        pool.memset(pick[:], 0.0).then_inc(ident_step, 1)
        pool.wait_ge(ident_step, 2)
        pool.affine_select(out=ident[:], in_=ident[:], compare_op=ALU.not_equal, fill=1.0, base=0,
                           pattern=[[-1, P]], channel_multiplier=1).then_inc(ident_step, 1)
        pool.affine_select(out=pick[:], in_=pick[:], compare_op=ALU.not_equal, fill=1.0, base=0,
                           pattern=[[-1, RUNS]], channel_multiplier=1).then_inc(pick_ready, 1)
        pool.wait_ge(mask_in, 16)
        pool.tensor_scalar(mask_bias[:], mask_u8, -1.0, -MASKED, ALU.add, ALU.mult).then_inc(bias_ready, 1)
        pool.wait_ge(missing_counted, 1)
        pool.partition_all_reduce(missing_all[:], missing[:], RUNS, RMAX).then_inc(missing_step, 1)
        pool.wait_ge(missing_step, 1)
        pool.tensor_copy(missing_int[:, 0:1], missing_all[:]).then_inc(missing_ready, 1)

        def reduce_suspect(t):
            pool.wait_ge(suspect_sent, t + 1)
            pool.tensor_tensor(suspect_twice[:], suspect[:], suspect[:], ALU.add).then_inc(suspect_step, 1)
            pool.wait_ge(suspect_step, 1)
            pool.partition_all_reduce(suspect_all[:], suspect_twice[:], P, RMAX).then_inc(suspect_step, 1)
            pool.wait_ge(suspect_step, 2)
            pool.tensor_copy(suspect_int[:, 0:1], suspect_all[:]).then_inc(suspect_step, 1)
            pool.wait_ge(suspect_step, 3)
            pool.sem_clear(suspect_step)
            pool.sem_inc(suspect_ready, 1)

        def add_output(g, row):
            pool.wait_ge(ring_free, use_index(g + 1, ("OP", 0, 0)) + 1)
            pool.tensor_tensor(row, row, o_proj[:], ALU.add).then_inc(x_added, 1)

        def x_rows(g):
            if isinstance(g, int):
                b = g // NB
                return x_sb[:, b * TT:(b + 1) * TT, :]
            return x_sb[:, bass.ds((g // NB) * TT, TT), :]

        def split_keys(g, head, index):
            rows = slice(head * D, (head + 1) * D)
            if head == 1 and isinstance(g, int) and g == 0:
                pool.wait_ge(keys_high, 4)
            for c in range(NC):
                pool.wait_ge(ring_free, index(c) + 1)
                pool.tensor_tensor(pool_waited[rows, c:c + 1], ident[rows, 0:1], ident[rows, 0:1], ALU.add)
                pool.tensor_scalar(keys_split[rows, head, c * CH:(c + 1) * CH], keys[rows, c * CH:(c + 1) * CH],
                                   1.0, 1.0, ALU.mult, ALU.mult).then_inc(keys_high, 1)
            if head == 1:
                pool.wait_ge(keys_high, 8 * g + 8)

        def split_q(g, parity, index):
            pool.wait_ge(ring_free, index + 1)
            pool.tensor_tensor(pool_waited[:, NC:NC + 1], ident[:, 0:1], ident[:, 0:1], ALU.add)
            pool.tensor_scalar(q_high[:, parity], q_both[:], 1.0, 1.0, ALU.mult, ALU.mult).then_inc(q_high_done, 1)
            pool.wait_ge(q_high_done, g + 1)
            pool.tensor_tensor(q_low[:, parity], q_both[:], q_high[:, parity].bitcast(F32), ALU.subtract)\
                .then_inc(q_split, 1)

        def pair(g, parity):
            first, last = (isinstance(g, int) and g == k for k in (0, PAIRS - 1))
            if not first:
                reduce_suspect(4 * g - 1)
                split_keys(g, 1, lambda c: use_index(g - 1, ("S", 3, NC - 1)))
            for j in range(3):
                reduce_suspect(4 * g + j)
            if not last:
                split_q(g + 1, 1 - parity, use_index(g, ("QO", 0, 0)))
                split_keys(g + 1, 0, lambda c: use_index(g, ("K", c, 0)))
            if not first:
                add_output(g - 1, x_rows(g - 1))

        split_q(0, 0, use_index(-1, ("Q", 0, 0)))
        for head in range(2):
            split_keys(0, head, lambda c: use_index(-1, ("K", c, 0)))
        pair(0, 0)
        pair(1, 1)
        with pool.Fori(1, PAIRS // 2 - 1) as i:
            pair(2 * i, 0)
            pair(2 * i + 1, 1)
        pair(PAIRS - 2, 0)
        pair(PAIRS - 1, 1)
        reduce_suspect(4 * PAIRS - 1)
        add_output(PAIRS - 1, x_rows(PAIRS - 1))

    @block.vector
    def _(dve):
        steps = [0]

        def then(ins):
            steps[0] += 1
            ins.then_inc(ln_step, 1)
            dve.wait_ge(ln_step, steps[0])

        dve.memset(eps_col[:], EPS)
        dve.wait_ge(mask_in, 16)
        dve.tensor_scalar(counts[:], mask_u8, 0.5, None, ALU.is_lt, ALU.add, accum_out=missing[:])\
            .then_inc(missing_counted, 1)
        dve.wait_ge(x_in, 16)
        for i in range(B * TT):
            last = dve.bn_stats(stats[:, i, :], x_sb[:, i, :])
        then(last)
        for i in range(B * TT):
            last = dve.bn_aggr(mean_var[:, i, :], stats[:, i, :])
        then(last)
        dve.wait_ge(std_ready, 1)
        then(dve.reciprocal(rstd[:], std[:]))
        for i in range(B * TT):
            last = dve.tensor_scalar(xn[:, i, :], x_sb[:, i, :], mean_var[:, i, 0:1], rstd[:, i:i + 1],
                                     ALU.subtract, ALU.mult)
        last.then_inc(xn_ready, 1)

        PER_TILE = 8

        def group_tops(g, j, c):
            if c == 0 and not (isinstance(g, int) and g == 0 and j == 0):
                dve.wait_ge(suspect_sent, 4 * g + j)
            dve.wait_ge(ring_free, use_index(g, ("S", j, c)) + 1)
            dve.memset(waited[:, c:c + 1], 0.0)
            for k in range(c * (CH // GRP), (c + 1) * (CH // GRP)):
                last = dve.max(cand[:, 8 * k:8 * k + 8], scores[:, j % 2, k * GRP:(k + 1) * GRP])
            return last

        def largest(g, j, last):
            q = j % 2
            n = [0]

            def link(ins):
                n[0] += 1
                ins.then_inc(topk_step, 1)
                dve.wait_ge(topk_step, n[0])

            link(last)
            link(dve.max(top[:, q, 0:8], cand[:]))
            dve.tensor_scalar(neg_max[:, q:q + 1], top[:, q, 0:1], -float(D) ** -0.5, None,
                              ALU.mult).then_inc(max_ready, 1)
            for r in range(1, TOPK // 8):
                link(dve.match_replace(cand_left[:], top[:, q, 8 * r - 8:8 * r], cand[:] if r == 1 else cand_left[:],
                                       LOWEST))
                link(dve.max(top[:, q, 8 * r:8 * r + 8], cand_left[:]))
            assert n[0] == PER_TILE
            dve.tensor_scalar(over[:], cand[:, 7:8 * NG:8], top[:, q, TOPK - 1:TOPK], None, ALU.is_gt, ALU.add,
                              accum_out=suspect[:]).then_inc(suspect_sent, 1)

        def keep(t, q):
            dve.wait_ge(exp_done, t + 1)
            dve.scalar_tensor_tensor(out=probs[:, q, :], in0=scores[:, q, :], scalar=top[:, q, TOPK - 1:TOPK],
                                     in1=probs[:, q, :], op0=ALU.is_ge, op1=ALU.mult,
                                     accum_out=kept_sum[:, q:q + 1]).then_inc(masked, 1)
            dve.wait_ge(masked, t + 1)
            dve.scalar_tensor_tensor(out=denom[:, q:q + 1], in0=full_sum[:, q:q + 1], scalar=1e-8,
                                     in1=kept_sum[:, q:q + 1], op0=ALU.mult, op1=ALU.add).then_inc(denom_ready, 1)
            dve.wait_ge(denom_ready, t + 1)
            dve.reciprocal(inv_denom[:, q:q + 1], denom[:, q:q + 1]).then_inc(norm_ready, 1)

        def settle(t, q):
            dve.wait_ge(suspect_ready, t + 1)
            dve.memset(waited[:, NC:NC + 1], 0.0).then_inc(topk_step, 1)
            dve.wait_ge(topk_step, PER_TILE + 1)
            flag = dve.value_load(suspect_int[0:1, 0:1], min_val=0, max_val=2 * NG)
            dve.sem_clear(topk_step)
            with dve.If(flag):
                for c in range(S // SLOW):
                    for r in range(TOPK // 8):
                        src = scores[:, q, c * SLOW:(c + 1) * SLOW] if r == 0 else cand_left[:]
                        at = c * TOPK + 8 * r
                        dve.max(slow_cand[:, at:at + 8], src)
                        dve.drain()
                        if r < TOPK // 8 - 1:
                            dve.match_replace(cand_left[:], slow_cand[:, at:at + 8], src, LOWEST)
                            dve.drain()
                for r in range(TOPK // 8):
                    dve.max(top[:, q, 8 * r:8 * r + 8], slow_cand[:])
                    dve.drain()
                    if r < TOPK // 8 - 1:
                        dve.match_replace(slow_cand[:], top[:, q, 8 * r:8 * r + 8], slow_cand[:], LOWEST)
                        dve.drain()

        def low_keys(g, head):
            rows = slice(head * D, (head + 1) * D)
            other = slice((1 - head) * D, (2 - head) * D)
            for c in range(NC):
                part = slice(c * CH, (c + 1) * CH)
                dve.wait_ge(keys_high, 8 * g + 4 * head + c + 1)
                dve.tensor_tensor(keys_split[other, head, part], keys[rows, part],
                                  keys_split[rows, head, part].bitcast(F32), ALU.subtract).then_inc(keys_low, 1)

        def pair(g):
            first, last = (isinstance(g, int) and g == k for k in (0, PAIRS - 1))
            for j in range(4):
                t = 4 * g + j
                group_tops(g, j, 0)
                if not (first and j == 0):
                    settle(t - 1, (j - 1) % 2)
                group_tops(g, j, 1)
                if j == 0 and not first:
                    low_keys(g, 1)
                if not (first and j == 0):
                    keep(t - 1, (j - 1) % 2)
                group_tops(g, j, 2)
                if j == 3 and not last:
                    low_keys(g + 1, 0)
                largest(g, j, group_tops(g, j, 3))

        low_keys(0, 0)
        low_keys(0, 1)
        pair(0)
        with dve.Fori(1, PAIRS - 1) as g:
            pair(g)
        pair(PAIRS - 1)
        settle(4 * PAIRS - 1, 1)
        keep(4 * PAIRS - 1, 1)

    @block.scalar
    def _(act):
        act.wait_ge(ln_step, 2)
        act.activation(std[:], mean_var[:, :, 1], ACT.Sqrt, bias=eps_col[:]).then_inc(std_ready, 1)

        def copy(dst, src):
            return act.activation(dst, src, ACT.Copy)

        def take_q(parity, slot):
            for head in range(2):
                ins = act.activation(q_both[:, head, :], ring[slot][:, head * T:(head + 1) * T], ACT.Copy,
                                     scale=weights[:, parity, WT + head:WT + head + 1])
            return ins

        def take_kv(kind, n, slot):
            if kind == "K":
                return copy(keys[:, n * CH:(n + 1) * CH], ring[slot][:])
            return copy(v_sb[:, n * (CH // P):(n + 1) * (CH // P), :],
                        ring[slot][:].rearrange("p (a c) -> p a c", c=P))

        for use in PROLOGUE:
            kind, n, _ = use
            slot = use_slot(-1, use)
            act.wait_ge(ring_full, use_index(-1, use) + 1)
            if kind == "X":
                ins = copy(xnT[:, n, :], ring[slot][:])
            elif kind == "Q":
                ins = take_q(0, slot)
            else:
                ins = take_kv(kind, n, slot)
            ins.then_inc(ring_free, 1)

        def exponentials(t, q):
            act.wait_ge(max_ready, t + 1)
            act.activation(probs[:, q, :], scores[:, q, :], ACT.Exp, bias=neg_max[:, q:q + 1], scale=float(D) ** -0.5,
                           accum_out=full_sum[:, q:q + 1]).then_inc(exp_done, 1)

        def take_output(t, j):
            head, half = j // 2, j % 2
            act.wait_ge(pv_done, 4 * t + 4)
            act.wait_ge(norm_ready, t + 1)
            act.activation(o_pair[:, half, head * D:(head + 1) * D], o_acc[j % 2][:, 0:D], ACT.Copy,
                           scale=inv_denom[:, j % 2:j % 2 + 1]).then_inc(o_read, 1)

        def pair(g, parity):
            first, last, left = (isinstance(g, int) and g == k for k in (0, PAIRS - 1, PAIRS))
            for use in (uses_of(g) if isinstance(g, int) else ORDER):
                kind, j, c = use
                t = 4 * g + j
                slot = use_slot(g, use)
                if left and kind == "QO":
                    take_output(4 * PAIRS - 1, 3)
                act.wait_ge(ring_full, use_index(g, use) + 1)
                if kind == "S":
                    if not (first and j < 2):
                        act.wait_ge(masked, t - 1)
                    copy(scores[:, j % 2, c * CH:(c + 1) * CH], ring[slot][:]).then_inc(ring_free, 1)
                elif kind == "T":
                    if not (first and j == 2 and c < 2):
                        act.wait_ge(pv_done, 4 * (t - 2) + (c - 1))
                    copy(probsT[:, c % 2, :], ring[slot][:]).then_inc(ring_free, 1)
                elif kind in "KV":
                    if kind == "K" and j == 0:
                        act.wait_ge(keys_low, 8 * g + 8)
                    take_kv(kind, j, slot).then_inc(ring_free, 1)
                elif kind == "QO":
                    if not first:
                        if not (isinstance(g, int) and g == 1):
                            act.wait_ge(x_added, g - 1)
                        ins = copy(oT, ring[slot][:, 512:512 + TT * P])
                    if not (last or left):
                        act.wait_ge(q_split, g + 1)
                        ins = take_q(1 - parity, slot)
                    ins.then_inc(ring_free, 1)
                elif kind == "OP":
                    copy(o_proj[:].rearrange("p t c -> p (t c)"), ring[slot][:, 0:TT * DM]).then_inc(ring_free, 1)
                if c == 1 and (kind == "T" or (kind == "S" and first and j < 2)):
                    if not (first and j < 3):
                        take_output(t - 3, (j - 3) % 4)
                    if not (first and j == 0) and not (left and j == 1):
                        exponentials(t - 1, (j - 1) % 2)

        pair(0, 0)
        pair(1, 1)
        with act.Fori(1, PAIRS // 2 - 1) as i:
            pair(2 * i, 0)
            pair(2 * i + 1, 1)
        pair(PAIRS - 2, 0)
        pair(PAIRS - 1, 1)
        pair(PAIRS, 0)

    @block.tensor
    def _(pe):
        def begin(index):
            if not (isinstance(index, int) and index < 3):
                pe.wait_ge(ring_free, index - 2)

        def turn_x(c, slot):
            for i in range(B * TT):
                last = pe.transpose(ring[slot][:, i * P:(i + 1) * P], xn[:, i, c * P:(c + 1) * P], ident[:])
            return last

        def project_q(g, parity, slot):
            if isinstance(g, int):
                at = g // NB * T
            else:
                at = (g // NB) * T
            for head in range(2):
                for c in range(2):
                    w = WQ + (2 * c + head) * P
                    last = pe.matmul(ring[slot][:, head * T:(head + 1) * T], weights[:, parity, w:w + P],
                                     xnT[:, c, bass.ds(at, T)], start=(c == 0), stop=(c == 1))
            return last

        def project_k(parity, n, slot):
            for u in range(CH // 512):
                for c in range(2):
                    at = n * CH + u * 512
                    w = WK + c * P
                    last = pe.matmul(ring[slot][:, u * 512:(u + 1) * 512], weights[:, parity, w:w + P],
                                     ctx_sb[:, c, at:at + 512], start=(c == 0), stop=(c == 1))
            return last

        def project_v(parity, n, slot):
            for i in range(CH // P):
                for c in range(2):
                    at = n * CH + i * P
                    w = WV + c * P
                    last = pe.matmul(ring[slot][:, i * P:(i + 1) * P], ctx_sb[:, c, at:at + P],
                                     weights[:, parity, w:w + P], start=(c == 0), stop=(c == 1))
            return last

        def need_context(g, n):
            pe.wait_ge(ctx_in[n], (g // NB) * 16 + 16)

        pe.wait_ge(ident_step, 3)
        pe.wait_ge(xn_ready, 1)
        for use in PROLOGUE:
            kind, n, _ = use
            slot = use_slot(-1, use)
            begin(use_index(-1, use))
            if kind == "X":
                ins = turn_x(n, slot)
            elif kind == "Q":
                pe.wait_ge(weights_in[0], 16)
                pe.wait_ge(ring_free, 2)
                ins = project_q(0, 0, slot)
            elif kind == "K":
                need_context(0, n)
                ins = project_k(0, n, slot)
            ins.then_inc(ring_full, 1)
        pe.wait_ge(pick_ready, 1)
        pe.wait_ge(bias_ready, 1)

        def multiply_values(tile, j, c, index):
            pe.wait_ge(ring_free, index + 1)
            head = j // 2
            for i in range(CH // P):
                last = pe.matmul(o_acc[j % 2][:, 0:D], probsT[:, c % 2, i * P:(i + 1) * P],
                                 v_sb[:, c * (CH // P) + i, head * D:(head + 1) * D],
                                 start=(c == 0 and i == 0), stop=(c == NC - 1 and i == CH // P - 1))
            last.then_inc(pv_done, 1)

        def pair(g, i, parity, with_mask):
            first, last, left = (isinstance(g, int) and g == k for k in (0, PAIRS - 1, PAIRS))

            def last_chunk(j):
                where = (g, ("T", j - 1, NC - 1)) if j else ((g - 1), ("T", 3, NC - 1))
                multiply_values(4 * g + j - 3, (j - 3) % 4, NC - 1, use_index(*where))

            for use in (uses_of(g) if isinstance(g, int) else ORDER):
                kind, j, c = use
                slot = use_slot(g, use)
                index = use_index(g, use)
                if left and kind == "T" and c == 0:
                    last_chunk(j)
                if left and kind == "QO":
                    last_chunk(2)
                begin(index)
                if kind == "S":
                    head, half = j // 2, j % 2
                    b = g // NB
                    if half == 0:
                        pe.wait_ge(keys_low, 8 * g + 4 * head + c + 1)
                    if j == 0 and c == 0:
                        pe.wait_ge(q_split, g + 1)
                    for u in range(CH // 512):
                        o = ring[slot][:, u * 512:(u + 1) * 512]
                        at = c * CH + u * 512
                        pe.matmul(o, q_high[:, parity, head, half * P:(half + 1) * P],
                                  keys_split[:, head, at:at + 512], start=True, stop=False)
                        ins = pe.matmul(o, q_low[:, parity, head, half * P:(half + 1) * P],
                                        keys_split[:, head, at:at + 512], start=False, stop=not with_mask)
                        if with_mask:
                            run = b * (S // RUN) + at // RUN
                            column = pick[:, run:run + 1] if isinstance(g, int) else pick[:, bass.ds(run, 1)]
                            ins = pe.matmul(o, column.broadcast_to((RUNS, P)), mask_bias[:], start=False, stop=True)
                    ins.then_inc(ring_full, 1)
                    if c == 0 and not (first and j < 3):
                        last_chunk(j)
                elif kind == "T":
                    tile, jj = 4 * g + j - 2, (j - 2) % 4
                    if c == 0:
                        pe.wait_ge(masked, tile + 1)
                    for k in range(CH // P):
                        at = c * CH + k * P
                        ins = pe.transpose(ring[slot][:, k * P:(k + 1) * P], probs[:, jj % 2, at:at + P], ident[:])
                    ins.then_inc(ring_full, 1)
                    if c == 1 and not (first and j < 4):
                        pe.wait_ge(o_read, tile - 1)
                    if c >= 1:
                        multiply_values(tile, jj, c - 1, use_index(g, ("T", j, c - 1)))
                elif kind in "KV":
                    if kind == "K":
                        need_context(g + 1, j)
                        project_k(1 - parity, j, slot).then_inc(ring_full, 1)
                    else:
                        project_v(parity, j, slot).then_inc(ring_full, 1)
                elif kind == "QO":
                    if not first:
                        pe.wait_ge(o_read, 4 * g)
                        for half in range(TT):
                            ins = pe.transpose(ring[slot][:, 512 + half * P:512 + (half + 1) * P], o_pair[:, half, :],
                                               ident[:])
                    if not (last or left):
                        pe.wait_ge(weights_in[1 - parity], (i + 1 + parity) * 16)
                        ins = project_q(g + 1, 1 - parity, slot)
                    ins.then_inc(ring_full, 1)
                elif kind == "OP":
                    pe.wait_ge(ring_free, use_index(g, ("QO", 0, 0)) + 1)
                    pe.wait_ge(wo_in[1 - parity], (i + parity) * 16)
                    for half in range(TT):
                        ins = pe.matmul(ring[slot][:, half * DM:(half + 1) * DM], oT[:, half * P:(half + 1) * P],
                                        wo_sb[:, 1 - parity, :], start=True, stop=True)
                    ins.then_inc(ring_full, 1)

        def all_pairs(with_mask):
            pair(0, 0, 0, with_mask)
            pair(1, 0, 1, with_mask)
            with pe.Fori(1, PAIRS // 2 - 1) as i:
                pair(2 * i, i, 0, with_mask)
                pair(2 * i + 1, i, 1, with_mask)
            pair(PAIRS - 2, PAIRS // 2 - 1, 0, with_mask)
            pair(PAIRS - 1, PAIRS // 2 - 1, 1, with_mask)
            pair(PAIRS, PAIRS // 2, 0, with_mask)

        pe.wait_ge(missing_ready, 1)
        flag = pe.value_load(missing_int[0:1, 0:1], min_val=0, max_val=RUN)
        with pe.If(flag):
            all_pairs(True)
        with pe.Else():
            all_pairs(False)


I = 704
IT = -(-I // P)
FH, FD = 16, 16
FPAD = 32
QC = FH * FPAD // P
HG = 4
UNITS = TT * (FH // HG)
BLK = 16
PHASE = 0.1 * math.sin(2.0 * math.pi * 0.25)
OUT_EPS = 0.1 * math.sin(2.0 * math.pi * 0.5)
ROUND_HALF = 1.5 * 2.0 ** 22
ROUND_ONE = 1.5 * 2.0 ** 23
ROUND_TWO = 1.5 * 2.0 ** 24
TWO_PI_A = 6.28125
TWO_PI_B = float(np.float32(2.0 * math.pi - 6.28125))
TWO_PI_C = 2.0 * math.pi - 6.28125 - TWO_PI_B
PI_BELOW = 3.1415925


def head_of(u, h):
    return h * (FH // HG) + u % (FH // HG)


def self_attention_and_ffn(nc, ctx, x_sb, ident, out, sa_wq, sa_wk, sa_wv, sa_wo, sa_cols, sa_rows, rby, freqs, positions,
                           w_gate, w_up, w_down):
    def sb(name, shape, dt=F32):
        return ctx.enter_context(nc.sbuf_tensor(name, shape, dt))

    def psum(name, shape, dt=F32):
        return ctx.enter_context(nc.psum_tensor(name, shape, dt))

    def sem(name):
        return ctx.enter_context(nc.semaphore(name))

    wq_sb = sb("wq_sb", [P, 2, QC * P])
    wk_sb = sb("wk_sb", [P, 2, QC * P])
    wv_sb = sb("wv_sb", [P, 2, DM])
    wo2_sb = sb("wo2_sb", [P, 2, DM])
    cols = sb("cols", [P, 2, QC])
    rows = sb("rows", [P, 4, DM])
    rby_sb = sb("rby_sb", [P, 3])
    freqs_sb = sb("freqs_sb", [P, DM // 2])
    pos_sb = sb("pos_sb", [P, TT])
    logit_scale = sb("logit_scale", [P, 1])
    out_scale = sb("out_scale", [P, 1])
    eps2 = sb("eps2", [P, 1])
    eps1 = sb("eps1", [P, 1])
    gamma_scale = sb("gamma_scale", [P, 1])
    small = sb("small", [P, 1])
    angle = sb("angle", [P, TT, DM // 2])
    turns = sb("turns", [P, TT, DM // 2])
    reduced = sb("reduced", [P, 2, TT, DM // 2])
    encoding = sb("encoding", [P, TT, DM])
    gate_in = sb("gate_in", [P, IT * DM])
    up_in = sb("up_in", [P, IT * DM])
    down_in = sb("down_in", [P, TT * I])
    gateT = sb("gateT", [P, 2, IT * P])
    upT = sb("upT", [P, 2, IT * P])
    downT = sb("downT", [P, IT, DM])
    WIDE = IT * DM
    qa = sb("qa", [P, WIDE])
    qb = sb("qb", [P, WIDE])
    qn = sb("qn", [P, WIDE])
    scale = sb("scale", [P, WIDE // BLK])
    inv_scale = sb("inv_scale", [P, WIDE // BLK])
    stats2 = sb("stats2", [P, TT, 6])
    mv2 = sb("mv2", [P, TT, 2])
    std2 = sb("std2", [P, TT])
    rstd2 = sb("rstd2", [P, TT])
    xq = sb("xq", [P, TT, DM])
    turned = sb("turned", [P, 2, T])
    q_sb = sb("q_sb", [P, QC, T])
    k_sb = sb("k_sb", [P, QC, T])
    v2_sb = sb("v2_sb", [P, TT, DM])
    neg_top = sb("neg_top", [P, 2, HG])
    e_sb = sb("e_sb", [P, 2, HG, T])
    sums = sb("sums", [P, TT, FH])
    inv_sums = sb("inv_sums", [P, TT, FH])
    eT_sb = sb("eT_sb", [P, 2, HG * TT * P])
    o_sb = sb("o_sb", [P, TT, DM])
    y_sb = sb("y_sb", [P, TT, DM])
    xf = sb("xf", [P, TT, DM])
    xfq = sb("xfq", [P, TT, DM])
    silu_sb = sb("silu_sb", [P, I])
    h_sb = sb("h_sb", [P, I])
    hq_sb = sb("hq_sb", [P, I])
    hT_sb = sb("hT_sb", [P, IT * P])
    x_out = sb("x_out", [P, TT, DM])

    logits = [psum(f"logits{i}", [P, HG * T]) for i in range(2)]
    eT_ps = psum("eT_ps", [P, HG * TT * P])
    o_ps = psum("o_ps", [P, 512])
    turn_ps = psum("turn_ps", [P, 512])

    consts_in = sem("consts_in")
    ffn_in = sem("ffn_in")
    prep_step = sem("prep_step")
    reduced_ready = sem("reduced_ready")
    encoding_ready = sem("encoding_ready")
    w_quant = sem("w_quant")
    w_turned = sem("w_turned")
    w_taken = sem("w_taken")
    dve_step = sem("dve_step")
    var_ready = sem("var_ready")
    std_done = sem("std_done")
    rows_ready = sem("rows_ready")
    turned_full = sem("turned_full")
    turned_taken = sem("turned_taken")
    q_full, k_full, v_full = sem("q_full"), sem("k_full"), sem("v_full")
    q_taken, k_taken, v_taken = sem("q_taken"), sem("k_taken"), sem("v_taken")
    logits_full, top_ready, exp_ready = sem("logits_full"), sem("top_ready"), sem("exp_ready")
    eT_full, eT_taken, av_done = sem("eT_full"), sem("eT_taken"), sem("av_done")
    proj_full = sem("proj_full")
    gate_full, up_full, silu_ready = sem("gate_full"), sem("up_full"), sem("silu_ready")
    hq_ready, hT_full, hT_taken = sem("hq_ready"), sem("hT_full"), sem("hT_taken")
    down_full, row_done, out_done = sem("down_full"), sem("row_done"), [sem(f"out_done{i}") for i in range(TT)]

    block = ctx.enter_context(nc.Block())
    HALVES = [(0, 512), (512, I - 512)]

    def weight_turned(dst, n):
        if dst == 2:
            return downT[:, 2 * n:2 * n + 2, :].rearrange("p a c -> p (a c)")
        return (gateT, upT)[dst][:, n, :]

    WEIGHT_TURNS = [(0, 0), (0, 1), (1, 0), (1, 1), (2, 0), (2, 1), (2, 2)]


    @block.sync
    def _(sp):
        for dst, src in ((wq_sb, sa_wq), (wk_sb, sa_wk), (wv_sb, sa_wv), (wo2_sb, sa_wo), (cols, sa_cols),
                         (rows, sa_rows), (rby_sb, rby), (freqs_sb, freqs), (pos_sb, positions)):
            sp.dma_start(dst[:], src).then_inc(consts_in, 16)
        for dst, src in ((gate_in, w_gate), (up_in, w_up), (down_in, w_down)):
            sp.dma_start(dst[:], src).then_inc(ffn_in, 16)
        out_rows = out.rearrange("b (t p) c -> b p t c", p=P)
        with sp.Fori(0, B) as b:
            for half in range(TT):
                sp.wait_ge(row_done, b * TT + half + 1)
                sp.dma_start(out_rows[b, :, half, :], x_out[:, half, :]).then_inc(out_done[half], 16)
        for half in range(TT):
            sp.wait_ge(out_done[half], 16 * B)

    @block.vector
    def _(dve):
        class Chain:
            def __init__(self, sem):
                self.sem, self.n = sem, 0

            def __call__(self, ins):
                self.n += 1
                ins.then_inc(self.sem, 1)
                dve.wait_ge(self.sem, self.n)

            def restart(self):
                self.n += 1
                dve.memset(small[:], 0.0).then_inc(self.sem, 1)
                dve.wait_ge(self.sem, self.n)
                dve.sem_clear(self.sem)

        def quantise(link, dst, src, n):
            k = n // BLK
            blocks = src.rearrange("p (k e) -> p k e", e=BLK)

            def blocked(t):
                return t[:, 0:n].rearrange("p (k e) -> p k e", e=BLK)

            def spread(t):
                return t[:, 0:k].unsqueeze(2).broadcast_to((P, k, BLK))

            link(dve.tensor_reduce(scale[:, 0:k], blocks, AX.X, ALU.max, apply_absolute_value=True))
            link(dve.tensor_scalar(scale[:, 0:k], scale[:, 0:k], 1.0 / 6.0, 1e-12, ALU.mult, ALU.max))
            link(dve.reciprocal(inv_scale[:, 0:k], scale[:, 0:k]))
            link(dve.tensor_scalar(inv_scale[:, 0:k], inv_scale[:, 0:k], 1.0 - 2.0 ** -24, None, ALU.mult))
            link(dve.tensor_tensor(blocked(qn), blocks, spread(inv_scale), ALU.mult))
            link(dve.tensor_scalar(qn[:, 0:n].bitcast(U32), qn[:, 0:n].bitcast(U32), 0x7FFFFFFF, None,
                                   ALU.bitwise_and))
            link(dve.tensor_scalar(qa[:, 0:n], qn[:, 0:n], 2.0, ROUND_HALF, ALU.min, ALU.add))
            link(dve.tensor_scalar(qb[:, 0:n], qn[:, 0:n], 4.0, 2.0, ALU.min, ALU.max))
            link(dve.tensor_scalar(qb[:, 0:n], qb[:, 0:n], ROUND_ONE, ROUND_ONE + 2.0, ALU.add, ALU.subtract))
            link(dve.scalar_tensor_tensor(out=qa[:, 0:n], in0=qa[:, 0:n], scalar=ROUND_HALF, in1=qb[:, 0:n],
                                          op0=ALU.subtract, op1=ALU.add))
            link(dve.tensor_scalar(qn[:, 0:n], qn[:, 0:n], 4.0, ROUND_TWO, ALU.max, ALU.add))
            link(dve.scalar_tensor_tensor(out=qa[:, 0:n], in0=qn[:, 0:n], scalar=ROUND_TWO + 4.0, in1=qa[:, 0:n],
                                          op0=ALU.subtract, op1=ALU.add))
            link(dve.tensor_tensor(blocked(qa), blocked(qa), spread(scale), ALU.mult))
            return dve.scalar_tensor_tensor(out=dst.bitcast(U32), in0=src.bitcast(U32), scalar=0x80000000,
                                            in1=qa[:, 0:n].bitcast(U32), op0=ALU.bitwise_and, op1=ALU.bitwise_or)

        link = Chain(prep_step)
        dve.memset(eps1[:], EPS)
        dve.wait_ge(consts_in, 16 * 9)
        red, blue, yellow = (rby_sb[:, i:i + 1] for i in range(3))
        MUL, ADD = ALU.mult, ALU.add

        def weighted(dst, base, *terms):
            link(dve.memset(dst, base))
            for col, w in terms:
                link(dve.scalar_tensor_tensor(out=dst, in0=col, scalar=w, in1=dst, op0=MUL, op1=ADD))

        weighted(logit_scale[:], 1.0, (red, 0.1), (blue, 0.05), (yellow, 0.15))
        link(dve.tensor_scalar(logit_scale[:], logit_scale[:], FD ** -0.5, None, MUL))
        weighted(out_scale[:], 1.0, (yellow, OUT_EPS))
        weighted(gamma_scale[:], 1.0, (red, 0.1), (yellow, 0.05))
        weighted(eps2[:], 1.0, (blue, 0.1))
        link(dve.tensor_scalar(eps2[:], eps2[:], EPS, None, MUL))
        link(dve.tensor_scalar(rows[:, 2, :], rows[:, 2, :], gamma_scale[:], None, MUL))
        weighted(small[:], 1.0, (yellow, PHASE))
        link(dve.tensor_scalar(freqs_sb[:], freqs_sb[:], small[:], None, MUL))
        link(dve.reciprocal(freqs_sb[:], freqs_sb[:]))
        for half in range(TT):
            link(dve.tensor_scalar(angle[:, half, :], freqs_sb[:], pos_sb[:, half:half + 1], None, MUL))
        for c in range(2):
            link(dve.tensor_scalar(turns[:], angle[:], 0.5 / math.pi, 0.25 * c, MUL, ADD))
            link(dve.tensor_scalar(turns[:], turns[:], ROUND_ONE, ROUND_ONE, ADD, ALU.subtract))
            link(dve.scalar_tensor_tensor(out=reduced[:, c], in0=turns[:], scalar=-TWO_PI_A, in1=angle[:], op0=MUL, op1=ADD))
            for part in (TWO_PI_B, TWO_PI_C):
                link(dve.scalar_tensor_tensor(out=reduced[:, c], in0=turns[:], scalar=-part, in1=reduced[:, c],
                                              op0=MUL, op1=ADD))
            if c:
                link(dve.tensor_scalar(reduced[:, c], reduced[:, c], 0.5 * math.pi, None, ADD))
            link(dve.tensor_scalar(reduced[:, c], reduced[:, c], PI_BELOW, -PI_BELOW, ALU.min, ALU.max))
        dve.sem_inc(reduced_ready, 1)
        dve.wait_ge(ffn_in, 16 * 3)
        for t, n in ((gate_in, IT * DM), (up_in, IT * DM), (down_in, TT * I)):
            link(quantise(link, t[:, 0:n], t[:, 0:n], n))
            dve.sem_inc(w_quant, 1)
        dve.wait_ge(encoding_ready, 1)

        def normalise(link, dst, src, k, eps_ready=None):
            for half in range(TT):
                ins = dve.bn_stats(stats2[:, half, :], src[:, half, :])
            link(ins)
            for half in range(TT):
                ins = dve.bn_aggr(mv2[:, half, :], stats2[:, half, :])
            ins.then_inc(var_ready, 1)
            dve.wait_ge(std_done, k + 1)
            link(dve.reciprocal(rstd2[:], std2[:]))
            for half in range(TT):
                ins = dve.tensor_scalar(dst[:, half, :], src[:, half, :], mv2[:, half, 0:1], rstd2[:, half:half + 1],
                                        ALU.subtract, MUL)
            return ins

        def batch(b):
            link = Chain(dve_step)
            x_rows = x_sb[:, bass.ds(b * TT, TT), :]
            link(normalise(link, xq, x_rows, 3 * b))
            dve.tensor_tensor(xq[:], xq[:], encoding[:], ADD).then_inc(rows_ready, 1)
            dve.wait_ge(q_full, b + 1)
            for c in range(QC):
                ins = dve.tensor_scalar(q_sb[:, c, :], logits[0][:, c * T:(c + 1) * T], cols[:, 0, c:c + 1],
                                        logit_scale[:], ADD, MUL)
            ins.then_inc(q_taken, 1)
            dve.wait_ge(v_full, b + 1)
            dve.tensor_tensor(v2_sb[:], o_ps[:].rearrange("p (t c) -> p t c", c=DM),
                              rows[:, 0, :].unsqueeze(1).broadcast_to((P, TT, DM)), ADD).then_inc(v_taken, 1)

            def take_turned(u):
                dve.wait_ge(eT_full, b * UNITS + u + 1)
                if u >= 2:
                    dve.wait_ge(av_done, b * UNITS + u - 1)
                dve.tensor_copy(eT_sb[:, u % 2, :], eT_ps[:]).then_inc(eT_taken, 1)

            for u in range(UNITS):
                dve.wait_ge(logits_full, b * UNITS + u + 1)
                if u >= 2:
                    dve.wait_ge(exp_ready, b * UNITS + u - 1)
                dve.tensor_reduce(neg_top[:, u % 2, :], logits[u % 2][:].rearrange("p (h k) -> p h k", k=T), AX.X,
                                  ALU.max, negate=True).then_inc(top_ready, 1)
                if u >= 1:
                    take_turned(u - 1)
            take_turned(UNITS - 1)
            dve.wait_ge(exp_ready, (b + 1) * UNITS)
            link(dve.reciprocal(inv_sums[:], sums[:]))
            link(dve.tensor_scalar(inv_sums[:], inv_sums[:], out_scale[:], None, MUL))
            dve.wait_ge(av_done, (b + 1) * UNITS)
            dve.tensor_tensor(o_sb[:].rearrange("p t (h d) -> p (t h) d", d=FD), o_ps[:].rearrange("p (k d) -> p k d", d=FD),
                              inv_sums[:].rearrange("p t h -> p (t h)").unsqueeze(2).broadcast_to((P, TT * FH, FD)),
                              MUL).then_inc(rows_ready, 1)
            link(dve.tensor_tensor(xq[:], xq[:], rows[:, 1, :].unsqueeze(1).broadcast_to((P, TT, DM)), ADD))
            dve.wait_ge(proj_full, b + 1)
            link(dve.tensor_tensor(y_sb[:], eT_ps[:, 0:512].rearrange("p (t c) -> p t c", c=DM), xq[:], ADD))
            link(normalise(link, y_sb, y_sb, 3 * b + 1))
            link(dve.tensor_tensor(y_sb[:], y_sb[:], rows[:, 2, :].unsqueeze(1).broadcast_to((P, TT, DM)), MUL))
            link(dve.tensor_tensor(y_sb[:], y_sb[:], rows[:, 3, :].unsqueeze(1).broadcast_to((P, TT, DM)), ADD))
            link(dve.tensor_tensor(y_sb[:], y_sb[:], x_rows, ADD))
            link(normalise(link, xf, y_sb, 3 * b + 2))
            flat = "p t c -> p (t c)"
            quantise(link, xfq[:].rearrange(flat), xf[:].rearrange(flat), TT * DM).then_inc(rows_ready, 1)
            for half in range(TT):
                n = b * TT + half + 1
                dve.wait_ge(silu_ready, n)
                dve.wait_ge(up_full, n)
                link(dve.tensor_tensor(h_sb[:], silu_sb[:], logits[1][:, 0:I], MUL))
                quantise(link, hq_sb[:], h_sb[:], I).then_inc(hq_ready, 1)
                dve.wait_ge(down_full, n)
                if not isinstance(b, int):
                    dve.wait_ge(out_done[half], 16 * b)
                dve.tensor_tensor(x_out[:, half, :], o_ps[:, 0:DM], y_sb[:, half, :], ADD).then_inc(row_done, 1)
            link.restart()

        batch(0)
        with dve.Fori(1, B) as b:
            batch(b)

    @block.scalar
    def _(act):
        act.wait_ge(reduced_ready, 1)
        act.activation(encoding[:, :, 0:DM:2], reduced[:, 0], ACT.Sin)
        act.activation(encoding[:, :, 1:DM:2], reduced[:, 1], ACT.Sin).then_inc(encoding_ready, 1)
        for k, (dst, n) in enumerate(WEIGHT_TURNS):
            act.wait_ge(w_turned, k + 1)
            act.activation(weight_turned(dst, n), logits[k % 2][:, 0:IT * P] if dst < 2 else
                           logits[k % 2][:, 0:512], ACT.Copy).then_inc(w_taken, 1)

        def std(k, eps):
            act.wait_ge(var_ready, k + 1)
            act.activation(std2[:], mv2[:, :, 1], ACT.Sqrt, bias=eps[:]).then_inc(std_done, 1)

        def take_turned(k):
            act.wait_ge(turned_full, k + 1)
            act.activation(turned[:].rearrange("p c t -> p (c t)"), turn_ps[:], ACT.Copy).then_inc(turned_taken, 1)

        with act.Fori(0, B) as b:
            std(3 * b, eps1)
            take_turned(3 * b)
            act.wait_ge(k_full, b + 1)
            for c in range(QC):
                ins = act.activation(k_sb[:, c, :], logits[1][:, c * T:(c + 1) * T], ACT.Identity, bias=cols[:, 1, c:c + 1])
            ins.then_inc(k_taken, 1)
            for u in range(UNITS):
                act.wait_ge(top_ready, b * UNITS + u + 1)
                if u >= 2:
                    act.wait_ge(eT_full, b * UNITS + u - 1)
                for h in range(HG):
                    half, head = u // (FH // HG), head_of(u, h)
                    ins = act.activation(e_sb[:, u % 2, h, :], logits[u % 2][:, h * T:(h + 1) * T], ACT.Exp,
                                         bias=neg_top[:, u % 2, h:h + 1], accum_out=sums[:, half, head:head + 1])
                ins.then_inc(exp_ready, 1)
            take_turned(3 * b + 1)
            std(3 * b + 1, eps2)
            std(3 * b + 2, eps1)
            take_turned(3 * b + 2)
            for half in range(TT):
                n = b * TT + half + 1
                act.wait_ge(gate_full, n)
                act.activation(silu_sb[:], logits[0][:, 0:I], ACT.Silu).then_inc(silu_ready, 1)
                act.wait_ge(hT_full, n)
                act.activation(hT_sb[:, 0:5 * P], eT_ps[:, 0:5 * P], ACT.Copy)
                act.activation(hT_sb[0:I - 5 * P, 5 * P:6 * P], eT_ps[0:I - 5 * P, 5 * P:6 * P], ACT.Copy).then_inc(hT_taken, 1)

    @block.tensor
    def _(pe):
        for k, (dst, n) in enumerate(WEIGHT_TURNS):
            pe.wait_ge(w_quant, dst + 1)
            if k >= 2:
                pe.wait_ge(w_taken, k - 1)
            o = logits[k % 2]
            if dst < 2:
                src = (gate_in, up_in)[dst]
                for i in range(IT):
                    ins = pe.transpose(o[:, i * P:(i + 1) * P], src[:, i * DM + n * P:i * DM + (n + 1) * P], ident[:])
            else:
                for i in range(2):
                    kk = 2 * n + i
                    w = min(P, I - kk * P)
                    for r in range(TT):
                        ins = pe.transpose(o[0:w, i * DM + r * P:i * DM + (r + 1) * P],
                                           down_in[:, r * I + kk * P:r * I + kk * P + w], ident[:])
            ins.then_inc(w_turned, 1)
        pe.wait_ge(w_taken, len(WEIGHT_TURNS))

        def turn(k, src):
            pe.wait_ge(rows_ready, k + 1)
            for c in range(2):
                for half in range(TT):
                    at = c * T + half * P
                    ins = pe.transpose(turn_ps[:, at:at + P], src[:, half, c * P:(c + 1) * P], ident[:])
            ins.then_inc(turned_full, 1)
            pe.wait_ge(turned_taken, k + 1)

        def halves(half):
            return slice(half * P, (half + 1) * P)

        with pe.Fori(0, B) as b:
            turn(3 * b, xq)
            for w, o, full in ((wq_sb, logits[0], q_full), (wk_sb, logits[1], k_full)):
                for m in range(QC):
                    for c in range(2):
                        ins = pe.matmul(o[:, m * T:(m + 1) * T], w[:, c, m * P:(m + 1) * P], turned[:, c, :],
                                        start=(c == 0), stop=(c == 1))
                ins.then_inc(full, 1)
            for half in range(TT):
                for c in range(2):
                    ins = pe.matmul(o_ps[:, half * DM:(half + 1) * DM], turned[:, c, halves(half)], wv_sb[:, c, :],
                                    start=(c == 0), stop=(c == 1))
            ins.then_inc(v_full, 1)
            pe.wait_ge(q_taken, b + 1)
            pe.wait_ge(k_taken, b + 1)

            def values(u):
                pe.wait_ge(eT_taken, b * UNITS + u + 1)
                half = u // (FH // HG)
                for h in range(HG):
                    head = head_of(u, h)
                    for s in range(TT):
                        at = (h * TT + s) * P
                        ins = pe.matmul(o_ps[:, half * DM + head * FD:half * DM + (head + 1) * FD],
                                        eT_sb[:, u % 2, at:at + P], v2_sb[:, s, head * FD:(head + 1) * FD],
                                        start=(s == 0), stop=(s == TT - 1))
                ins.then_inc(av_done, 1)

            def turn_probs(u):
                pe.wait_ge(exp_ready, b * UNITS + u + 1)
                if u >= 1:
                    pe.wait_ge(eT_taken, b * UNITS + u)
                for h in range(HG):
                    for s in range(TT):
                        at = (h * TT + s) * P
                        ins = pe.transpose(eT_ps[:, at:at + P], e_sb[:, u % 2, h, s * P:(s + 1) * P], ident[:])
                ins.then_inc(eT_full, 1)

            for u in range(UNITS):
                half = u // (FH // HG)
                if u >= 2:
                    pe.wait_ge(exp_ready, b * UNITS + u - 1)
                for h in range(HG):
                    head = head_of(u, h)
                    r = head * FPAD % P
                    ins = pe.matmul(logits[u % 2][:, h * T:(h + 1) * T], q_sb[r:r + FPAD, head * FPAD // P, halves(half)],
                                    k_sb[r:r + FPAD, head * FPAD // P, :], start=True, stop=True)
                ins.then_inc(logits_full, 1)
                if u == 1:
                    pe.wait_ge(v_taken, b + 1)
                if u >= 1:
                    turn_probs(u - 1)
                if u >= 2:
                    values(u - 2)
            turn_probs(UNITS - 1)
            values(UNITS - 2)
            values(UNITS - 1)
            turn(3 * b + 1, o_sb)
            for half in range(TT):
                for c in range(2):
                    ins = pe.matmul(eT_ps[:, half * DM:(half + 1) * DM], turned[:, c, halves(half)], wo2_sb[:, c, :],
                                    start=(c == 0), stop=(c == 1))
            ins.then_inc(proj_full, 1)
            turn(3 * b + 2, xfq)
            for half in range(TT):
                n = b * TT + half + 1
                for w, o, full in ((gateT, logits[0], gate_full), (upT, logits[1], up_full)):
                    for at, width in HALVES:
                        for c in range(2):
                            ins = pe.matmul(o[:, at:at + width], turned[:, c, halves(half)], w[:, c, at:at + width],
                                            start=(c == 0), stop=(c == 1))
                    ins.then_inc(full, 1)
                pe.wait_ge(hq_ready, n)
                for i in range(IT):
                    w = min(P, I - i * P)
                    ins = pe.transpose(eT_ps[0:w, i * P:(i + 1) * P], hq_sb[:, i * P:i * P + w], ident[:])
                ins.then_inc(hT_full, 1)
                pe.wait_ge(hT_taken, n)
                for i in range(IT):
                    w = min(P, I - i * P)
                    ins = pe.matmul(o_ps[:, 0:DM], hT_sb[0:w, i * P:(i + 1) * P], downT[0:w, i, :],
                                    start=(i == 0), stop=(i == IT - 1))
                ins.then_inc(down_full, 1)
                pe.wait_ge(row_done, n)


def kernel(**inputs):
    import concourse.bacc as _bacc
    from concourse.bass_utils import run_bass_kernel_spmd as _run

    a = {k: np.asarray(v) for k, v in inputs.items()}
    half = P // 2

    def pair_columns(w):
        return w.reshape(2, P, NB, P).transpose(2, 1, 0, 3).reshape(NB, P, 2 * P)

    def rows_of(w):
        return w.reshape(-1, P, w.shape[1]).transpose(1, 0, 2)

    def padded_heads(w):
        w = w.reshape(FH, FD, -1)
        return np.concatenate([w, np.zeros((FH, FPAD - FD, w.shape[2]), w.dtype)], axis=1).reshape(FH * FPAD, -1)

    def across(v):
        return np.broadcast_to(v[None, ...], (P,) + v.shape)

    def padded_rows(w):
        return np.concatenate([w, np.zeros((IT * P - I, w.shape[1]), w.dtype)], axis=0)

    freqs = np.power(np.float32(10000.0), (2.0 * np.arange(0, DM, 2, dtype=np.float32) / DM).astype(np.float32))
    def twice(w):
        w = w.reshape(2, P, NB, 2, 1, half).transpose(2, 1, 0, 3, 4, 5)
        return np.broadcast_to(w, w.shape[:4] + (2, half)).reshape(NB, P, 4 * P)

    temps = np.broadcast_to(a["L0_xattn_inv_temp"].reshape(NB, 1, 2), (NB, P, 2))
    arrays = {
        "x": a["x"],
        "ctx_t": a["ctx_1024"].transpose(0, 2, 1).reshape(B, 2, P, S),
        "mask": a["mask_BxS2_bf1"].view(np.uint8),
        "w_pack": np.concatenate([twice(a["L0_xattn_Wq"]), pair_columns(a["L0_xattn_Wk"]),
                                  pair_columns(a["L0_xattn_Wv"]), temps], axis=2),
        "w_out": a["L0_xattn_Wo"].reshape(NB, P, DM),
        "sa_wq": rows_of(padded_heads(a["L0_attn_Wq"]).T),
        "sa_wk": rows_of(padded_heads(a["L0_attn_Wk"]).T),
        "sa_wv": rows_of(a["L0_attn_Wv"].T),
        "sa_wo": rows_of(a["L0_attn_Wo"].T),
        "sa_cols": np.stack([padded_heads(a[f"L0_attn_b{n}"][:, None]).reshape(QC, P).T for n in "qk"], axis=1),
        "sa_rows": across(np.stack([a["L0_attn_bv"], a["L0_attn_bo"], a["L0_attn_ln_gamma"], a["L0_attn_ln_beta"]])),
        "rby": across(a["L0_attn_rby"]),
        "freqs": across(freqs.astype(np.float32)),
        "positions": np.arange(T, dtype=np.float32).reshape(TT, P).T,
        "w_gate": rows_of(padded_rows(a["L0_ffn_w_gate"])).reshape(P, IT * DM),
        "w_up": rows_of(padded_rows(a["L0_ffn_w_up"])).reshape(P, IT * DM),
        "w_down": rows_of(a["L0_ffn_w_down"]).reshape(P, TT * I),
    }
    nc = _bacc.Bacc("TRN2", target_bir_lowering=False, num_devices=1, dynamic_dma_scratch_size=1024)
    aps = {}
    arrays = {k: np.ascontiguousarray(v) for k, v in arrays.items()}
    for name, v in arrays.items():
        aps[name] = nc.dram_tensor(name, v.shape, mybir.dt.from_np(v.dtype), kind="ExternalInput").ap()
    out = nc.dram_tensor("out", (B, T, DM), F32, kind="ExternalOutput").ap()
    build(nc, out=out, **aps)
    r = _run(nc, [arrays], core_ids=[0])
    return r.results[0]["out"]
```

```python
import math
from contextlib import ExitStack

import numpy as np
import concourse.bass as bass
from concourse import mybir

F32 = mybir.dt.float32
F32R = mybir.dt.float32r
BF16 = mybir.dt.bfloat16
I32 = mybir.dt.int32
U8 = mybir.dt.uint8
U32 = mybir.dt.uint32
ALU = mybir.AluOpType
ACT = mybir.ActivationFunctionType
AX = mybir.AxisListType
RMAX = bass.bass_isa.ReduceOp.max

P = 128
B, T, DM = 4, 256, 256
S = 4096
H, D = 16, 64
TOPK = 32
NB = 2 * H // 2 // 2
PAIRS = B * NB
TT = T // P
CH = 1024
NC = S // CH
GRP = 128
NG = S // GRP
RUN = 512
RUNS = B * S // RUN
SLOW = 8 * NG
MASKED = -1.0e30
LOWEST = -3.0e38
EPS = 1e-5


WHOLE = (3,)
SPLIT = [c for c in range(NC) if c not in WHOLE]
PARTS = 1
assert 0 in SPLIT


def lows(tile, c):
    return len(SPLIT) * tile + SPLIT.index(c) + 1


def pair_schedule():
    behind = {(0, 3): ["V0"], (1, 0): ["V1"], (1, 2): ["V2"], (2, 0): ["V3"], (2, 1): ["K0"], (2, 2): ["QO"],
              (2, 3): ["OP"], (3, 0): ["K1"], (3, 1): ["K2"], (3, 3): ["K3"]}
    order = []
    for j in range(4):
        for c in range(NC):
            order += [("S", j, c), ("T", j, c)]
            for what in behind.get((j, c), []):
                order.append((what, 0, 0) if what in ("QO", "OP") else (what[0], int(what[1]), 0))
    return order


ORDER = pair_schedule()
USES = len(ORDER)
assert USES % 3 == 0
PROLOGUE = [("X", c, 0) for c in range(2)] + [("Q", 0, 0)] + [("K", n, 0) for n in range(NC)]


def uses_of(g):
    def there(use):
        kind, j, _ = use
        late = (kind == "T" and j < 2) or kind == "OP"
        if g == 0:
            return not late
        if g == PAIRS - 1:
            return kind != "K"
        if g == PAIRS:
            return late or kind == "QO"
        return True
    uses = [u for u in ORDER if there(u)]
    if g == PAIRS:
        uses.remove(("OP", 0, 0))
        uses.append(("OP", 0, 0))
    return uses


INDEX = {}
for _use in PROLOGUE:
    INDEX[(-1, _use)] = len(INDEX)
for _g in range(PAIRS + 1):
    for _use in uses_of(_g):
        INDEX[(_g, _use)] = len(INDEX)
PLACES = list(INDEX)
for _g in range(1, PAIRS - 1):
    assert all(INDEX[(_g, u)] == INDEX[(1, u)] + (_g - 1) * USES for u in ORDER)


def use_index(g, use):
    if isinstance(g, int):
        return INDEX[(g, use)]
    return g * USES + (INDEX[(1, use)] - USES)


def occupant(g, use):
    like = g if isinstance(g, int) else 2
    g0, before = PLACES[INDEX[(like, use)] - 3]
    return (g0 - like, before), g


def use_slot(g, use):
    return INDEX[(g if isinstance(g, int) else 1, use)] % 3


def build(nc, x, ctx_t, mask, w_pack, w_out, out, **later):
    with nc.sbuf_tensor("x_sb", [P, B * TT, DM], F32) as x_sb, nc.sbuf_tensor("ident", [P, P], F32) as ident:
        with ExitStack() as ctx:
            cross_attention(nc, ctx, x, ctx_t, mask, w_pack, w_out, x_sb, ident)
        with ExitStack() as ctx:
            self_attention_and_ffn(nc, ctx, x_sb, ident, out, **later)


def cross_attention(nc, ctx, x, ctx_t, mask, w_pack, w_out, x_sb, ident):
    def sb(name, shape, dt=F32):
        return ctx.enter_context(nc.sbuf_tensor(name, shape, dt))

    def psum(name, shape, dt=F32):
        return ctx.enter_context(nc.psum_tensor(name, shape, dt))

    def sem(name):
        return ctx.enter_context(nc.semaphore(name))

    WQ, WK, WT = 0, 4 * P, 6 * P
    ctx_sb = sb("ctx_sb", [P, 2, S])
    xnT = sb("xnT", [P, 2, B * T])
    weights = sb("weights", [P, WT + 2])
    weights_v = sb("weights_v", [P, 2 * P])
    wo_sb = sb("wo_sb", [P, 2, DM])
    keys = sb("keys", [P, S])
    keys_split = sb("keys_split", [P, 2, S], F32R)
    v_split = sb("v_split", [P, 2 * S // P, 2, D], F32R)
    q_both = sb("q_both", [P, 2, T])
    q_high = sb("q_high", [P, 2, T], F32R)
    q_low = sb("q_low", [P, 2, T], F32R)
    scores = sb("scores", [P, 2, S])
    probs = sb("probs", [P, 2, S])
    parts = sb("parts", [P, PARTS, 2, CH], F32R)
    cand = sb("cand", [P, 8 * NG])
    cand_left = sb("cand_left", [P, 8 * NG])
    top = sb("top", [P, 2, TOPK])
    slow_cand = sb("slow_cand", [P, S // SLOW * TOPK])
    over = sb("over", [P, NG])
    waited = sb("waited", [P, NC + 1])
    pool_waited = sb("pool_waited", [P, NC + 1])
    suspect = sb("suspect", [P, 1])
    suspect_twice = sb("suspect_twice", [P, 1])
    suspect_all = sb("suspect_all", [P, 1])
    suspect_int = sb("suspect_int", [P, 2], I32)
    neg_max = sb("neg_max", [P, 2])
    part_sums = sb("part_sums", [P, 2, 2, NC])
    row_sums = sb("row_sums", [P, 2, 2])
    fold = sb("fold", [P, D])
    o_raw = sb("o_raw", [P, 2 * P])
    denom = sb("denom", [P, 2])
    inv_denom = sb("inv_denom", [P, 2])
    o_pair = sb("o_pair", [P, TT, P])
    o_proj = sb("o_proj", [P, TT, DM])
    oT = o_proj[:].rearrange("p t c -> p (t c)")[:, 0:TT * P]
    mask_u8 = scores[0:RUNS, 1, 0:RUN // 4].bitcast(U8)
    mask_bias = sb("mask_bias", [RUNS, RUN], BF16)
    pick = sb("pick", [RUNS, RUNS], BF16)
    counts = scores[0:RUNS, 0, 0:RUN]
    missing = sb("missing", [RUNS, 1])
    missing_all = sb("missing_all", [RUNS, 1])
    missing_int = sb("missing_int", [RUNS, 2], I32)
    stats, mean_var, std, rstd = (cand[:, B * TT * i:B * TT * (i + k)].rearrange("p (i k) -> p i k", k=k)
                                  for i, k in ((0, 6), (6, 2), (8, 1), (9, 1)))
    xn = probs[:, 1, 0:B * TT * DM].rearrange("p (i c) -> p i c", c=DM)
    eps_col = sb("eps_col", [P, 1])

    ring = [psum(f"ring{i}", [P, CH]) for i in range(3)]
    o_acc = psum("o_acc", [P, 2, 2 * P])
    o_folded = psum("o_folded", [P, 2, 256])

    x_in = sem("x_in")
    mask_in = sem("mask_in")
    weights_in = sem("weights_in")
    weights_v_in = sem("weights_v_in")
    wo_in = [sem("wo_in0"), sem("wo_in1")]
    ctx_in = [sem(f"ctx_in{n}") for n in range(NC)]
    ident_step = sem("ident_step")
    pick_ready = sem("pick_ready")
    bias_ready = sem("bias_ready")
    missing_counted, missing_step, missing_ready = sem("missing_counted"), sem("missing_step"), sem("missing_ready")
    ln_step = sem("ln_step")
    std_ready = sem("std_ready")
    xn_ready = sem("xn_ready")
    ring_full = sem("ring_full")
    ring_free = sem("ring_free")
    max_ready = sem("max_ready")
    exp_done = sem("exp_done")
    masked = sem("masked")
    denom_ready = sem("denom_ready")
    norm_ready = sem("norm_ready")
    pv_done = sem("pv_done")
    turned_low = sem("turned_low")
    sums_ready = sem("sums_ready")
    fold_ready = sem("fold_ready")
    raw_taken = sem("raw_taken")
    folded = sem("folded")
    v_high, v_low = sem("v_high"), sem("v_low")
    o_read = sem("o_read")
    x_added = sem("x_added")
    suspect_sent = sem("suspect_sent")
    keys_high, keys_low, q_high_done, q_split = sem("keys_high"), sem("keys_low"), sem("q_high_done"), sem("q_split")
    suspect_step = sem("suspect_step")
    suspect_ready = sem("suspect_ready")
    topk_step = sem("topk_step")

    block = ctx.enter_context(nc.Block())
    LOOPS = PAIRS // 2

    @block.sync
    def _(sp):
        def load_weights(p):
            sp.dma_start(weights[:], w_pack[p, :, 0:WT + 2]).then_inc(weights_in, 16)

        def load_weights_v(p):
            sp.dma_start(weights_v[:], w_pack[p, :, WT + 2:]).then_inc(weights_v_in, 16)

        def load_wo(g, parity, p):
            sp.dma_start(wo_sb[:, parity, :], w_out[p]).then_inc(wo_in[parity], 16)

        def load_ctx(b, n):
            sp.dma_start(ctx_sb[:, :, n * CH:(n + 1) * CH],
                         ctx_t[b, :, :, n * CH:(n + 1) * CH].rearrange("c p s -> p c s")).then_inc(ctx_in[n], 16)

        sp.dma_start(x_sb[:], x.rearrange("b (t p) c -> p (b t) c", p=P)).then_inc(x_in, 16)
        sp.dma_start(mask_u8, mask.rearrange("b (n k) -> (b n) k", k=RUN)).then_inc(mask_in, 16)
        load_weights(0)
        for n in range(NC):
            load_ctx(0, n)
        load_weights_v(0)
        load_wo(0, 0, 0)
        sp.wait_ge(ring_full, use_index(-1, ("K", NC - 1, 0)) + 1)
        load_weights(1)

        for k in range(PAIRS):
            if k % NB == NB - 1 and k + 1 < PAIRS:
                for n in range(NC):
                    sp.wait_ge(ring_full, use_index(k, ("V", n, 0)) + 1)
                    load_ctx((k + 1) // NB, n)
            if k + 1 < PAIRS:
                sp.wait_ge(ring_full, use_index(k, ("V", NC - 1, 0)) + 1)
                load_weights_v((k + 1) % NB)
            if k + 2 < PAIRS:
                sp.wait_ge(ring_full, use_index(k, ("K", NC - 1, 0)) + 1)
                load_weights((k + 2) % NB)
            if k + 1 < PAIRS:
                sp.wait_ge(ring_full, use_index(k, ORDER[-1]) + 1)
                load_wo(k + 1, (k + 1) % 2, (k + 1) % NB)

    @block.gpsimd
    def _(pool):
        pool.memset(ident[:], 0.0).then_inc(ident_step, 1)
        pool.memset(pick[:], 0.0).then_inc(ident_step, 1)
        pool.wait_ge(ident_step, 2)
        pool.affine_select(out=ident[:], in_=ident[:], compare_op=ALU.not_equal, fill=1.0, base=0,
                           pattern=[[-1, P]], channel_multiplier=1).then_inc(ident_step, 1)
        pool.affine_select(out=pick[:], in_=pick[:], compare_op=ALU.not_equal, fill=1.0, base=0,
                           pattern=[[-1, RUNS]], channel_multiplier=1).then_inc(pick_ready, 1)
        pool.wait_ge(mask_in, 16)
        pool.tensor_scalar(mask_bias[:], mask_u8, -1.0, -MASKED, ALU.add, ALU.mult).then_inc(bias_ready, 1)
        pool.wait_ge(missing_counted, 1)
        pool.partition_all_reduce(missing_all[:], missing[:], RUNS, RMAX).then_inc(missing_step, 1)
        pool.wait_ge(missing_step, 1)
        pool.tensor_copy(missing_int[:, 0:1], missing_all[:]).then_inc(missing_ready, 1)

        def reduce_suspect(t):
            pool.wait_ge(suspect_sent, t + 1)
            pool.tensor_tensor(suspect_twice[:], suspect[:], suspect[:], ALU.add).then_inc(suspect_step, 1)
            pool.wait_ge(suspect_step, 1)
            pool.partition_all_reduce(suspect_all[:], suspect_twice[:], P, RMAX).then_inc(suspect_step, 1)
            pool.wait_ge(suspect_step, 2)
            pool.tensor_copy(suspect_int[:, 0:1], suspect_all[:]).then_inc(suspect_step, 1)
            pool.wait_ge(suspect_step, 3)
            pool.sem_clear(suspect_step)
            pool.sem_inc(suspect_ready, 1)

        def add_output(g, row):
            pool.wait_ge(ring_free, use_index(g + 1, ("OP", 0, 0)) + 1)
            pool.tensor_tensor(row, row, o_proj[:], ALU.add).then_inc(x_added, 1)

        def x_rows(g):
            if isinstance(g, int):
                b = g // NB
                return x_sb[:, b * TT:(b + 1) * TT, :]
            return x_sb[:, bass.ds((g // NB) * TT, TT), :]

        def addition(rows, c):
            pool.tensor_tensor(pool_waited[rows, c:c + 1], ident[rows, 0:1], ident[rows, 0:1], ALU.add)

        def split_keys(g, head, c, ready):
            rows = slice(head * D, (head + 1) * D)
            other = slice((1 - head) * D, (2 - head) * D)
            chunk = slice(c * CH, (c + 1) * CH)
            n = 8 * g + (2 * c + head if isinstance(g, int) and g == 0 else 4 * head + c) + 1
            pool.wait_ge(ring_free, ready + 1)
            addition(rows, c)
            pool.tensor_scalar(keys_split[rows, head, chunk], keys[rows, chunk], 1.0, 1.0, ALU.mult, ALU.mult)\
                .then_inc(keys_high, 1)
            pool.wait_ge(keys_high, n)
            pool.tensor_tensor(keys_split[other, head, chunk], keys[rows, chunk],
                               keys_split[rows, head, chunk].bitcast(F32), ALU.subtract).then_inc(keys_low, 1)
            pool.wait_ge(keys_low, n)

        def split_q(g, head, ready):
            pool.wait_ge(ring_free, ready + 1)
            addition(slice(0, P), NC)
            pool.tensor_scalar(q_high[:, head], q_both[:, head], 1.0, 1.0, ALU.mult, ALU.mult).then_inc(q_high_done, 1)
            pool.wait_ge(q_high_done, 2 * g + head + 1)
            pool.tensor_tensor(q_low[:, head], q_both[:, head], q_high[:, head].bitcast(F32), ALU.subtract)\
                .then_inc(q_split, 1)
            pool.wait_ge(q_split, 2 * g + head + 1)

        def split_v(g, n):
            raw = keys[:, n * CH:(n + 1) * CH].rearrange("p (a d) -> p a d", d=D)
            at = n * (2 * CH // P)
            high, low = (v_split[:, at:at + 2 * CH // P, i, :] for i in range(2))
            if not (isinstance(g, int) and g == 0):
                pool.wait_ge(pv_done, 4 * (4 * g - 1) + n + 1)
            pool.wait_ge(ring_free, use_index(g, ("V", n, 0)) + 1)
            addition(slice(0, P), n)
            pool.tensor_scalar(high, raw, 1.0, 1.0, ALU.mult, ALU.mult).then_inc(v_high, 1)
            pool.wait_ge(v_high, 4 * g + n + 1)
            pool.tensor_tensor(low, raw, high.bitcast(F32), ALU.subtract).then_inc(v_low, 1)
            pool.wait_ge(v_low, 4 * g + n + 1)

        def pair(g):
            first, last = (isinstance(g, int) and g == k for k in (0, PAIRS - 1))
            if not first:
                reduce_suspect(4 * g - 1)
                before = use_index(g - 1, ("S", 3, NC - 1))
                split_q(g, 1, before)
                for c in range(NC):
                    split_keys(g, 1, c, before)
            reduce_suspect(4 * g)
            split_v(g, 0)
            split_v(g, 1)
            reduce_suspect(4 * g + 1)
            split_v(g, 2)
            split_v(g, 3)
            for c in range(NC):
                if c == 1 and not last:
                    split_q(g + 1, 0, use_index(g, ("QO", 0, 0)))
                if c == 2:
                    reduce_suspect(4 * g + 2)
                if c == 3 and not first:
                    add_output(g - 1, x_rows(g - 1))
                    pool.wait_ge(x_added, g)
                if not last:
                    split_keys(g + 1, 0, c, use_index(g, ("K", c, 0)))

        for head in range(2):
            split_q(0, head, use_index(-1, ("Q", 0, 0)))
        for c in range(NC):
            for head in range(2):
                split_keys(0, head, c, use_index(-1, ("K", c, 0)))
        pair(0)
        with pool.Fori(1, PAIRS - 1) as g:
            pair(g)
        pair(PAIRS - 1)
        reduce_suspect(4 * PAIRS - 1)
        add_output(PAIRS - 1, x_rows(PAIRS - 1))

    @block.vector
    def _(dve):
        steps = [0]

        def then(ins):
            steps[0] += 1
            ins.then_inc(ln_step, 1)
            dve.wait_ge(ln_step, steps[0])

        dve.memset(eps_col[:], EPS)
        dve.wait_ge(mask_in, 16)
        dve.tensor_scalar(counts, mask_u8, 0.5, None, ALU.is_lt, ALU.add, accum_out=missing[:])\
            .then_inc(missing_counted, 1)
        dve.wait_ge(ident_step, 3)
        dve.tensor_tensor(fold[:], ident[:, 0:D], ident[:, D:2 * D], ALU.add).then_inc(fold_ready, 1)
        dve.wait_ge(x_in, 16)
        for i in range(B * TT):
            last = dve.bn_stats(stats[:, i, :], x_sb[:, i, :])
        then(last)
        for i in range(B * TT):
            last = dve.bn_aggr(mean_var[:, i, :], stats[:, i, :])
        then(last)
        dve.wait_ge(std_ready, 1)
        then(dve.reciprocal(rstd, std))
        for i in range(B * TT):
            last = dve.tensor_scalar(xn[:, i, :], x_sb[:, i, :], mean_var[:, i, 0:1], rstd[:, i, :],
                                     ALU.subtract, ALU.mult)
        last.then_inc(xn_ready, 1)

        def group_tops(g, j, c):
            if c == 0 and not (isinstance(g, int) and g == 0 and j == 0):
                dve.wait_ge(suspect_sent, 4 * g + j)
            dve.wait_ge(ring_free, use_index(g, ("S", j, c)) + 1)
            dve.memset(waited[:, c:c + 1], 0.0)
            for k in range(c * (CH // GRP), (c + 1) * (CH // GRP)):
                last = dve.max(cand[:, 8 * k:8 * k + 8], scores[:, j % 2, k * GRP:(k + 1) * GRP])
            return last

        def largest(g, j, last):
            q, t = j % 2, 4 * g + j
            first = isinstance(g, int) and g == 0

            def replaced(r):
                return dve.match_replace(cand_left[:], top[:, q, 8 * r - 8:8 * r], cand[:] if r == 1 else cand_left[:],
                                         LOWEST)

            def next_eight(r):
                return dve.max(top[:, q, 8 * r:8 * r + 8], cand_left[:])

            last.then_inc(topk_step, 1)
            dve.wait_ge(topk_step, 1)
            dve.max(top[:, q, 0:8], cand[:]).then_inc(topk_step, 1)
            dve.wait_ge(topk_step, 2)
            dve.tensor_scalar(neg_max[:, q:q + 1], top[:, q, 0:1], -float(D) ** -0.5, None,
                              ALU.mult).then_inc(max_ready, 1)
            replaced(1).then_inc(topk_step, 1)
            if NC - 1 in SPLIT and not (first and j < 2):
                low_turned(g, j, NC - 1)
            dve.wait_ge(topk_step, 3)
            next_eight(1).then_inc(topk_step, 1)
            if not (first and j == 0):
                keep(t - 1, 1 - q, NC - 2)
            dve.wait_ge(topk_step, 4)
            replaced(2).then_inc(topk_step, 1)
            if not (first and j == 0):
                keep(t - 1, 1 - q, NC - 1)
            dve.wait_ge(topk_step, 5)
            next_eight(2).then_inc(topk_step, 1)
            if not (first and j == 0):
                sum_parts(t - 1, 1 - q)
            dve.wait_ge(topk_step, 6)
            replaced(3).then_inc(topk_step, 1)
            if not (first and j == 0):
                divisor(t - 1, 1 - q)
            dve.wait_ge(topk_step, 7)
            next_eight(3).then_inc(topk_step, 1)
            if not (first and j == 0):
                inverse(t - 1, 1 - q)
            dve.wait_ge(topk_step, 8)
            dve.sem_clear(topk_step)
            dve.tensor_scalar(over[:], cand[:, 7:8 * NG:8], top[:, q, TOPK - 1:TOPK], None, ALU.is_gt, ALU.add,
                              accum_out=suspect[:]).then_inc(suspect_sent, 1)

        def keep(t, q, c):
            dve.wait_ge(exp_done, 4 * t + c + 1)
            chunk = probs[:, q, c * CH:(c + 1) * CH]
            dve.scalar_tensor_tensor(out=chunk, in0=scores[:, q, c * CH:(c + 1) * CH],
                                     scalar=top[:, q, TOPK - 1:TOPK], in1=chunk, op0=ALU.is_ge, op1=ALU.mult,
                                     accum_out=part_sums[:, q, 1, c:c + 1]).then_inc(masked, 1)

        def sum_parts(t, q):
            dve.wait_ge(masked, 4 * t + NC)
            dve.tensor_reduce(row_sums[:, q, :], part_sums[:, q], AX.X, ALU.add).then_inc(sums_ready, 1)

        def divisor(t, q):
            dve.wait_ge(sums_ready, t + 1)
            dve.scalar_tensor_tensor(out=denom[:, q:q + 1], in0=row_sums[:, q, 0:1], scalar=1e-8,
                                     in1=row_sums[:, q, 1:2], op0=ALU.mult, op1=ALU.add).then_inc(denom_ready, 1)

        def inverse(t, q):
            dve.wait_ge(denom_ready, t + 1)
            dve.reciprocal(inv_denom[:, q:q + 1], denom[:, q:q + 1]).then_inc(norm_ready, 1)

        def low_turned(g, j, c):
            k = c % PARTS
            dve.wait_ge(ring_free, use_index(g, ("T", j, c)) + 1)
            dve.tensor_tensor(parts[:, k, 1, :], ring[use_slot(g, ("T", j, c))][:], parts[:, k, 0, :].bitcast(F32),
                              ALU.subtract).then_inc(turned_low, 1)

        def settle(t, q):
            dve.wait_ge(suspect_ready, 1)
            flag = dve.value_load(suspect_int[0:1, 0:1], min_val=0, max_val=2 * NG)
            dve.sem_clear(suspect_ready)
            with dve.If(flag):
                for c in range(S // SLOW):
                    for r in range(TOPK // 8):
                        src = scores[:, q, c * SLOW:(c + 1) * SLOW] if r == 0 else cand_left[:]
                        at = c * TOPK + 8 * r
                        dve.max(slow_cand[:, at:at + 8], src)
                        dve.drain()
                        if r < TOPK // 8 - 1:
                            dve.match_replace(cand_left[:], slow_cand[:, at:at + 8], src, LOWEST)
                            dve.drain()
                for r in range(TOPK // 8):
                    dve.max(top[:, q, 8 * r:8 * r + 8], slow_cand[:])
                    dve.drain()
                    if r < TOPK // 8 - 1:
                        dve.match_replace(slow_cand[:], top[:, q, 8 * r:8 * r + 8], slow_cand[:], LOWEST)
                        dve.drain()

        def pair(g):
            first = isinstance(g, int) and g == 0
            for j in range(4):
                t = 4 * g + j
                before = not (first and j == 0)
                q = (j - 1) % 2
                for c in range(NC):
                    if c == 0 and not (first and j < 2):
                        low_turned(g, j, c)
                    last = group_tops(g, j, c)
                    if 0 < c < NC - 1 and c in SPLIT and not (first and j < 2):
                        low_turned(g, j, c)
                    if before and c == 1:
                        settle(t - 1, q)
                    if before and 1 <= c < NC - 1:
                        keep(t - 1, q, c - 1)
                largest(g, j, last)

        pair(0)
        with dve.Fori(1, PAIRS - 1) as g:
            pair(g)
        pair(PAIRS - 1)
        for c in SPLIT:
            low_turned(PAIRS, 0, c)
        settle(4 * PAIRS - 1, 1)
        for c in range(NC):
            keep(4 * PAIRS - 1, 1, c)
        sum_parts(4 * PAIRS - 1, 1)
        divisor(4 * PAIRS - 1, 1)
        inverse(4 * PAIRS - 1, 1)
        for c in SPLIT:
            low_turned(PAIRS, 1, c)

    @block.scalar
    def _(act):
        act.wait_ge(ln_step, 2)
        act.activation(std, mean_var[:, :, 1:2], ACT.Sqrt, bias=eps_col[:]).then_inc(std_ready, 1)

        def copy(dst, src):
            return act.activation(dst, src, ACT.Copy)

        def take_q(slot):
            for head in range(2):
                ins = act.activation(q_both[:, head, :], ring[slot][:, head * T:(head + 1) * T], ACT.Copy,
                                     scale=weights[:, WT + head:WT + head + 1])
            return ins

        def take_kv(n, slot):
            return copy(keys[:, n * CH:(n + 1) * CH], ring[slot][:])

        for use in PROLOGUE:
            kind, n, _ = use
            slot = use_slot(-1, use)
            act.wait_ge(ring_full, use_index(-1, use) + 1)
            if kind == "X":
                ins = copy(xnT[:, n, :], ring[slot][:])
            elif kind == "Q":
                ins = take_q(slot)
            else:
                ins = take_kv(n, slot)
            ins.then_inc(ring_free, 1)

        def exponentials(t, q, c):
            if c == 0:
                act.wait_ge(max_ready, t + 1)
            act.activation(probs[:, q, c * CH:(c + 1) * CH], scores[:, q, c * CH:(c + 1) * CH], ACT.Exp,
                           bias=neg_max[:, q:q + 1], scale=float(D) ** -0.5,
                           accum_out=part_sums[:, q, 0, c:c + 1]).then_inc(exp_done, 1)

        def take_raw(t, j):
            act.wait_ge(pv_done, 4 * t + 4)
            copy(o_raw[:], o_acc[:, j % 2, :]).then_inc(raw_taken, 1)

        def take_output(t, j):
            head, half = j // 2, j % 2
            act.wait_ge(folded, t + 1)
            act.wait_ge(norm_ready, t + 1)
            act.activation(o_pair[:, half, head * D:(head + 1) * D], o_folded[:, j % 2, 0:D], ACT.Copy,
                           scale=inv_denom[:, j % 2:j % 2 + 1]).then_inc(o_read, 1)

        def pair(g, parity):
            first, last, left = (isinstance(g, int) and g == k for k in (0, PAIRS - 1, PAIRS))
            for use in (uses_of(g) if isinstance(g, int) else ORDER):
                kind, j, c = use
                t = 4 * g + j
                slot = use_slot(g, use)
                if left and kind == "QO":
                    take_raw(4 * PAIRS - 1, 3)
                    take_output(4 * PAIRS - 1, 3)
                act.wait_ge(ring_full, use_index(g, use) + 1)
                if kind == "S":
                    if not (first and j < 2):
                        act.wait_ge(masked, 4 * (t - 2) + c + 1)
                    copy(scores[:, j % 2, c * CH:(c + 1) * CH], ring[slot][:]).then_inc(ring_free, 1)
                elif kind == "T":
                    if c in SPLIT and not (first and j == 2 and c < PARTS):
                        act.wait_ge(pv_done, 4 * (t - 2) + (c - PARTS + 1 if c >= PARTS else SPLIT[c - PARTS] - 3))
                    copy(parts[:, c % PARTS, 0, :] if c in SPLIT else probs[:, j % 2, c * CH:(c + 1) * CH],
                         ring[slot][:]).then_inc(ring_free, 1)
                elif kind in "KV":
                    if kind == "V":
                        act.wait_ge(keys_low, 8 if first else 8 * g + 4 + j + 1)
                    elif kind == "K":
                        act.wait_ge(v_low, 4 * g + j + 1)
                    take_kv(j, slot).then_inc(ring_free, 1)
                elif kind == "QO":
                    if not first:
                        if not (isinstance(g, int) and g == 1):
                            act.wait_ge(x_added, g - 1)
                        ins = copy(oT, ring[slot][:, 512:512 + TT * P])
                    if not (last or left):
                        act.wait_ge(q_split, 2 * g + 2)
                        ins = take_q(slot)
                    ins.then_inc(ring_free, 1)
                elif kind == "OP":
                    copy(o_proj[:].rearrange("p t c -> p (t c)"), ring[slot][:, 0:TT * DM]).then_inc(ring_free, 1)
                if kind == "T" or (kind == "S" and first and j < 2):
                    if c < 2 and not (first and j < 3):
                        (take_raw if c == 0 else take_output)(t - 3, (j - 3) % 4)
                    if not (first and j == 0) and not (left and j == 1):
                        exponentials(t - 1, (j - 1) % 2, c)

        pair(0, 0)
        pair(1, 1)
        with act.Fori(1, PAIRS // 2 - 1) as i:
            pair(2 * i, 0)
            pair(2 * i + 1, 1)
        pair(PAIRS - 2, 0)
        pair(PAIRS - 1, 1)
        pair(PAIRS, 0)

    @block.tensor
    def _(pe):
        def begin(g, use):
            index = use_index(g, use)
            if not (isinstance(index, int) and index < 3):
                pe.wait_ge(ring_free, index - 2)
                (g0, (kind, j, c)), at = occupant(g, use)
                if kind == "T" and c in SPLIT:
                    pe.wait_ge(turned_low, lows(4 * (at + g0) + j - 2, c))

        def turn_x(c, slot):
            for i in range(B * TT):
                last = pe.transpose(ring[slot][:, i * P:(i + 1) * P], xn[:, i, c * P:(c + 1) * P], ident[:])
            return last

        def project_q(g, slot):
            if isinstance(g, int):
                at = g // NB * T
            else:
                at = (g // NB) * T
            for head in range(2):
                for c in range(2):
                    w = WQ + (2 * c + head) * P
                    last = pe.matmul(ring[slot][:, head * T:(head + 1) * T],
                                     weights[:, w:w + P],
                                     xnT[:, c, bass.ds(at, T)], start=(c == 0), stop=(c == 1))
            return last

        def project_k(n, slot):
            for u in range(CH // 512):
                for c in range(2):
                    at = n * CH + u * 512
                    w = WK + c * P
                    last = pe.matmul(ring[slot][:, u * 512:(u + 1) * 512], weights[:, w:w + P],
                                     ctx_sb[:, c, at:at + 512], start=(c == 0), stop=(c == 1))
            return last

        def project_v(n, slot):
            for i in range(CH // P):
                for c in range(2):
                    at = n * CH + i * P
                    w = c * P
                    last = pe.matmul(ring[slot][:, i * P:(i + 1) * P], ctx_sb[:, c, at:at + P],
                                     weights_v[:, w:w + P], start=(c == 0), stop=(c == 1))
            return last

        def need_context(g, n):
            pe.wait_ge(ctx_in[n], (g // NB) * 16 + 16)

        pe.wait_ge(ident_step, 3)
        pe.wait_ge(xn_ready, 1)
        for use in PROLOGUE:
            kind, n, _ = use
            slot = use_slot(-1, use)
            begin(-1, use)
            if kind == "X":
                ins = turn_x(n, slot)
            elif kind == "Q":
                pe.wait_ge(weights_in, 16)
                pe.wait_ge(ring_free, 2)
                ins = project_q(0, slot)
            elif kind == "K":
                need_context(0, n)
                ins = project_k(n, slot)
            ins.then_inc(ring_full, 1)
        pe.wait_ge(pick_ready, 1)
        pe.wait_ge(fold_ready, 1)
        pe.wait_ge(bias_ready, 1)

        def multiply_values(tile, j, c, g, turned_index):
            if c in SPLIT:
                pe.wait_ge(turned_low, lows(tile, c))
            else:
                pe.wait_ge(ring_free, turned_index + 1)
            head = j // 2
            if j == 0:
                pe.wait_ge(v_low, 4 * g + c + 1)
            for i in range(CH // P):
                k = 2 * (c * (CH // P) + i) + head
                values = v_split[:, k, :, :].rearrange("p a d -> p (a d)")
                if c in SPLIT:
                    last = pe.matmul(o_acc[:, j % 2, :], values, parts[:, c % PARTS, :, i * P:(i + 1) * P],
                                     start=(c == 0 and i == 0), stop=(c == NC - 1 and i == CH // P - 1))
                else:
                    last = pe.matmul(o_acc[:, j % 2, 0:P], values.bitcast(F32),
                                     probs[:, j % 2, c * CH + i * P:c * CH + (i + 1) * P],
                                     start=False, stop=(c == NC - 1 and i == CH // P - 1))
            last.then_inc(pv_done, 1)

        def add_parts(tile, j):
            pe.wait_ge(raw_taken, tile + 1)
            if not (isinstance(tile, int) and tile < 2):
                pe.wait_ge(o_read, tile - 1)
            for i in range(2):
                last = pe.matmul(o_folded[:, j % 2, 0:D], o_raw[:, i * P:(i + 1) * P], fold[:], start=(i == 0), stop=(i == 1))
            last.then_inc(folded, 1)

        def pair(g, i, parity, with_mask):
            first, last, left = (isinstance(g, int) and g == k for k in (0, PAIRS - 1, PAIRS))

            def last_chunk(j):
                multiply_values(4 * g + j - 3, (j - 3) % 4, NC - 1, g if j == 3 else g - 1,
                                use_index(g, ("T", j - 1, NC - 1)) if j else use_index(g - 1, ("T", 3, NC - 1)))

            for use in (uses_of(g) if isinstance(g, int) else ORDER):
                kind, j, c = use
                slot = use_slot(g, use)
                index = use_index(g, use)
                if left and kind == "T" and c == 0:
                    last_chunk(j)
                if left and kind == "T" and c == 1:
                    add_parts(4 * g + j - 3, (j - 3) % 4)
                if left and kind == "QO":
                    last_chunk(2)
                    add_parts(4 * g - 1, 3)
                begin(g, use)
                if kind == "S":
                    head, half = j // 2, j % 2
                    b = g // NB
                    if half == 0:
                        pe.wait_ge(keys_low, 8 * g + (2 * c + head if first else 4 * head + c) + 1)
                    if half == 0 and c == 0:
                        pe.wait_ge(q_split, 2 * g + head + 1)
                    for u in range(CH // 512):
                        o = ring[slot][:, u * 512:(u + 1) * 512]
                        at = c * CH + u * 512
                        pe.matmul(o, q_high[:, head, half * P:(half + 1) * P],
                                  keys_split[:, head, at:at + 512], start=True, stop=False)
                        ins = pe.matmul(o, q_low[:, head, half * P:(half + 1) * P],
                                        keys_split[:, head, at:at + 512], start=False, stop=not with_mask)
                        if with_mask:
                            run = b * (S // RUN) + at // RUN
                            column = pick[:, run:run + 1] if isinstance(g, int) else pick[:, bass.ds(run, 1)]
                            ins = pe.matmul(o, column.broadcast_to((RUNS, P)), mask_bias[:], start=False, stop=True)
                    ins.then_inc(ring_full, 1)
                    if c == 0 and not (first and j < 3):
                        last_chunk(j)
                    if c == 1 and not (first and j < 3):
                        add_parts(4 * g + j - 3, (j - 3) % 4)
                elif kind == "T":
                    tile, jj = 4 * g + j - 2, (j - 2) % 4
                    pe.wait_ge(masked, 4 * tile + c + 1)
                    for k in range(CH // P):
                        at = c * CH + k * P
                        ins = pe.transpose(ring[slot][:, k * P:(k + 1) * P], probs[:, jj % 2, at:at + P], ident[:])
                    ins.then_inc(ring_full, 1)
                    if c == 1 and not (first and j < 4):
                        pe.wait_ge(raw_taken, tile - 1)
                    if c >= 1:
                        multiply_values(tile, jj, c - 1, g if j >= 2 else g - 1, use_index(g, ("T", j, c - 1)))
                elif kind in "KV":
                    if kind == "K":
                        if j == 0:
                            pe.wait_ge(weights_in, 16 * g + 32)
                        need_context(g + 1, j)
                        project_k(j, slot).then_inc(ring_full, 1)
                    else:
                        if j == 0:
                            pe.wait_ge(weights_v_in, 16 * g + 16)
                        project_v(j, slot).then_inc(ring_full, 1)
                elif kind == "QO":
                    if not first:
                        pe.wait_ge(o_read, 4 * g)
                        for half in range(TT):
                            ins = pe.transpose(ring[slot][:, 512 + half * P:512 + (half + 1) * P], o_pair[:, half, :],
                                               ident[:])
                    if not (last or left):
                        ins = project_q(g + 1, slot)
                    ins.then_inc(ring_full, 1)
                elif kind == "OP":
                    pe.wait_ge(ring_free, use_index(g, ("QO", 0, 0)) + 1)
                    pe.wait_ge(wo_in[1 - parity], (i + parity) * 16)
                    for half in range(TT):
                        ins = pe.matmul(ring[slot][:, half * DM:(half + 1) * DM], oT[:, half * P:(half + 1) * P],
                                        wo_sb[:, 1 - parity, :], start=True, stop=True)
                    ins.then_inc(ring_full, 1)

        def all_pairs(with_mask):
            pair(0, 0, 0, with_mask)
            pair(1, 0, 1, with_mask)
            with pe.Fori(1, PAIRS // 2 - 1) as i:
                pair(2 * i, i, 0, with_mask)
                pair(2 * i + 1, i, 1, with_mask)
            pair(PAIRS - 2, PAIRS // 2 - 1, 0, with_mask)
            pair(PAIRS - 1, PAIRS // 2 - 1, 1, with_mask)
            pair(PAIRS, PAIRS // 2, 0, with_mask)

        pe.wait_ge(missing_ready, 1)
        flag = pe.value_load(missing_int[0:1, 0:1], min_val=0, max_val=RUN)
        with pe.If(flag):
            all_pairs(True)
        with pe.Else():
            all_pairs(False)


I = 704
IT = -(-I // P)
FH, FD = 16, 16
FPAD = 32
QC = FH * FPAD // P
HG = 4
UNITS = TT * (FH // HG)
BLK = 16
PHASE = 0.1 * math.sin(2.0 * math.pi * 0.25)
OUT_EPS = 0.1 * math.sin(2.0 * math.pi * 0.5)
ROUND_HALF = 1.5 * 2.0 ** 22
ROUND_ONE = 1.5 * 2.0 ** 23
ROUND_TWO = 1.5 * 2.0 ** 24
TWO_PI_A = 6.28125
TWO_PI_B = float(np.float32(2.0 * math.pi - 6.28125))
TWO_PI_C = 2.0 * math.pi - 6.28125 - TWO_PI_B
PI_BELOW = 3.1415925


def head_of(u, h):
    return h * (FH // HG) + u % (FH // HG)


def self_attention_and_ffn(nc, ctx, x_sb, ident, out, sa_wq, sa_wk, sa_wv, sa_wo, sa_cols, sa_rows, rby, freqs, positions,
                           w_gate, w_up, w_down):
    def sb(name, shape, dt=F32):
        return ctx.enter_context(nc.sbuf_tensor(name, shape, dt))

    def psum(name, shape, dt=F32):
        return ctx.enter_context(nc.psum_tensor(name, shape, dt))

    def sem(name):
        return ctx.enter_context(nc.semaphore(name))

    wq_sb = sb("wq_sb", [P, 2, QC * P])
    wk_sb = sb("wk_sb", [P, 2, QC * P])
    wv_sb = sb("wv_sb", [P, 2, DM])
    wo2_sb = sb("wo2_sb", [P, 2, DM])
    cols = sb("cols", [P, 2, QC])
    rows = sb("rows", [P, 4, DM])
    rby_sb = sb("rby_sb", [P, 3])
    freqs_sb = sb("freqs_sb", [P, DM // 2])
    pos_sb = sb("pos_sb", [P, TT])
    logit_scale = sb("logit_scale", [P, 1])
    out_scale = sb("out_scale", [P, 1])
    eps2 = sb("eps2", [P, 1])
    eps1 = sb("eps1", [P, 1])
    gamma_scale = sb("gamma_scale", [P, 1])
    small = sb("small", [P, 1])
    angle = sb("angle", [P, TT, DM // 2])
    turns = sb("turns", [P, TT, DM // 2])
    reduced = sb("reduced", [P, 2, TT, DM // 2])
    encoding = sb("encoding", [P, TT, DM])
    gate_in = sb("gate_in", [P, IT * DM])
    up_in = sb("up_in", [P, IT * DM])
    down_in = sb("down_in", [P, TT * I])
    gateT = sb("gateT", [P, 2, IT * P])
    upT = sb("upT", [P, 2, IT * P])
    downT = sb("downT", [P, IT, DM])
    WIDE = IT * DM
    qa = sb("qa", [P, WIDE])
    qb = sb("qb", [P, WIDE])
    qn = sb("qn", [P, WIDE])
    scale = sb("scale", [P, WIDE // BLK])
    inv_scale = sb("inv_scale", [P, WIDE // BLK])
    stats2 = sb("stats2", [P, TT, 6])
    mv2 = sb("mv2", [P, TT, 2])
    std2 = sb("std2", [P, TT])
    rstd2 = sb("rstd2", [P, TT])
    xq = sb("xq", [P, TT, DM])
    turned = sb("turned", [P, 2, T])
    q_sb = sb("q_sb", [P, QC, T])
    k_sb = sb("k_sb", [P, QC, T])
    v2_sb = sb("v2_sb", [P, TT, FH, FPAD])
    avT_sb = sb("avT_sb", [P, UNITS, P])
    neg_top = sb("neg_top", [P, 2, HG])
    e_sb = sb("e_sb", [P, 2, HG, T])
    sums = sb("sums", [P, TT, FH])
    inv_sums = sb("inv_sums", [P, TT, FH])
    eT_sb = sb("eT_sb", [P, 2, HG * TT * P])
    o_sb = sb("o_sb", [P, TT, DM])
    y_sb = sb("y_sb", [P, TT, DM])
    xf = sb("xf", [P, TT, DM])
    xfq = sb("xfq", [P, TT, DM])
    silu_sb = sb("silu_sb", [P, TT, I])
    h_sb = sb("h_sb", [P, I])
    hq_sb = sb("hq_sb", [P, TT, I])
    hT_sb = sb("hT_sb", [P, TT, IT * P])
    x_out = sb("x_out", [P, TT, DM])

    logits = [psum(f"logits{i}", [P, HG * T]) for i in range(2)]
    eT_ps = psum("eT_ps", [P, HG * TT * P])
    o_ps = psum("o_ps", [P, 512])
    turn_ps = psum("turn_ps", [P, 512])
    down_ps = (o_ps, turn_ps)
    avT_ps = (o_ps, turn_ps)

    consts_in = sem("consts_in")
    ffn_in = sem("ffn_in")
    prep_step = sem("prep_step")
    reduced_ready = sem("reduced_ready")
    encoding_ready = sem("encoding_ready")
    w_quant = sem("w_quant")
    w_turned = sem("w_turned")
    w_taken = sem("w_taken")
    dve_step = sem("dve_step")
    var_ready = sem("var_ready")
    std_done = sem("std_done")
    rows_ready = sem("rows_ready")
    turned_full = sem("turned_full")
    turned_taken = sem("turned_taken")
    q_full, k_full, v_full = sem("q_full"), sem("k_full"), sem("v_full")
    q_taken, k_taken, v_taken = sem("q_taken"), sem("k_taken"), sem("v_taken")
    logits_full, top_ready, exp_ready = sem("logits_full"), sem("top_ready"), sem("exp_ready")
    eT_full, eT_taken, av_done = sem("eT_full"), sem("eT_taken"), sem("av_done")
    av_taken, av_turned = sem("av_taken"), sem("av_turned")
    proj_full = sem("proj_full")
    gate_full, up_full, silu_ready = sem("gate_full"), sem("up_full"), sem("silu_ready")
    h_done = sem("h_done")
    hq_ready, hT_full, hT_taken = sem("hq_ready"), sem("hT_full"), sem("hT_taken")
    down_full, row_done, out_done = sem("down_full"), sem("row_done"), [sem(f"out_done{i}") for i in range(TT)]

    block = ctx.enter_context(nc.Block())
    HALVES = [(0, 512), (512, I - 512)]

    def weight_turned(dst, n):
        if dst == 2:
            return downT[:, 2 * n:2 * n + 2, :].rearrange("p a c -> p (a c)")
        return (gateT, upT)[dst][:, n, :]

    WEIGHT_TURNS = [(0, 0), (0, 1), (1, 0), (1, 1), (2, 0), (2, 1), (2, 2)]


    @block.sync
    def _(sp):
        for dst, src in ((wq_sb, sa_wq), (wk_sb, sa_wk), (wv_sb, sa_wv), (wo2_sb, sa_wo), (cols, sa_cols),
                         (rows, sa_rows), (rby_sb, rby), (freqs_sb, freqs), (pos_sb, positions)):
            sp.dma_start(dst[:], src).then_inc(consts_in, 16)
        for dst, src in ((gate_in, w_gate), (up_in, w_up), (down_in, w_down)):
            sp.dma_start(dst[:], src).then_inc(ffn_in, 16)
        out_rows = out.rearrange("b (t p) c -> b p t c", p=P)
        with sp.Fori(0, B) as b:
            for half in range(TT):
                sp.wait_ge(row_done, b * TT + half + 1)
                sp.dma_start(out_rows[b, :, half, :], x_out[:, half, :]).then_inc(out_done[half], 16)
        for half in range(TT):
            sp.wait_ge(out_done[half], 16 * B)

    @block.vector
    def _(dve):
        class Chain:
            def __init__(self, sem):
                self.sem, self.n = sem, 0

            def __call__(self, ins):
                self.n += 1
                ins.then_inc(self.sem, 1)
                dve.wait_ge(self.sem, self.n)

            def restart(self):
                self.n += 1
                dve.memset(small[:], 0.0).then_inc(self.sem, 1)
                dve.wait_ge(self.sem, self.n)
                dve.sem_clear(self.sem)

        def quantise(link, dst, src, n):
            k = n // BLK
            blocks = src.rearrange("p (k e) -> p k e", e=BLK)

            def blocked(t):
                return t[:, 0:n].rearrange("p (k e) -> p k e", e=BLK)

            def spread(t):
                return t[:, 0:k].unsqueeze(2).broadcast_to((P, k, BLK))

            link(dve.tensor_reduce(scale[:, 0:k], blocks, AX.X, ALU.max, apply_absolute_value=True))
            link(dve.tensor_scalar(scale[:, 0:k], scale[:, 0:k], 1.0 / 6.0, 1e-12, ALU.mult, ALU.max))
            link(dve.reciprocal(inv_scale[:, 0:k], scale[:, 0:k]))
            link(dve.tensor_scalar(inv_scale[:, 0:k], inv_scale[:, 0:k], 1.0 - 2.0 ** -24, None, ALU.mult))
            link(dve.tensor_tensor(blocked(qn), blocks, spread(inv_scale), ALU.mult))
            link(dve.tensor_scalar(qn[:, 0:n].bitcast(U32), qn[:, 0:n].bitcast(U32), 0x7FFFFFFF, None,
                                   ALU.bitwise_and))
            link(dve.tensor_scalar(qa[:, 0:n], qn[:, 0:n], 2.0, ROUND_HALF, ALU.min, ALU.add))
            link(dve.tensor_scalar(qb[:, 0:n], qn[:, 0:n], 4.0, 2.0, ALU.min, ALU.max))
            link(dve.tensor_scalar(qb[:, 0:n], qb[:, 0:n], ROUND_ONE, ROUND_ONE + 2.0, ALU.add, ALU.subtract))
            link(dve.scalar_tensor_tensor(out=qa[:, 0:n], in0=qa[:, 0:n], scalar=ROUND_HALF, in1=qb[:, 0:n],
                                          op0=ALU.subtract, op1=ALU.add))
            link(dve.tensor_scalar(qn[:, 0:n], qn[:, 0:n], 4.0, ROUND_TWO, ALU.max, ALU.add))
            link(dve.scalar_tensor_tensor(out=qa[:, 0:n], in0=qn[:, 0:n], scalar=ROUND_TWO + 4.0, in1=qa[:, 0:n],
                                          op0=ALU.subtract, op1=ALU.add))
            link(dve.tensor_tensor(blocked(qa), blocked(qa), spread(scale), ALU.mult))
            return dve.scalar_tensor_tensor(out=dst.bitcast(U32), in0=src.bitcast(U32), scalar=0x80000000,
                                            in1=qa[:, 0:n].bitcast(U32), op0=ALU.bitwise_and, op1=ALU.bitwise_or)

        link = Chain(prep_step)
        dve.memset(eps1[:], EPS)
        dve.memset(v2_sb[:], 0.0)
        dve.wait_ge(consts_in, 16 * 9)
        red, blue, yellow = (rby_sb[:, i:i + 1] for i in range(3))
        MUL, ADD = ALU.mult, ALU.add

        def weighted(dst, base, *terms):
            link(dve.memset(dst, base))
            for col, w in terms:
                link(dve.scalar_tensor_tensor(out=dst, in0=col, scalar=w, in1=dst, op0=MUL, op1=ADD))

        weighted(logit_scale[:], 1.0, (red, 0.1), (blue, 0.05), (yellow, 0.15))
        link(dve.tensor_scalar(logit_scale[:], logit_scale[:], FD ** -0.5, None, MUL))
        weighted(out_scale[:], 1.0, (yellow, OUT_EPS))
        weighted(gamma_scale[:], 1.0, (red, 0.1), (yellow, 0.05))
        weighted(eps2[:], 1.0, (blue, 0.1))
        link(dve.tensor_scalar(eps2[:], eps2[:], EPS, None, MUL))
        link(dve.tensor_scalar(rows[:, 2, :], rows[:, 2, :], gamma_scale[:], None, MUL))
        weighted(small[:], 1.0, (yellow, PHASE))
        link(dve.tensor_scalar(freqs_sb[:], freqs_sb[:], small[:], None, MUL))
        link(dve.reciprocal(freqs_sb[:], freqs_sb[:]))
        for half in range(TT):
            link(dve.tensor_scalar(angle[:, half, :], freqs_sb[:], pos_sb[:, half:half + 1], None, MUL))
        for c in range(2):
            link(dve.tensor_scalar(turns[:], angle[:], 0.5 / math.pi, 0.25 * c, MUL, ADD))
            link(dve.tensor_scalar(turns[:], turns[:], ROUND_ONE, ROUND_ONE, ADD, ALU.subtract))
            link(dve.scalar_tensor_tensor(out=reduced[:, c], in0=turns[:], scalar=-TWO_PI_A, in1=angle[:], op0=MUL, op1=ADD))
            for part in (TWO_PI_B, TWO_PI_C):
                link(dve.scalar_tensor_tensor(out=reduced[:, c], in0=turns[:], scalar=-part, in1=reduced[:, c],
                                              op0=MUL, op1=ADD))
            if c:
                link(dve.tensor_scalar(reduced[:, c], reduced[:, c], 0.5 * math.pi, None, ADD))
            link(dve.tensor_scalar(reduced[:, c], reduced[:, c], PI_BELOW, -PI_BELOW, ALU.min, ALU.max))
        dve.sem_inc(reduced_ready, 1)

        def quantise_weights(link, k):
            t = (gate_in, up_in, down_in)[k // 3]
            blocks = (TT * I if k // 3 == 2 else IT * DM) // BLK
            start, end = (blocks * i // 3 * BLK for i in (k % 3, k % 3 + 1))
            dve.wait_ge(ffn_in, 16 * 3)
            link(quantise(link, t[:, start:end], t[:, start:end], end - start))
            if k % 3 == 2:
                dve.sem_inc(w_quant, 1)

        def normalise(link, dst, src, k, eps_ready=None):
            for half in range(TT):
                ins = dve.bn_stats(stats2[:, half, :], src[:, half, :])
            link(ins)
            for half in range(TT):
                ins = dve.bn_aggr(mv2[:, half, :], stats2[:, half, :])
            ins.then_inc(var_ready, 1)
            dve.wait_ge(std_done, k + 1)
            link(dve.reciprocal(rstd2[:], std2[:]))
            for half in range(TT):
                ins = dve.tensor_scalar(dst[:, half, :], src[:, half, :], mv2[:, half, 0:1], rstd2[:, half:half + 1],
                                        ALU.subtract, MUL)
            return ins

        def begin(link, b):
            link(normalise(link, xq, x_sb[:, bass.ds(b * TT, TT), :], 3 * b))
            if isinstance(b, int) and b == 0:
                dve.wait_ge(encoding_ready, 1)
            dve.tensor_tensor(xq[:], xq[:], encoding[:], ADD).then_inc(rows_ready, 1)

        def take_q(b):
            dve.wait_ge(q_full, b + 1)
            for c in range(QC):
                ins = dve.tensor_scalar(q_sb[:, c, :], logits[0][:, c * T:(c + 1) * T], cols[:, 0, c:c + 1],
                                        logit_scale[:], ADD, MUL)
            ins.then_inc(q_taken, 1)

        def batch(b):
            link = Chain(dve_step)
            first, last = (isinstance(b, int) and b == k for k in (0, B - 1))
            x_rows = x_sb[:, bass.ds(b * TT, TT), :]
            if first:
                begin(link, b)
                quantise_weights(link, 0)
                take_q(b)
            dve.wait_ge(v_full, b + 1)
            dve.tensor_tensor(v2_sb[:, :, :, 0:FD], o_ps[:].rearrange("p (t h d) -> p t h d", t=TT, d=FD),
                              rows[:, 0, :].rearrange("p (h d) -> p h d", d=FD).unsqueeze(1)
                              .broadcast_to((P, TT, FH, FD)), ADD).then_inc(v_taken, 1)

            def take_turned(u):
                dve.wait_ge(eT_full, b * UNITS + u + 1)
                if u >= 2:
                    dve.wait_ge(av_done, b * UNITS + u - 1)
                dve.tensor_copy(eT_sb[:, u % 2, :], eT_ps[:]).then_inc(eT_taken, 1)

            for u in range(UNITS):
                dve.wait_ge(logits_full, b * UNITS + u + 1)
                if u >= 2:
                    dve.wait_ge(exp_ready, b * UNITS + u - 1)
                dve.tensor_reduce(neg_top[:, u % 2, :], logits[u % 2][:].rearrange("p (h k) -> p h k", k=T), AX.X,
                                  ALU.max, negate=True).then_inc(top_ready, 1)
                if u >= 1:
                    take_turned(u - 1)
                if first:
                    quantise_weights(link, u + 1)
            take_turned(UNITS - 1)
            dve.wait_ge(exp_ready, (b + 1) * UNITS)
            link(dve.reciprocal(inv_sums[:], sums[:]))
            link(dve.tensor_scalar(inv_sums[:], inv_sums[:], out_scale[:], None, MUL))
            dve.wait_ge(av_turned, b + 1)
            for half in range(TT):
                at = half * (FH // HG) * P
                ins = dve.tensor_tensor(
                    o_sb[:, half, :].rearrange("p (h u d) -> p u h d", h=HG, d=FD),
                    logits[1][:, at:at + (FH // HG) * P].rearrange("p (u h e) -> p u h e", h=HG, e=FPAD)[:, :, :, 0:FD],
                    inv_sums[:, half, :].rearrange("p (h u) -> p u h", h=HG).unsqueeze(3)
                    .broadcast_to((P, FH // HG, HG, FD)), MUL)
            ins.then_inc(rows_ready, 1)
            link(dve.tensor_tensor(xq[:], xq[:], rows[:, 1, :].unsqueeze(1).broadcast_to((P, TT, DM)), ADD))
            dve.wait_ge(proj_full, b + 1)
            link(dve.tensor_tensor(y_sb[:], eT_ps[:, 0:512].rearrange("p (t c) -> p t c", c=DM), xq[:], ADD))
            link(normalise(link, y_sb, y_sb, 3 * b + 1))
            link(dve.tensor_tensor(y_sb[:], y_sb[:], rows[:, 2, :].unsqueeze(1).broadcast_to((P, TT, DM)), MUL))
            link(dve.tensor_tensor(y_sb[:], y_sb[:], rows[:, 3, :].unsqueeze(1).broadcast_to((P, TT, DM)), ADD))
            link(dve.tensor_tensor(y_sb[:], y_sb[:], x_rows, ADD))
            link(normalise(link, xf, y_sb, 3 * b + 2))
            flat = "p t c -> p (t c)"
            quantise(link, xfq[:].rearrange(flat), xf[:].rearrange(flat), TT * DM).then_inc(rows_ready, 1)
            if not last:
                begin(link, b + 1)
            for half in range(TT):
                n = b * TT + half + 1
                dve.wait_ge(silu_ready, n)
                dve.wait_ge(up_full, n)
                dve.tensor_tensor(h_sb[:], silu_sb[:, half, :], logits[1][:, 0:I], MUL).then_inc(h_done, 1)
                dve.wait_ge(h_done, n)
                link(quantise(link, hq_sb[:, half, :], h_sb[:], I))
                dve.sem_inc(hq_ready, 1)
            if not last:
                take_q(b + 1)
            for half in range(TT):
                dve.wait_ge(down_full, b * TT + half + 1)
                if not first:
                    dve.wait_ge(out_done[half], 16 * b)
                dve.tensor_tensor(x_out[:, half, :], down_ps[half][:, 0:DM], y_sb[:, half, :], ADD)\
                    .then_inc(row_done, 1)
            link.restart()

        batch(0)
        with dve.Fori(1, B - 1) as b:
            batch(b)
        batch(B - 1)

    @block.scalar
    def _(act):
        act.wait_ge(reduced_ready, 1)
        act.activation(encoding[:, :, 0:DM:2], reduced[:, 0], ACT.Sin)
        act.activation(encoding[:, :, 1:DM:2], reduced[:, 1], ACT.Sin).then_inc(encoding_ready, 1)

        def take_weights(*steps):
            for k in steps:
                dst, n = WEIGHT_TURNS[k]
                act.wait_ge(w_turned, k + 1)
                act.activation(weight_turned(dst, n), logits[k % 2][:, 0:IT * P] if dst < 2 else
                               logits[k % 2][:, 0:512], ACT.Copy).then_inc(w_taken, 1)

        def std(k, eps):
            act.wait_ge(var_ready, k + 1)
            act.activation(std2[:], mv2[:, :, 1], ACT.Sqrt, bias=eps[:]).then_inc(std_done, 1)

        def take_turned(k):
            act.wait_ge(turned_full, k + 1)
            act.activation(turned[:].rearrange("p c t -> p (c t)"), turn_ps[:], ACT.Copy).then_inc(turned_taken, 1)

        def take_k(b):
            act.wait_ge(k_full, b + 1)
            for c in range(QC):
                ins = act.activation(k_sb[:, c, :], logits[1][:, c * T:(c + 1) * T], ACT.Identity, bias=cols[:, 1, c:c + 1])
            ins.then_inc(k_taken, 1)

        def batch(b):
            first, last = (isinstance(b, int) and b == k for k in (0, B - 1))
            if first:
                std(0, eps1)
                take_turned(0)
                take_k(0)

            def take_outputs(u):
                act.wait_ge(av_done, b * UNITS + u + 1)
                act.activation(avT_sb[:, u, :], avT_ps[u % 2][:, 0:P], ACT.Copy).then_inc(av_taken, 1)

            for u in range(UNITS):
                act.wait_ge(top_ready, b * UNITS + u + 1)
                if u >= 2:
                    act.wait_ge(eT_full, b * UNITS + u - 1)
                for h in range(HG):
                    half, head = u // (FH // HG), head_of(u, h)
                    ins = act.activation(e_sb[:, u % 2, h, :], logits[u % 2][:, h * T:(h + 1) * T], ACT.Exp,
                                         bias=neg_top[:, u % 2, h:h + 1], accum_out=sums[:, half, head:head + 1])
                ins.then_inc(exp_ready, 1)
                if u >= 2:
                    take_outputs(u - 2)
            take_outputs(UNITS - 2)
            take_outputs(UNITS - 1)
            take_turned(3 * b + 1)
            if first:
                take_weights(0)
            std(3 * b + 1, eps2)
            if first:
                take_weights(1, 2, 3)
            std(3 * b + 2, eps1)
            if first:
                take_weights(4, 5, 6)
            take_turned(3 * b + 2)
            if not last:
                std(3 * b + 3, eps1)
            for half in range(TT):
                n = b * TT + half + 1
                act.wait_ge(gate_full, n)
                act.activation(silu_sb[:, half, :], logits[0][:, 0:I], ACT.Silu).then_inc(silu_ready, 1)
            if not last:
                take_turned(3 * b + 3)
            for half in range(TT):
                if half and not last:
                    take_k(b + 1)
                act.wait_ge(hT_full, b * TT + half + 1)
                act.activation(hT_sb[:, half, 0:5 * P], eT_ps[:, 0:5 * P], ACT.Copy)
                act.activation(hT_sb[0:I - 5 * P, half, 5 * P:6 * P], eT_ps[0:I - 5 * P, 5 * P:6 * P],
                               ACT.Copy).then_inc(hT_taken, 1)

        batch(0)
        with act.Fori(1, B - 1) as b:
            batch(b)
        batch(B - 1)

    @block.tensor
    def _(pe):
        def turn_weights():
            for k, (dst, n) in enumerate(WEIGHT_TURNS):
                pe.wait_ge(w_quant, dst + 1)
                if k >= 2:
                    pe.wait_ge(w_taken, k - 1)
                o = logits[k % 2]
                if dst < 2:
                    src = (gate_in, up_in)[dst]
                    for i in range(IT):
                        ins = pe.transpose(o[:, i * P:(i + 1) * P], src[:, i * DM + n * P:i * DM + (n + 1) * P], ident[:])
                else:
                    for i in range(2):
                        kk = 2 * n + i
                        w = min(P, I - kk * P)
                        for r in range(TT):
                            ins = pe.transpose(o[0:w, i * DM + r * P:i * DM + (r + 1) * P],
                                               down_in[:, r * I + kk * P:r * I + kk * P + w], ident[:])
                ins.then_inc(w_turned, 1)
            pe.wait_ge(w_taken, len(WEIGHT_TURNS))

        def turn(k, src):
            pe.wait_ge(rows_ready, k + 1)
            for c in range(2):
                for half in range(TT):
                    at = c * T + half * P
                    ins = pe.transpose(turn_ps[:, at:at + P], src[:, half, c * P:(c + 1) * P], ident[:])
            ins.then_inc(turned_full, 1)
            pe.wait_ge(turned_taken, k + 1)

        def halves(half):
            return slice(half * P, (half + 1) * P)

        def project_qk(b):
            for w, o, full in ((wq_sb, logits[0], q_full), (wk_sb, logits[1], k_full)):
                for m in range(QC):
                    for c in range(2):
                        ins = pe.matmul(o[:, m * T:(m + 1) * T], w[:, c, m * P:(m + 1) * P], turned[:, c, :],
                                        start=(c == 0), stop=(c == 1))
                ins.then_inc(full, 1)

        def attention(b):
            for half in range(TT):
                for c in range(2):
                    ins = pe.matmul(o_ps[:, half * DM:(half + 1) * DM], turned[:, c, halves(half)], wv_sb[:, c, :],
                                    start=(c == 0), stop=(c == 1))
            ins.then_inc(v_full, 1)
            pe.wait_ge(q_taken, b + 1)
            pe.wait_ge(k_taken, b + 1)

            def values(u):
                pe.wait_ge(eT_taken, b * UNITS + u + 1)
                if u >= 2:
                    pe.wait_ge(av_taken, b * UNITS + u - 1)
                for h in range(HG):
                    for s in range(TT):
                        at = (h * TT + s) * P
                        ins = pe.matmul(avT_ps[u % 2][h * FPAD:(h + 1) * FPAD, 0:P], v2_sb[:, s, head_of(u, h), :],
                                        eT_sb[:, u % 2, at:at + P], start=(s == 0), stop=(s == TT - 1))
                ins.then_inc(av_done, 1)

            def turn_probs(u):
                pe.wait_ge(exp_ready, b * UNITS + u + 1)
                if u >= 1:
                    pe.wait_ge(eT_taken, b * UNITS + u)
                for h in range(HG):
                    for s in range(TT):
                        at = (h * TT + s) * P
                        ins = pe.transpose(eT_ps[:, at:at + P], e_sb[:, u % 2, h, s * P:(s + 1) * P], ident[:])
                ins.then_inc(eT_full, 1)

            for u in range(UNITS):
                half = u // (FH // HG)
                if u >= 2:
                    pe.wait_ge(exp_ready, b * UNITS + u - 1)
                for h in range(HG):
                    head = head_of(u, h)
                    r = head * FPAD % P
                    ins = pe.matmul(logits[u % 2][:, h * T:(h + 1) * T], q_sb[r:r + FPAD, head * FPAD // P, halves(half)],
                                    k_sb[r:r + FPAD, head * FPAD // P, :], start=True, stop=True)
                ins.then_inc(logits_full, 1)
                if u == 1:
                    pe.wait_ge(v_taken, b + 1)
                if u >= 1:
                    turn_probs(u - 1)
                if u >= 2:
                    values(u - 2)
            turn_probs(UNITS - 1)
            values(UNITS - 2)
            values(UNITS - 1)
            pe.wait_ge(av_taken, (b + 1) * UNITS)
            for u in range(UNITS):
                ins = pe.transpose(logits[1][:, u * P:(u + 1) * P], avT_sb[:, u, :], ident[:])
            ins.then_inc(av_turned, 1)
            turn(3 * b + 1, o_sb)
            for half in range(TT):
                for c in range(2):
                    ins = pe.matmul(eT_ps[:, half * DM:(half + 1) * DM], turned[:, c, halves(half)], wo2_sb[:, c, :],
                                    start=(c == 0), stop=(c == 1))
            ins.then_inc(proj_full, 1)

        def feed_forward(b):
            last = isinstance(b, int) and b == B - 1
            turn(3 * b + 2, xfq)
            for half in range(TT):
                n = b * TT + half + 1
                if half:
                    pe.wait_ge(h_done, n - 1)
                for w, o, full in ((gateT, logits[0], gate_full), (upT, logits[1], up_full)):
                    for at, width in HALVES:
                        for c in range(2):
                            ins = pe.matmul(o[:, at:at + width], turned[:, c, halves(half)], w[:, c, at:at + width],
                                            start=(c == 0), stop=(c == 1))
                    ins.then_inc(full, 1)
            if not last:
                turn(3 * b + 3, xq)
            for half in range(TT):
                n = b * TT + half + 1
                if half and not last:
                    pe.wait_ge(h_done, n)
                    project_qk(b + 1)
                pe.wait_ge(hq_ready, n)
                for i in range(IT):
                    w = min(P, I - i * P)
                    ins = pe.transpose(eT_ps[0:w, i * P:(i + 1) * P], hq_sb[:, half, i * P:i * P + w], ident[:])
                ins.then_inc(hT_full, 1)
                pe.wait_ge(hT_taken, n)
                for i in range(IT):
                    w = min(P, I - i * P)
                    ins = pe.matmul(down_ps[half][:, 0:DM], hT_sb[0:w, half, i * P:(i + 1) * P],
                                    downT[0:w, i, :], start=(i == 0), stop=(i == IT - 1))
                ins.then_inc(down_full, 1)
            pe.wait_ge(row_done, (b + 1) * TT)

        turn(0, xq)
        project_qk(0)
        attention(0)
        turn_weights()
        feed_forward(0)
        with pe.Fori(1, B - 1) as b:
            attention(b)
            feed_forward(b)
        attention(B - 1)
        feed_forward(B - 1)


def kernel(**inputs):
    import concourse.bacc as _bacc
    from concourse.bass_utils import run_bass_kernel_spmd as _run

    a = {k: np.asarray(v) for k, v in inputs.items()}
    half = P // 2

    def pair_columns(w):
        return w.reshape(2, P, NB, P).transpose(2, 1, 0, 3).reshape(NB, P, 2 * P)

    def rows_of(w):
        return w.reshape(-1, P, w.shape[1]).transpose(1, 0, 2)

    def padded_heads(w):
        w = w.reshape(FH, FD, -1)
        return np.concatenate([w, np.zeros((FH, FPAD - FD, w.shape[2]), w.dtype)], axis=1).reshape(FH * FPAD, -1)

    def across(v):
        return np.broadcast_to(v[None, ...], (P,) + v.shape)

    def padded_rows(w):
        return np.concatenate([w, np.zeros((IT * P - I, w.shape[1]), w.dtype)], axis=0)

    freqs = np.power(np.float32(10000.0), (2.0 * np.arange(0, DM, 2, dtype=np.float32) / DM).astype(np.float32))
    def twice(w):
        w = w.reshape(2, P, NB, 2, 1, half).transpose(2, 1, 0, 3, 4, 5)
        return np.broadcast_to(w, w.shape[:4] + (2, half)).reshape(NB, P, 4 * P)

    temps = np.broadcast_to(a["L0_xattn_inv_temp"].reshape(NB, 1, 2), (NB, P, 2))
    arrays = {
        "x": a["x"],
        "ctx_t": a["ctx_1024"].transpose(0, 2, 1).reshape(B, 2, P, S),
        "mask": a["mask_BxS2_bf1"].view(np.uint8),
        "w_pack": np.concatenate([twice(a["L0_xattn_Wq"]), pair_columns(a["L0_xattn_Wk"]), temps,
                                  pair_columns(a["L0_xattn_Wv"])], axis=2),
        "w_out": a["L0_xattn_Wo"].reshape(NB, P, DM),
        "sa_wq": rows_of(padded_heads(a["L0_attn_Wq"]).T),
        "sa_wk": rows_of(padded_heads(a["L0_attn_Wk"]).T),
        "sa_wv": rows_of(a["L0_attn_Wv"].T),
        "sa_wo": rows_of(a["L0_attn_Wo"].T),
        "sa_cols": np.stack([padded_heads(a[f"L0_attn_b{n}"][:, None]).reshape(QC, P).T for n in "qk"], axis=1),
        "sa_rows": across(np.stack([a["L0_attn_bv"], a["L0_attn_bo"], a["L0_attn_ln_gamma"], a["L0_attn_ln_beta"]])),
        "rby": across(a["L0_attn_rby"]),
        "freqs": across(freqs.astype(np.float32)),
        "positions": np.arange(T, dtype=np.float32).reshape(TT, P).T,
        "w_gate": rows_of(padded_rows(a["L0_ffn_w_gate"])).reshape(P, IT * DM),
        "w_up": rows_of(padded_rows(a["L0_ffn_w_up"])).reshape(P, IT * DM),
        "w_down": rows_of(a["L0_ffn_w_down"]).reshape(P, TT * I),
    }
    nc = _bacc.Bacc("TRN2", target_bir_lowering=False, num_devices=1, dynamic_dma_scratch_size=1024)
    aps = {}
    arrays = {k: np.ascontiguousarray(v) for k, v in arrays.items()}
    for name, v in arrays.items():
        aps[name] = nc.dram_tensor(name, v.shape, mybir.dt.from_np(v.dtype), kind="ExternalInput").ap()
    out = nc.dram_tensor("out", (B, T, DM), F32, kind="ExternalOutput").ap()
    build(nc, out=out, **aps)
    r = _run(nc, [arrays], core_ids=[0])
    return r.results[0]["out"]
```
